# Optimizing a Trainium2 kernel written in Bass

```python
import numpy as np
import jax
import jax.numpy as jnp

def _softmax(x, axis=-1):
    return jax.nn.softmax(x, axis=axis)

def _gelu(x):
    return jax.nn.gelu(x, approximate=True)

def _silu(x):
    return jax.nn.silu(x)

def _sigmoid(x):
    return jax.nn.sigmoid(x)

def _layernorm(x, axis=-1, eps=1e-05):
    m = jnp.mean(x, axis=axis, keepdims=True)
    v = jnp.var(x, axis=axis, keepdims=True)
    return (x - m) / jnp.sqrt(v + eps)

def _scatter_add(tgt, idx, src, axis=0):
    return tgt.at[idx].add(src)

def _segment_sum(src, seg, n):
    return jax.ops.segment_sum(src, seg, n)
kernel_name = 'mk_flamingo_gated_d4_seqx_r8_dc3a0c'

def setup_inputs(seed: int=0):
    np.random.seed(seed)
    _w = jnp.asarray

    def _rec_inputs():
        import jax
        import jax.numpy as jnp
        _rk = jax.random.key(seed)
        x = -0.0002928 + 1 * jax.random.normal(jax.random.fold_in(_rk, 1), (8, 128, 128), jnp.float32)
        _lenS = 128 - jax.random.randint(jax.random.fold_in(_rk, 7), (8,), 0, max(1, 128 // 4) + 1, jnp.int32)
        _lenS2 = 128 - jax.random.randint(jax.random.fold_in(_rk, 8), (8,), 0, max(1, 128 // 4) + 1, jnp.int32)
        _ctx_1024P = jax.random.normal(jax.random.fold_in(_rk, 11), (8, 16, 128), jnp.float32)
        _ctx_1024c = jax.random.dirichlet(jax.random.fold_in(_rk, 511), 0.3 * jnp.ones((16,), jnp.float32), (8, 128))
        _ctx_1024t = jnp.einsum('bsk,bkd->bsd', _ctx_1024c, _ctx_1024P)
        _ctx_1024t = _ctx_1024t * jax.lax.rsqrt(jnp.mean(jnp.square(_ctx_1024t)) + 1e-12) * 0.953939
        ctx_1024 = -1.39393e-06 + 0.999914 * (_ctx_1024t + 0.3 * jax.random.normal(jax.random.fold_in(_rk, 611), (8, 128, 128), jnp.float32))
        _validS = jnp.arange(128)[None, :] < _lenS[:, None]
        _validS2 = jnp.arange(128)[None, :] < _lenS2[:, None]
        _causal = jnp.tril(jnp.ones((128, 128), dtype=bool))
        mask_BxSxS2_bf0 = jnp.logical_not(jnp.ones((8, 128, 128), dtype=bool))
        mask_BxSxS2_ik0 = jnp.where(jnp.broadcast_to(_validS2[:, None, :], (8, 128, 128)), 0, 1).astype(jnp.int32)
        _g = jax.random.normal(jax.random.fold_in(_rk, 9001), (2, 4), jnp.float32)
        _g = jnp.sign(_g) * jnp.maximum(jnp.abs(_g), 1.0) + (_g == 0) * 1.0
        g_xattn = _g[0]
        g_ffn = _g[1]
        return (x, ctx_1024, _lenS2, mask_BxSxS2_bf0, mask_BxSxS2_ik0, g_xattn, g_ffn)
    x, ctx_1024, _lenS2, mask_BxSxS2_bf0, mask_BxSxS2_ik0, g_xattn, g_ffn = _rec_inputs()

    def _L0_xattn_setup():
        import jax, jax.numpy as jnp
        import numpy as np
        B, S, D = (2, 256, 128)
        H, HK, HV, OUT = (16, 64, 64, 128)
        NEG = -1e+30
        key = jax.random.key(seed)
        ks = jax.random.split(key, 8)
        scale = 1.0 / np.sqrt(D)
        return {'query': jax.random.normal(ks[0], (B, S, D), jnp.float32), 'key': jax.random.normal(ks[1], (B, S, D), jnp.float32), 'value': jax.random.normal(ks[2], (B, S, D), jnp.float32), 'padding_mask': jnp.zeros((B, S, S), dtype=bool), 'Wq': jax.random.uniform(ks[3], (H, HK, D), jnp.float32, -scale, scale), 'Wk': jax.random.uniform(ks[4], (H, HK, D), jnp.float32, -scale, scale), 'Wv': jax.random.uniform(ks[5], (H, HV, D), jnp.float32, -scale, scale), 'Wo': jax.random.uniform(ks[6], (OUT, H * HV), jnp.float32, -scale, scale)}
    _L0_xattn_all = _L0_xattn_setup()
    _L0_xattn_in = {k: v for k, v in _L0_xattn_all.items() if k in ('Wq', 'Wk', 'Wv', 'Wo')}
    del _L0_xattn_all

    def _L0_ffn_setup():
        import jax, jax.numpy as jnp
        import numpy as np
        HIDDEN = 128
        INNER = 512

        def _weight_quant(w):
            scale = 1.0 / jnp.clip(jnp.mean(jnp.abs(w)), 1e-05)
            wq = jnp.clip(jnp.round(w * scale), -1.0, 1.0) / scale
            return w + jax.lax.stop_gradient(wq - w)

        def _act_quant(x):
            scale = 127.0 / jnp.clip(jnp.max(jnp.abs(x), axis=-1, keepdims=True), 1e-05)
            xq = jnp.clip(jnp.round(x * scale), -128.0, 127.0) / scale
            return x + jax.lax.stop_gradient(xq - x)

        def _bitlinear(x, w):
            return jnp.einsum('bsi,oi->bso', _act_quant(x), _weight_quant(w))
        key = jax.random.key(seed)
        k0, k1, k2, k3 = jax.random.split(key, 4)
        x = jax.random.normal(k0, (4, 256, HIDDEN), dtype=jnp.float32)
        w_gate = jax.random.normal(k1, (INNER, HIDDEN), dtype=jnp.float32) / np.sqrt(HIDDEN)
        w_up = jax.random.normal(k2, (INNER, HIDDEN), dtype=jnp.float32) / np.sqrt(HIDDEN)
        w_down = jax.random.normal(k3, (HIDDEN, INNER), dtype=jnp.float32) / np.sqrt(INNER)
        return {'x': x, 'w_gate': w_gate, 'w_up': w_up, 'w_down': w_down}
    _L0_ffn_all = _L0_ffn_setup()
    _L0_ffn_in = {k: v for k, v in _L0_ffn_all.items() if k in ('w_gate', 'w_up', 'w_down')}
    del _L0_ffn_all

    def _L1_xattn_setup():
        import jax, jax.numpy as jnp
        import numpy as np
        D_MODEL = 128
        NUM_HEADS = 16
        D_K = D_MODEL // NUM_HEADS
        BATCH = 2
        SEQ = 256
        key = jax.random.key(seed)
        k = jax.random.split(key, 8)
        query = jax.random.normal(k[0], (BATCH, SEQ, D_MODEL), dtype=jnp.float32)
        key_t = jax.random.normal(k[1], (BATCH, SEQ, D_MODEL), dtype=jnp.float32)
        value = jax.random.normal(k[2], (BATCH, SEQ, D_MODEL), dtype=jnp.float32)
        mask = jnp.broadcast_to(jnp.tril(jnp.ones((SEQ, SEQ), dtype=jnp.int32)), (BATCH, SEQ, SEQ))
        scale = 1.0 / np.sqrt(D_MODEL)
        w_q = jax.random.normal(k[3], (D_MODEL, D_MODEL), dtype=jnp.float32) * scale
        w_k = jax.random.normal(k[4], (D_MODEL, D_MODEL), dtype=jnp.float32) * scale
        w_v = jax.random.normal(k[5], (D_MODEL, D_MODEL), dtype=jnp.float32) * scale
        w_o = jax.random.normal(k[6], (D_MODEL, D_MODEL), dtype=jnp.float32) * scale
        b_o = jnp.zeros((D_MODEL,), dtype=jnp.float32)
        return {'query': query, 'key': key_t, 'value': value, 'mask': mask, 'w_q': w_q, 'w_k': w_k, 'w_v': w_v, 'w_o': w_o, 'b_o': b_o}
    _L1_xattn_all = _L1_xattn_setup()
    _L1_xattn_in = {k: v for k, v in _L1_xattn_all.items() if k in ('w_q', 'w_k', 'w_v', 'w_o', 'b_o')}
    del _L1_xattn_all

    def _L1_ffn_setup():
        import math
        import jax, jax.numpy as jnp
        import numpy as np
        B, S, D, H, E, K = (4, 256, 128, 512, 8, 2)
        CAPACITY_RATIO = 1.05
        key = jax.random.key(seed)
        k0, k1, k2, k3 = jax.random.split(key, 4)
        x = jax.random.normal(k0, (B, S, D), jnp.float32)
        Wg = jax.random.normal(k1, (D, E), jnp.float32) * 0.02
        W1 = jax.random.normal(k2, (E, D, H), jnp.float32) * 0.02
        b1 = jnp.zeros((E, H), jnp.float32)
        W2 = jax.random.normal(k3, (E, H, D), jnp.float32) * 0.02
        b2 = jnp.zeros((E, D), jnp.float32)
        return {'x': x, 'Wg': Wg, 'W1': W1, 'b1': b1, 'W2': W2, 'b2': b2}
    _L1_ffn_all = _L1_ffn_setup()
    _L1_ffn_in = {k: v for k, v in _L1_ffn_all.items() if k in ('Wg', 'W1', 'b1', 'W2', 'b2')}
    del _L1_ffn_all

    def _L2_xattn_setup():
        import jax, jax.numpy as jnp
        import numpy as np
        NEG = -10000000000000.0
        key = jax.random.key(seed)
        ks = jax.random.split(key, 7)
        B, L, D, E = (8, 256, 128, 128)
        Q = jax.random.normal(ks[0], (B, L, D), dtype=jnp.float32)
        K = jax.random.normal(ks[1], (B, L, D), dtype=jnp.float32)
        V = jax.random.normal(ks[2], (B, L, D), dtype=jnp.float32)
        query_pad_idxs = jax.random.randint(ks[3], (B,), 0, L)
        key_pad_idxs = jax.random.randint(ks[4], (B,), 0, L)
        W = jax.random.normal(ks[5], (E, D), dtype=jnp.float32) / np.sqrt(D)
        b = jax.random.normal(ks[6], (E,), dtype=jnp.float32) * 0.01
        return {'Q': Q, 'K': K, 'V': V, 'query_pad_idxs': query_pad_idxs, 'key_pad_idxs': key_pad_idxs, 'W': W, 'b': b}
    _L2_xattn_all = _L2_xattn_setup()
    _L2_xattn_in = {k: v for k, v in _L2_xattn_all.items() if k in ('W', 'b')}
    del _L2_xattn_all

    def _L2_ffn_setup():
        import jax, jax.numpy as jnp
        import numpy as np
        EPS = 1e-06
        LN_EPS = 1e-05

        def _absmean_core(W):
            gamma = jnp.mean(jnp.abs(W)) + EPS
            Ws = W / gamma
            Wq = jnp.sign(Ws) * jnp.minimum(jnp.round(jnp.abs(Ws)), 1.0)
            return (Wq, gamma)

        @jax.custom_vjp
        def absmean(W):
            return _absmean_core(W)[0]

        def _absmean_fwd(W):
            Wq, gamma = _absmean_core(W)
            return (Wq, gamma)

        def _absmean_bwd(gamma, g):
            return (g / gamma,)
        absmean.defvjp(_absmean_fwd, _absmean_bwd)

        def layernorm(x, w, b, eps=LN_EPS):
            mu = jnp.mean(x, axis=-1, keepdims=True)
            var = jnp.mean((x - mu) ** 2, axis=-1, keepdims=True)
            return (x - mu) * jax.lax.rsqrt(var + eps) * w + b
        key = jax.random.key(seed)
        k1, k2, k3 = jax.random.split(key, 3)
        d, h = (128, 512)
        B, T = (8, 256)
        return {'x': jax.random.normal(k1, (B, T, d), jnp.float32), 'W_fc': jax.random.normal(k2, (h, d), jnp.float32), 'ln_w': jnp.ones((h,), jnp.float32), 'ln_b': jnp.zeros((h,), jnp.float32), 'W_proj': jax.random.normal(k3, (d, h), jnp.float32)}
    _L2_ffn_all = _L2_ffn_setup()
    _L2_ffn_in = {k: v for k, v in _L2_ffn_all.items() if k in ('W_fc', 'ln_w', 'ln_b', 'W_proj')}
    del _L2_ffn_all

    def _L3_xattn_setup():
        import jax, jax.numpy as jnp
        import numpy as np
        D_MODEL = 128
        N_HEAD = 16

        def _split_heads(x):
            B, S, D = x.shape
            return x.reshape(B, S, N_HEAD, D // N_HEAD).transpose(0, 2, 1, 3)
        key = jax.random.key(seed)
        ks = jax.random.split(key, 11)
        B, S, D = (2, 256, D_MODEL)
        s = 1.0 / np.sqrt(D)
        inp = {'q': jax.random.normal(ks[0], (B, S, D), jnp.float32), 'k': jax.random.normal(ks[1], (B, S, D), jnp.float32), 'v': jax.random.normal(ks[2], (B, S, D), jnp.float32), 'w_q': jax.random.normal(ks[3], (D, D), jnp.float32) * s, 'b_q': jnp.zeros((D,), jnp.float32), 'w_k': jax.random.normal(ks[4], (D, D), jnp.float32) * s, 'b_k': jnp.zeros((D,), jnp.float32), 'w_v': jax.random.normal(ks[5], (D, D), jnp.float32) * s, 'b_v': jnp.zeros((D,), jnp.float32), 'w_o': jax.random.normal(ks[6], (D, D), jnp.float32) * s, 'b_o': jnp.zeros((D,), jnp.float32)}
        return inp
    _L3_xattn_all = _L3_xattn_setup()
    _L3_xattn_in = {k: v for k, v in _L3_xattn_all.items() if k in ('w_q', 'b_q', 'w_k', 'b_k', 'w_v', 'b_v', 'w_o', 'b_o')}
    del _L3_xattn_all

    def _L3_ffn_setup():
        import jax, jax.numpy as jnp
        import numpy as np
        EPS_NORM = 1e-08
        EPS_Q = 1e-05

        def rmsnorm(x, w):
            v = jnp.mean(jnp.square(x.astype(jnp.float32)), axis=-1, keepdims=True)
            x_hat = x * jax.lax.rsqrt(v + EPS_NORM)
            return (x_hat * w).astype(x.dtype)

        def activation_quant(x):
            scale = 127.0 / jnp.clip(jnp.max(jnp.abs(x), axis=-1, keepdims=True), EPS_Q, None)
            return jnp.clip(jnp.round(x * scale), -128, 127) / scale

        def weight_quant(w):
            scale = 1.0 / jnp.clip(jnp.mean(jnp.abs(w)), EPS_Q, None)
            return jnp.clip(jnp.round(w * scale), -1, 1) / scale

        def bitlinear(x, norm_w, w):
            x_norm = rmsnorm(x, norm_w)
            x_q = x_norm + jax.lax.stop_gradient(activation_quant(x_norm) - x_norm)
            w_q = w + jax.lax.stop_gradient(weight_quant(w) - w)
            return jnp.einsum('bsd,hd->bsh', x_q, w_q)
        key = jax.random.key(seed)
        k1, k2, k3 = jax.random.split(key, 3)
        dim, hidden = (128, 512)
        return {'x': jax.random.normal(k1, (4, 256, dim), dtype=jnp.float32), 'norm1_w': jnp.ones((dim,), jnp.float32), 'w1': jax.random.normal(k2, (hidden, dim), jnp.float32) * 0.02, 'act_scale': jnp.ones((1,), jnp.float32), 'act_bias': jnp.zeros((1,), jnp.float32), 'norm2_w': jnp.ones((hidden,), jnp.float32), 'w2': jax.random.normal(k3, (dim, hidden), jnp.float32) * 0.02}
    _L3_ffn_all = _L3_ffn_setup()
    _L3_ffn_in = {k: v for k, v in _L3_ffn_all.items() if k in ('norm1_w', 'w1', 'act_scale', 'act_bias', 'norm2_w', 'w2')}
    del _L3_ffn_all
    return {'x': x, 'ctx_1024': ctx_1024, '_lenS2': _lenS2, 'mask_BxSxS2_bf0': mask_BxSxS2_bf0, 'mask_BxSxS2_ik0': mask_BxSxS2_ik0, 'g_xattn': g_xattn, 'g_ffn': g_ffn, 'L0_xattn_Wq': _L0_xattn_in['Wq'], 'L0_xattn_Wk': _L0_xattn_in['Wk'], 'L0_xattn_Wv': _L0_xattn_in['Wv'], 'L0_xattn_Wo': _L0_xattn_in['Wo'], 'L0_ffn_w_gate': _L0_ffn_in['w_gate'], 'L0_ffn_w_up': _L0_ffn_in['w_up'], 'L0_ffn_w_down': _L0_ffn_in['w_down'], 'L1_xattn_w_q': _L1_xattn_in['w_q'], 'L1_xattn_w_k': _L1_xattn_in['w_k'], 'L1_xattn_w_v': _L1_xattn_in['w_v'], 'L1_xattn_w_o': _L1_xattn_in['w_o'], 'L1_xattn_b_o': _L1_xattn_in['b_o'], 'L1_ffn_Wg': _L1_ffn_in['Wg'], 'L1_ffn_W1': _L1_ffn_in['W1'], 'L1_ffn_b1': _L1_ffn_in['b1'], 'L1_ffn_W2': _L1_ffn_in['W2'], 'L1_ffn_b2': _L1_ffn_in['b2'], 'L2_xattn_W': _L2_xattn_in['W'], 'L2_xattn_b': _L2_xattn_in['b'], 'L2_ffn_W_fc': _L2_ffn_in['W_fc'], 'L2_ffn_ln_w': _L2_ffn_in['ln_w'], 'L2_ffn_ln_b': _L2_ffn_in['ln_b'], 'L2_ffn_W_proj': _L2_ffn_in['W_proj'], 'L3_xattn_w_q': _L3_xattn_in['w_q'], 'L3_xattn_b_q': _L3_xattn_in['b_q'], 'L3_xattn_w_k': _L3_xattn_in['w_k'], 'L3_xattn_b_k': _L3_xattn_in['b_k'], 'L3_xattn_w_v': _L3_xattn_in['w_v'], 'L3_xattn_b_v': _L3_xattn_in['b_v'], 'L3_xattn_w_o': _L3_xattn_in['w_o'], 'L3_xattn_b_o': _L3_xattn_in['b_o'], 'L3_ffn_norm1_w': _L3_ffn_in['norm1_w'], 'L3_ffn_w1': _L3_ffn_in['w1'], 'L3_ffn_act_scale': _L3_ffn_in['act_scale'], 'L3_ffn_act_bias': _L3_ffn_in['act_bias'], 'L3_ffn_norm2_w': _L3_ffn_in['norm2_w'], 'L3_ffn_w2': _L3_ffn_in['w2']}

def reference(x, ctx_1024, _lenS2, mask_BxSxS2_bf0, mask_BxSxS2_ik0, g_xattn, g_ffn, L0_xattn_Wq, L0_xattn_Wk, L0_xattn_Wv, L0_xattn_Wo, L0_ffn_w_gate, L0_ffn_w_up, L0_ffn_w_down, L1_xattn_w_q, L1_xattn_w_k, L1_xattn_w_v, L1_xattn_w_o, L1_xattn_b_o, L1_ffn_Wg, L1_ffn_W1, L1_ffn_b1, L1_ffn_W2, L1_ffn_b2, L2_xattn_W, L2_xattn_b, L2_ffn_W_fc, L2_ffn_ln_w, L2_ffn_ln_b, L2_ffn_W_proj, L3_xattn_w_q, L3_xattn_b_q, L3_xattn_w_k, L3_xattn_b_k, L3_xattn_w_v, L3_xattn_b_v, L3_xattn_w_o, L3_xattn_b_o, L3_ffn_norm1_w, L3_ffn_w1, L3_ffn_act_scale, L3_ffn_act_bias, L3_ffn_norm2_w, L3_ffn_w2):
    import jax
    import jax.numpy as jnp

    def _L0_xattn_ref(query, key, value, padding_mask, Wq, Wk, Wv, Wo):
        import jax, jax.numpy as jnp
        import numpy as np
        B, S, D = (2, 256, 128)
        H, HK, HV, OUT = (16, 64, 64, 128)
        NEG = -1e+30
        b, s, _ = query.shape
        hk = Wq.shape[1]
        q = jnp.einsum('bsd,hkd->bhsk', query, Wq)
        k = jnp.einsum('bsd,hkd->bhsk', key, Wk)
        v = jnp.einsum('bsd,hvd->bhsv', value, Wv)
        scores = jnp.einsum('bhsk,bhtk->bhst', q, k) / jnp.sqrt(jnp.float32(hk))
        causal = jnp.triu(jnp.ones((s, s), dtype=bool), k=1)
        mask = causal[None, None, :, :] | padding_mask[:, None, :, :]
        scores = jnp.where(mask, NEG, scores)
        attn = jax.nn.softmax(scores, axis=-1)
        ctx = jnp.einsum('bhst,bhtv->bhsv', attn, v)
        ctx = jnp.transpose(ctx, (0, 2, 1, 3)).reshape(b, s, -1)
        return ctx @ Wo.T

    def _L0_ffn_ref(x, w_gate, w_up, w_down):
        import jax, jax.numpy as jnp
        import numpy as np
        HIDDEN = 128
        INNER = 512

        def _weight_quant(w):
            scale = 1.0 / jnp.clip(jnp.mean(jnp.abs(w)), 1e-05)
            wq = jnp.clip(jnp.round(w * scale), -1.0, 1.0) / scale
            return w + jax.lax.stop_gradient(wq - w)

        def _act_quant(x):
            scale = 127.0 / jnp.clip(jnp.max(jnp.abs(x), axis=-1, keepdims=True), 1e-05)
            xq = jnp.clip(jnp.round(x * scale), -128.0, 127.0) / scale
            return x + jax.lax.stop_gradient(xq - x)

        def _bitlinear(x, w):
            return jnp.einsum('bsi,oi->bso', _act_quant(x), _weight_quant(w))
        gate = jax.nn.silu(_bitlinear(x, w_gate))
        up = _bitlinear(x, w_up)
        return _bitlinear(gate * up, w_down)

    def _L1_xattn_ref(query, key, value, mask, w_q, w_k, w_v, w_o, b_o):
        import jax, jax.numpy as jnp
        import numpy as np
        D_MODEL = 128
        NUM_HEADS = 16
        D_K = D_MODEL // NUM_HEADS
        BATCH = 2
        SEQ = 256
        b, s, _ = query.shape

        def split_heads(x):
            return x.reshape(b, s, NUM_HEADS, D_K).transpose(0, 2, 1, 3)
        Q = split_heads(query @ w_q.T)
        K = split_heads(key @ w_k.T)
        V = split_heads(value @ w_v.T)
        scores = jnp.einsum('bhqd,bhkd->bhqk', Q, K) / jnp.sqrt(jnp.asarray(D_K, dtype=Q.dtype))
        scores = jnp.where(mask[:, None, :, :] == 0, -1000000000.0, scores)
        attn = jax.nn.softmax(scores, axis=-1)
        out = jnp.einsum('bhqk,bhkd->bhqd', attn, V)
        out = out.transpose(0, 2, 1, 3).reshape(b, s, D_MODEL)
        return out @ w_o.T + b_o

    def _L1_ffn_ref(x, Wg, W1, b1, W2, b2):
        import math
        import jax, jax.numpy as jnp
        import numpy as np
        B, S, D, H, E, K = (4, 256, 128, 512, 8, 2)
        CAPACITY_RATIO = 1.05
        b, s, d = x.shape
        e = Wg.shape[1]
        n = b * s
        cap = int(math.ceil(n * K / e * CAPACITY_RATIO))
        xf = x.reshape(n, d)
        probs = jax.nn.softmax(xf @ Wg, axis=-1)
        topv, topi = jax.lax.top_k(probs, K)
        gates = topv / jnp.sum(topv, axis=-1, keepdims=True)
        eidx = topi.reshape(-1)
        oh = jax.nn.one_hot(eidx, e, dtype=jnp.int32)
        pos = jnp.sum(jnp.cumsum(oh, axis=0) * oh, axis=-1) - 1
        keep = pos < cap
        dest = jnp.where(keep, eidx * cap + pos, e * cap)
        xr = jnp.repeat(xf, K, axis=0)
        buf = jnp.zeros((e * cap + 1, d), x.dtype).at[dest].set(xr)
        expert_in = buf[:e * cap].reshape(e, cap, d)
        h = jax.nn.gelu(jnp.einsum('ecd,edh->ech', expert_in, W1) + b1[:, None, :])
        y = jnp.einsum('ech,ehd->ecd', h, W2) + b2[:, None, :]
        yf = jnp.concatenate([y.reshape(e * cap, d), jnp.zeros((1, d), y.dtype)], axis=0)
        gathered = yf[dest]
        w = (gates.reshape(-1) * keep.astype(gates.dtype))[:, None]
        out = (gathered * w).reshape(n, K, d).sum(axis=1).reshape(b, s, d)
        return out

    def _L2_xattn_ref(Q, K, V, query_pad_idxs, key_pad_idxs, W, b):
        import jax, jax.numpy as jnp
        import numpy as np
        NEG = -10000000000000.0
        B, Lq, D = Q.shape
        Lk = K.shape[1]
        scale = 1.0 / jnp.sqrt(jnp.asarray(D, dtype=Q.dtype))
        scores = jnp.einsum('bqd,bkd->bqk', Q, K) * scale
        qpos = jnp.arange(Lq)[None, :, None]
        kpos = jnp.arange(Lk)[None, None, :]
        mask = (qpos >= query_pad_idxs[:, None, None]) & (kpos >= key_pad_idxs[:, None, None])
        scores = jnp.where(mask, jnp.asarray(NEG, scores.dtype), scores)
        attn = jax.nn.softmax(scores, axis=2)
        out = jnp.einsum('bqk,bkd->bqd', attn, V)
        return out @ W.T + b

    def _L2_ffn_ref(x, W_fc, ln_w, ln_b, W_proj):
        import jax, jax.numpy as jnp
        import numpy as np
        EPS = 1e-06
        LN_EPS = 1e-05

        def _absmean_core(W):
            gamma = jnp.mean(jnp.abs(W)) + EPS
            Ws = W / gamma
            Wq = jnp.sign(Ws) * jnp.minimum(jnp.round(jnp.abs(Ws)), 1.0)
            return (Wq, gamma)

        @jax.custom_vjp
        def absmean(W):
            return _absmean_core(W)[0]

        def _absmean_fwd(W):
            Wq, gamma = _absmean_core(W)
            return (Wq, gamma)

        def _absmean_bwd(gamma, g):
            return (g / gamma,)
        absmean.defvjp(_absmean_fwd, _absmean_bwd)

        def layernorm(x, w, b, eps=LN_EPS):
            mu = jnp.mean(x, axis=-1, keepdims=True)
            var = jnp.mean((x - mu) ** 2, axis=-1, keepdims=True)
            return (x - mu) * jax.lax.rsqrt(var + eps) * w + b
        h = jnp.einsum('btd,hd->bth', x, absmean(W_fc))
        h = jax.nn.gelu(h, approximate=False)
        h = layernorm(h, ln_w, ln_b)
        return jnp.einsum('bth,dh->btd', h, absmean(W_proj))

    def _L3_xattn_ref(q, k, v, w_q, b_q, w_k, b_k, w_v, b_v, w_o, b_o):
        import jax, jax.numpy as jnp
        import numpy as np
        D_MODEL = 128
        N_HEAD = 16

        def _split_heads(x):
            B, S, D = x.shape
            return x.reshape(B, S, N_HEAD, D // N_HEAD).transpose(0, 2, 1, 3)
        qh = _split_heads(q @ w_q.T + b_q)
        kh = _split_heads(k @ w_k.T + b_k)
        vh = _split_heads(v @ w_v.T + b_v)
        d_k = qh.shape[-1]
        scores = jnp.einsum('bhqd,bhkd->bhqk', qh, kh) / jnp.sqrt(jnp.float32(d_k))
        attn = jax.nn.softmax(scores, axis=-1)
        out = jnp.einsum('bhqk,bhkd->bhqd', attn, vh)
        B, H, S, d = out.shape
        out = out.transpose(0, 2, 1, 3).reshape(B, S, H * d)
        return out @ w_o.T + b_o

    def _L3_ffn_ref(x, norm1_w, w1, act_scale, act_bias, norm2_w, w2):
        import jax, jax.numpy as jnp
        import numpy as np
        EPS_NORM = 1e-08
        EPS_Q = 1e-05

        def rmsnorm(x, w):
            v = jnp.mean(jnp.square(x.astype(jnp.float32)), axis=-1, keepdims=True)
            x_hat = x * jax.lax.rsqrt(v + EPS_NORM)
            return (x_hat * w).astype(x.dtype)

        def activation_quant(x):
            scale = 127.0 / jnp.clip(jnp.max(jnp.abs(x), axis=-1, keepdims=True), EPS_Q, None)
            return jnp.clip(jnp.round(x * scale), -128, 127) / scale

        def weight_quant(w):
            scale = 1.0 / jnp.clip(jnp.mean(jnp.abs(w)), EPS_Q, None)
            return jnp.clip(jnp.round(w * scale), -1, 1) / scale

        def bitlinear(x, norm_w, w):
            x_norm = rmsnorm(x, norm_w)
            x_q = x_norm + jax.lax.stop_gradient(activation_quant(x_norm) - x_norm)
            w_q = w + jax.lax.stop_gradient(weight_quant(w) - w)
            return jnp.einsum('bsd,hd->bsh', x_q, w_q)
        h = bitlinear(x, norm1_w, w1)
        h = act_scale * jnp.square(jax.nn.relu(h)) + act_bias
        y = bitlinear(h, norm2_w, w2)
        return y
    x = x + jnp.tanh(g_xattn[0]) * _L0_xattn_ref(_layernorm(x, axis=-1), ctx_1024, ctx_1024, mask_BxSxS2_bf0, L0_xattn_Wq, L0_xattn_Wk, L0_xattn_Wv, L0_xattn_Wo)
    x = x + jnp.tanh(g_ffn[0]) * _L0_ffn_ref(_layernorm(x, axis=-1), L0_ffn_w_gate, L0_ffn_w_up, L0_ffn_w_down)
    x = x + jnp.tanh(g_xattn[1]) * _L1_xattn_ref(_layernorm(x, axis=-1), ctx_1024, ctx_1024, mask_BxSxS2_ik0, L1_xattn_w_q, L1_xattn_w_k, L1_xattn_w_v, L1_xattn_w_o, L1_xattn_b_o)
    x = x + jnp.tanh(g_ffn[1]) * _L1_ffn_ref(_layernorm(x, axis=-1), L1_ffn_Wg, L1_ffn_W1, L1_ffn_b1, L1_ffn_W2, L1_ffn_b2)
    x = x + jnp.tanh(g_xattn[2]) * _L2_xattn_ref(_layernorm(x, axis=-1), ctx_1024, ctx_1024, _lenS2, _lenS2, L2_xattn_W, L2_xattn_b)
    x = x + jnp.tanh(g_ffn[2]) * _L2_ffn_ref(_layernorm(x, axis=-1), L2_ffn_W_fc, L2_ffn_ln_w, L2_ffn_ln_b, L2_ffn_W_proj)
    x = x + jnp.tanh(g_xattn[3]) * _L3_xattn_ref(_layernorm(x, axis=-1), ctx_1024, ctx_1024, L3_xattn_w_q, L3_xattn_b_q, L3_xattn_w_k, L3_xattn_b_k, L3_xattn_w_v, L3_xattn_b_v, L3_xattn_w_o, L3_xattn_b_o)
    x = x + jnp.tanh(g_ffn[3]) * _L3_ffn_ref(_layernorm(x, axis=-1), L3_ffn_norm1_w, L3_ffn_w1, L3_ffn_act_scale, L3_ffn_act_bias, L3_ffn_norm2_w, L3_ffn_w2)
    return x

_drawn_inputs = setup_inputs


def setup_inputs(seed=0):
    import zlib

    import numpy as np

    out = dict(_drawn_inputs(seed))
    spreads = {'L1_xattn_b_o': (0.0, 0.1),
     'L1_ffn_b1': (0.0, 0.575),
     'L1_ffn_b2': (0.0, 0.1),
     'L2_ffn_ln_w': (1.0, 0.2),
     'L2_ffn_ln_b': (0.0, 0.1),
     'L3_xattn_b_q': (0.0, 0.8),
     'L3_xattn_b_k': (0.0, 0.8),
     'L3_xattn_b_v': (0.0, 0.8),
     'L3_xattn_b_o': (0.0, 0.8),
     'L3_ffn_norm1_w': (1.0, 0.6),
     'L3_ffn_norm2_w': (1.0, 0.6)}
    factors = {'g_ffn': 8.0,
     'L2_xattn_b': 7.492,
     'L3_xattn_w_q': 5.159,
     'L3_xattn_w_k': 5.337,
     'L3_ffn_w1': 3.432,
     'L3_ffn_w2': 3.133}
    for name, (base, spread) in spreads.items():
        noise = np.random.default_rng([zlib.crc32(name.encode()), seed]).standard_normal(out[name].shape)
        drawn = base * np.exp(spread * noise) if base else spread * noise
        out[name] = jnp.asarray(drawn.astype(out[name].dtype))
    for name, factor in factors.items():
        out[name] = (out[name] * factor).astype(out[name].dtype)
    return out
```

```python
from contextlib import ExitStack

import concourse.bass as bass
from concourse import mybir

F32 = mybir.dt.float32
BF16 = mybir.dt.bfloat16
I32 = mybir.dt.int32
U8 = mybir.dt.uint8
U32 = mybir.dt.uint32
ALU = mybir.AluOpType
ACT = mybir.ActivationFunctionType
AX = mybir.AxisListType

P = 128
B = 8
N = B * P
H = 16
DK0 = 64
DK = P // H
GH = 4
G = H // GH
VW = DK + 1
VW0 = DK0 + 1
F = 512
FT = F // P
NE = 8
TOPK = 2
CAP = -(-N * TOPK * 105 // (NE * 100))
NEG = -1e30
MAGIC = 1.5 * 2 ** 23
LN_EPS = 1e-5
STATS = 6

PACK_FIRST = dict(ctxT=N, wkT_1=P, wkT_3=P, wvT_13=2 * P, ident=P, ones=P, causal=P, hmask=H, bk_3=1, bq_3=1, gates=8, x=N)
PACK_ATT0 = dict(wkT_0=H * DK0, wqT_0=H * DK0, wvT_0=H * DK0, woT_0=H * DK0)
PACK_REST = dict(kiota=P, utri=P, eiota=NE, piota=1, act_sb=2, lnw_2=FT, wg=NE, lnb_2=FT,
                 wqT_1=P, woT_1=P, wqT_3=P, woT_3=P, woT_2=P)
PACK_FFN = dict(gateT=F, upT=F, downT=F, fcT=F, projT=F, w1T=F, w2T=F, nw1=P, nw2=F)
PACK_CTX = dict(ctx=N)
PACKS = [PACK_FIRST, PACK_ATT0, PACK_REST, PACK_FFN, PACK_CTX]
ROWS = dict(bv_13=2 * P, bo_1=P, bo_2=P, bo_3=P)
EXPERT = F + FT + F
TERNARY = ["gateT", "upT", "downT", "fcT", "projT", "w1T", "w2T"]


class Item:

    def __init__(self, b, rep):
        self.b, self.rep, self.k = b, rep, rep % 2

    def back(self, n):
        return Item(self.b - n, self.rep - n) if self.rep - n >= 0 else None


class Event:

    def __init__(self, sem, per):
        self.sem, self.per = sem, per

    def at(self, item, j=None):
        return self.per * item.b + (self.per if j is None else j)


def schedule(lags):
    out, drain = [], None
    for n, lag in enumerate(lags):
        over = lags[n - 1] if n else 0
        peel = max(lag + 1, over)
        peel += (B - peel) % 2
        for j in range(peel):
            steps = [(n - 1, B + j)] if n and j < over else []
            out.append(("peel", steps + [(n, j)]))
        if B > peel:
            out.append(("loop", n, peel, (B - peel) // 2))
    for j in range(lags[-1]):
        out.append(("peel", [(len(lags) - 1, B + j)]))
    return out


def walk(eng, plan, stages, before={}, after={}):

    def step(layer, s, off, loop=None):
        for lag, fn, *args in stages[layer]:
            rep = s + off - lag
            if 0 <= rep < B:
                fn(Item(rep if loop is None else 2 * loop + rep, rep), *args)

    for what in plan:
        if what[0] == "peel":
            for layer, s in what[1]:
                if (layer, s) in before:
                    before[layer, s]()
                step(layer, s, 0)
                if (layer, s) in after:
                    after[layer, s]()
        else:
            _, layer, first, pairs = what
            with eng.Fori(0, pairs) as i:
                for off in range(2):
                    step(layer, first, off, i)


RED_DONE = len(TERNARY) + 5
RT_CHOSEN = 3 + 2 * B + 6 + 1 + (B - 1)
RT_WEIGHTS = RT_CHOSEN + 7
RT_BIAS = RT_WEIGHTS + 2

A0, F0, A1, ROUTE, MOE, A2, F2, A3, F3 = range(9)
LAG = [3, 2, 3, 1, 1, 2, 2, 3, 2]
LAYERS = ["a0", "f0", "a1", "route", "moe", "a2", "f2", "a3", "f3"]
PLAN = schedule(LAG)


def build(nc, packs, rows_d, mask0_d, mask1_d, lens_d, b2blk_d, experts_d, out_d):
    with ExitStack() as ctx:
        def sb(name, shape, dt=F32):
            return ctx.enter_context(nc.sbuf_tensor(name, shape, dt))

        def sem(name):
            return ctx.enter_context(nc.semaphore(name))

        def events(layer, **per):
            return {k: Event(sem(f"{LAYERS[layer]}_{k}"), v) for k, v in per.items()}

        col = {}
        packed = []
        for n, pack in enumerate(PACKS):
            tile = sb(f"pack{n}", [P, sum(pack.values())])
            packed.append(tile)
            at = 0
            for name, w in pack.items():
                col[name] = tile[:, at:at + w]
                at += w
        rows_sb = sb("rows_sb", [1, sum(ROWS.values())])
        row = {}
        at = 0
        for name, w in ROWS.items():
            row[name] = rows_sb[0:1, at:at + w]
            at += w
        x_sb = col["x"].rearrange("p (b d) -> p b d", b=B)
        ctxT = col["ctxT"].rearrange("p (b t) -> p b t", b=B)
        ctx_tok = col["ctx"].rearrange("p (b d) -> p b d", b=B)
        ident = col["ident"]
        ones = col["ones"]
        identb = sb("identb", [P, P], BF16)
        onesb = sb("onesb", [P, P], BF16)
        utrib = sb("utrib", [P, P], BF16)
        tanh_g = sb("tanh_g", [P, 8])
        mask0_u8 = sb("mask0_u8", [P, B, P], U8)
        mask1_i32 = sb("mask1_i32", [P, B, P], I32)
        lens_i = sb("lens_i", [P, B], I32)
        lens_f = sb("lens_f", [P, B])
        qneg = sb("qneg", [P, B])
        neg0 = sb("neg0", [P, B, P], BF16)
        neg1 = sb("neg1", [P, B, P], BF16)
        neg2 = sb("neg2", [P, B, P], BF16)
        b2blk = sb("b2blk", [NE * B, N])
        kT_1 = sb("kT_1", [P, B, P])
        kT_3 = sb("kT_3", [P, B, P])
        va_1 = sb("va_1", [P, B, H, VW])
        va_3 = sb("va_3", [P, B, H, VW])

        stats = sb("stats", [P, 2, STATS])
        mv = sb("mv", [P, 2, 2])
        mv_h = sb("mv_h", [P, 2, 2])
        rstd = sb("rstd", [P, 2, 4])
        xn = sb("xn", [P, 2, P])
        xnT = sb("xnT", [P, 2, P])
        qT = sb("qT", [P, 2, H * DK0])
        ctk = sb("ctk", [P, 2, P])
        kz = sb("kz", [P, 2, 2 * H * DK0])
        va0 = sb("va0", [P, 2, H, VW0])
        prob = sb("prob", [P, 2, F])
        probT = sb("probT", [P, 2, F])
        mx = sb("mx", [P, 2, GH])
        rden = sb("rden", [P, 2, H])
        o_n = sb("o_n", [P, 2, H * DK0])
        oT = sb("oT", [P, 2, H * DK0])

        minus_half = sb("minus_half", [P, 1])[:, 0:1]
        minus_magic = sb("minus_magic", [P, 1])[:, 0:1]
        xm = sb("xm", [P, 2, P])
        xqT = sb("xqT", [P, 2, P], BF16)
        qs = sb("qs", [P, 2, 8])
        hs = sb("hs", [P, 2, 8])
        hid = sb("hid", [P, 2, F])
        hid2 = sb("hid2", [P, 2, F])
        sg = sb("sg", [P, 2, F])
        hqT = sb("hqT", [P, 2, F], BF16)
        tern = {n: sb(f"t_{n}", [P, F], F32 if n in ("fcT", "projT") else BF16) for n in TERNARY}
        tmp_t = sb("tmp_t", [P, 2, F])
        asum = sb("asum", [P, len(TERNARY)])
        wmean = sb("wmean", [P, len(TERNARY)])
        winv = sb("winv", [P, len(TERNARY)])
        projw = sb("projw", [P, F])
        crow = sb("crow", [1, P])

        xnT_all = sb("xnT_all", [P, B, P])
        lg = sb("lg", [P, B, NE])
        pr = sb("pr", [P, B, NE])
        psum_r = sb("psum_r", [P, B])
        top = sb("top", [P, B, NE])
        topi = sb("topi", [P, B, NE], U32)
        topf = sb("topf", [P, B, NE])
        gsum = sb("gsum", [P, B])
        g12 = sb("g12", [P, B, 2])
        oh1 = sb("oh1", [P, B, NE])
        oh2 = sb("oh2", [P, B, NE])
        chosen = sb("chosen", [P, B, NE], BF16)
        before_b = sb("before_b", [P, B, NE], BF16)
        keep = sb("keep", [P, B, NE])
        w_tok = sb("w_tok", [P, B, NE])
        w_tokT = sb("w_tokT", [B * NE, P])
        expert = sb("expert", [P, 2, EXPERT])
        hT = kz[:, :, :].rearrange("p k (t n) -> p k t n", t=FT)

        bank = [ctx.enter_context(nc.psum_tensor(f"bank{i}", [P, 512], F32)) for i in range(8)]
        S_BANK, T_BANK, O_BANK, R_BANK = (0, 1), (2, 3), (4, 5), (6, 7)

        loaded = [sem(f"loaded{n}") for n in range(len(PACKS) + 1)]
        rows_loaded, mask0_loaded, mask1_loaded = sem("rows_loaded"), sem("mask0_loaded"), sem("mask1_loaded")
        lens_loaded, b2_loaded = sem("lens_loaded"), sem("b2_loaded")
        ctk_loaded = [sem(f"ctk_loaded{k}") for k in range(2)]
        expert_loaded = [sem(f"expert_loaded{k}") for k in range(2)]
        stored = sem("stored")
        pool_const = sem("pool_const")
        tern_dve = sem("tern_dve")
        prep_pe = sem("prep_pe")
        prep_act = sem("prep_act")
        prep_dve = sem("prep_dve")
        act_const = sem("act_const")
        kz_zero = sem("kz_zero")
        pool_waited, dve_waited = sem("pool_waited"), sem("dve_waited")
        red_dve = sem("red_dve")
        red_pe = sem("red_pe")
        fold_dve = sem("fold_dve")
        fold_pe = sem("fold_pe")
        rt_dve = sem("rt_dve")
        rt_act = sem("rt_act")
        rt_pe = sem("rt_pe")

        att = dict(ln=3, rs=2, xt=1, xt_sb=1, scores=G, shifted=2 * G, probs=G, probsT=G, probsT_sb=G, pv=G, y=1, resid=1)
        E = {
            A0: events(A0, **att, kps=2, k_sb=4, qps=2, q_sb=2, vps=2, v_sb=2, norm=2 * G, ot=2, ot_sb=2),
            A1: events(A1, **att, q=1, q_sb=1, kz=1, norm=2, ot=1, ot_sb=1),
            A3: events(A3, **att, q=1, q_sb=1, kz=1, norm=2, ot=1, ot_sb=1),
            A2: events(A2, ln=3, rs=2, xt=1, xt_sb=1, scores=1, shift=2, probs=1, probsT=1, probsT_sb=1, pv=1,
                       norm=2, ot=1, ot_sb=1, y=1, resid=1),
            F0: events(F0, ln=3, rs=2, quant=5, xt=1, xt_sb=1, gate=1, up=1, silu=1, hid=6, ht=1, ht_sb=1, y=1, resid=1),
            F3: events(F3, ln=3, rs=2, quant=8, rq=2, rh=2, xt=1, xt_sb=1, up=1, relu=1, sq=1, hid=2, sumsq=1, hq=7, ht=1, ht_sb=1,
                       y=1, resid=1),
            F2: events(F2, ln=3, rs=2, xt=1, xt_sb=1, up=1, gelu=1, hid=3, rs_hid=2, ht=1, ht_sb=1, y=1, resid=1),
            ROUTE: events(ROUTE, ln=3, rs=2, xt=1, xt_sb=1, copied=1, logits=1, lg=2),
            MOE: events(MOE, h=8, gelu=8, y=2, acc=8),
        }
        emptied = {
            (A0, "xt"): ("xt_sb", 1), (A0, "k0"): ("k_sb", 2), (A0, "k1"): ("k_sb", 4), (A0, "q0"): ("q_sb", 1),
            (A0, "q1"): ("q_sb", 2), (A0, "v0"): ("v_sb", 1), (A0, "v1"): ("v_sb", 2), (A0, "ot0"): ("ot_sb", 1),
            (A0, "ot1"): ("ot_sb", 2), (A0, "y"): ("resid", 1),
            (A2, "xt"): ("xt_sb", 1), (A2, "s"): ("probs", 1), (A2, "t"): ("probsT_sb", 1), (A2, "pv"): ("norm", 2),
            (A2, "ot"): ("ot_sb", 1), (A2, "y"): ("resid", 1),
            (F0, "xt"): ("xt_sb", 1), (F0, "gate"): ("silu", 1), (F0, "up"): ("hid", 1), (F0, "ht"): ("ht_sb", 1),
            (F0, "y"): ("resid", 1),
            (F3, "xt"): ("xt_sb", 1), (F3, "up"): ("relu", 1), (F3, "ht"): ("ht_sb", 1), (F3, "y"): ("resid", 1),
            (F2, "xt"): ("xt_sb", 1), (F2, "up"): ("gelu", 1), (F2, "ht"): ("ht_sb", 1), (F2, "y"): ("resid", 1),
            (ROUTE, "xt"): ("xt_sb", 1), (ROUTE, "lg"): ("lg", 2),
        }
        for a in (A0, A1, A3):
            for g in range(G):
                emptied[a, f"s{g}"] = ("shifted", 2 * g + 2)
                emptied[a, f"t{g}"] = ("probsT_sb", g + 1)
                emptied[a, f"pv{g}"] = ("norm", 2 * g + 2 if a == A0 else 2)
        for a in (A1, A3):
            emptied[a, "xt"] = ("xt_sb", 1)
            emptied[a, "q"] = ("q_sb", 1)
            emptied[a, "ot"] = ("ot_sb", 1)
            emptied[a, "y"] = ("resid", 1)
        for tc in range(2):
            for ht in range(FT):
                emptied[MOE, f"h{tc}{ht}"] = ("gelu", 4 * tc + ht + 1)
            emptied[MOE, f"y{tc}"] = ("acc", 4 * tc + 4)

        def wait(eng, layer, name, item, j=None):
            if item is not None:
                ev = E[layer][name]
                eng.wait_ge(ev.sem, ev.at(item, j))

        block = ctx.enter_context(nc.Block())

        @block.sync
        def _(sp):
            cut = sum(PACK_FIRST.values()) - N
            sp.dma_start(packed[0][:, 0:cut], packs[0][:, 0:cut]).then_inc(loaded[0], 16)
            sp.dma_start(packed[0][:, cut:], packs[0][:, cut:]).then_inc(loaded[5], 16)
            sp.dma_start(rows_sb[:, :], rows_d).then_inc(rows_loaded, 16)
            sp.dma_start(mask0_u8[:, :, :], mask0_d).then_inc(mask0_loaded, 16)
            sp.dma_start(packed[1][:, :], packs[1]).then_inc(loaded[1], 16)
            sp.dma_start(packed[2][:, :], packs[2]).then_inc(loaded[2], 16)

            def load_ctk(it):
                wait(sp, A0, "vps", it.back(2))
                sp.dma_start(ctk[:, it.k, :], packs[0][:, 0:N].rearrange("p (b t) -> p b t", b=B)[:, bass.ds(it.b, 1), :]
                             ).then_inc(ctk_loaded[it.k], 16)

            def load_expert(it):
                wait(sp, MOE, "y", it.back(2))
                sp.dma_start(expert[:, it.k, :], experts_d[bass.ds(it.b, 1)].rearrange("a p n -> p (a n)")
                             ).then_inc(expert_loaded[it.k], 16)

            def rest():
                sp.dma_start(packed[3][:, :], packs[3]).then_inc(loaded[3], 16)
                sp.dma_start(mask1_i32[:, :, :], mask1_d).then_inc(mask1_loaded, 16)
                sp.dma_start(lens_i[:, :], lens_d).then_inc(lens_loaded, 16)
                sp.dma_start(b2blk[:, :], b2blk_d).then_inc(b2_loaded, 16)
                sp.dma_start(packed[4][:, :], packs[4]).then_inc(loaded[4], 16)

            stages = {n: [] for n in range(len(LAG))}
            stages[A0] = [(0, load_ctk)]
            stages[MOE] = [(0, load_expert)]
            walk(sp, PLAN, stages, after={(A0, 0): rest})
            wait(sp, F3, "resid", Item(B - 1, B - 1))
            sp.dma_start(out_d, col["x"]).then_inc(stored, 16)
            sp.wait_ge(stored, 16)

        @block.gpsimd
        def _(pool):
            pool.memset(minus_half, -0.5).then_inc(pool_const, 1)
            for k in range(2):
                pool.memset(kz[:, k, :], 0.0).then_inc(kz_zero, 1)
                pool.memset(va0[:, k, :, DK0:VW0], 1.0).then_inc(kz_zero, 1)
            for va in (va_1, va_3):
                pool.memset(va[:, :, :, DK:VW], 1.0).then_inc(kz_zero, 1)
            pool.wait_ge(loaded[0], 16)
            pool.tensor_copy(identb[:, :], ident).then_inc(pool_const, 1)
            pool.tensor_copy(onesb[:, :], ones).then_inc(pool_const, 1)
            def masks():
                pool.wait_ge(loaded[2], 16)
                pool.tensor_copy(utrib[:, :], col["utri"]).then_inc(pool_const, 1)
                pool.wait_ge(mask1_loaded, 16)
                pool.tensor_scalar(neg1[:, :, :], mask1_i32[:, :, :], 0.0, NEG, ALU.is_equal, ALU.mult).then_inc(pool_const, 1)
                pool.wait_ge(lens_loaded, 16)
                pool.tensor_copy(lens_f[:, :], lens_i[:, :]).then_inc(pool_const, 1)
                pool.wait_ge(pool_const, 6)
                pool.tensor_scalar(qneg[:, :], lens_f[:, :], col["piota"], NEG, ALU.is_le, ALU.mult).then_inc(pool_const, 1)
                pool.wait_ge(pool_const, 7)
                for b in range(B):
                    pool.tensor_scalar(neg2[:, b, :], col["kiota"], lens_f[:, b:b + 1], qneg[:, b:b + 1], ALU.is_ge,
                                       ALU.mult).then_inc(pool_const, 1)

            def inverse_root(it, layer, name, out, src, scale, eps):
                ev = E[layer][name]
                pool.tensor_scalar(out, src, scale, eps, ALU.mult, ALU.add).then_inc(ev.sem, 1)
                pool.wait_ge(ev.sem, ev.at(it, 1))
                pool.tensor_tensor(out, out, minus_half, ALU.pow).then_inc(ev.sem, 1)

            def rs(it, layer):
                wait(pool, layer, "ln", it, 2)
                pool.sem_inc(pool_waited)
                inverse_root(it, layer, "rs", rstd[:, it.k, 0:1], mv[:, it.k, 1:2], 1.0, LN_EPS)

            def rs_hid(it):
                wait(pool, F2, "hid", it, 2)
                pool.sem_inc(pool_waited)
                inverse_root(it, F2, "rs_hid", rstd[:, it.k, 1:2], mv_h[:, it.k, 1:2], 1.0, LN_EPS)

            def rms(it, src, j, v, n, name):
                wait(pool, F3, src, it, j)
                pool.sem_inc(pool_waited)
                inverse_root(it, F3, name, v[:, it.k, 4:5], v[:, it.k, 0:1], 1.0 / n, 1e-8)

            def mask_keys(it, layer, kT):
                wait(pool, layer, "scores", it.back(2))
                pool.tensor_tensor(kz[:, it.k, :].rearrange("p (h t) -> p h t", h=H),
                                   kT[:, bass.ds(it.b, 1), :].to_broadcast([P, H, P]),
                                   col["hmask"].rearrange("p (h a) -> p h a", a=1).to_broadcast([P, H, P]),
                                   ALU.mult).then_inc(E[layer]["kz"].sem, 1)

            def copy_xnT(it):
                wait(pool, ROUTE, "xt_sb", it)
                pool.tensor_copy(xnT_all[:, bass.ds(it.b, 1), :], xnT[:, it.k:it.k + 1, :]).then_inc(E[ROUTE]["copied"].sem, 1)

            def keys_ready():
                pool.wait_ge(prep_act, 4)
                wait(pool, A0, "scores", Item(B - 1, B - 1))

            stages = {n: [] for n in range(len(LAG))}
            for layer in (A0, F0, A1, ROUTE, A2, F2, A3, F3):
                stages[layer] = [(0, rs, layer)]
            stages[A1] += [(0, mask_keys, A1, kT_1)]
            stages[A3] += [(0, mask_keys, A3, kT_3)]
            stages[ROUTE] += [(0, copy_xnT)]
            stages[F2] += [(1, rs_hid)]
            stages[F3] += [(0, rms, "quant", 1, qs, P, "rq"), (1, rms, "sumsq", 1, hs, F, "rh")]
            walk(pool, PLAN, stages, before={(A1, 0): keys_ready}, after={(A0, 1): masks})

        @block.scalar
        def _(act):
            def evac(dst, src, layer, name, **kw):
                act.activation(dst, src, ACT.Identity if kw else ACT.Copy, **kw).then_inc(E[layer][name].sem, 1)

            def xt_sb(it, layer):
                wait(act, layer, "xt", it)
                if layer == ROUTE:
                    wait(act, ROUTE, "copied", it.back(2))
                evac(xnT[:, it.k, :], bank[R_BANK[0]][:, 0:P], layer, "xt_sb")

            def exps(it, layer, g):
                wait(act, layer, "shifted", it, 2 * g + 2)
                act.activation(prob[:, g % 2, :], prob[:, g % 2, :], ACT.Exp,
                               scale=float(DK0 if layer == A0 else DK) ** -0.5).then_inc(E[layer]["probs"].sem, 1)

            def probsT_sb(it, layer, g):
                wait(act, layer, "probsT", it, g + 1)
                evac(probT[:, g % 2, :], bank[T_BANK[g % 2]][:, :], layer, "probsT_sb")

            def k_sb(it, c):
                wait(act, A0, "kps", it, c + 1)
                kv = kz[:, it.k, :].rearrange("p (t a n) -> p t a n", t=8, a=2)
                src = bank[R_BANK[0]][:, :].rearrange("p (t n) -> p t n", t=4)
                for a in range(2):
                    evac(kv[64 * a:64 * a + 64, 4 * c:4 * c + 4, a, :], src[64 * a:64 * a + 64], A0, "k_sb")

            def q_sb0(it, c):
                wait(act, A0, "qps", it, c + 1)
                evac(qT[:, it.k, 512 * c:512 * c + 512], bank[R_BANK[1]][:, :], A0, "q_sb")

            def q_sb(it, layer):
                wait(act, layer, "q", it)
                if layer == A3:
                    evac(qT[:, it.k, 0:P], bank[R_BANK[1]][:, 0:P], layer, "q_sb", bias=col["bq_3"])
                else:
                    evac(qT[:, it.k, 0:P], bank[R_BANK[1]][:, 0:P], layer, "q_sb")

            def ot_sb(it, layer):
                wait(act, layer, "ot", it)
                evac(oT[:, it.k, 0:P], bank[R_BANK[0]][:, 0:P], layer, "ot_sb")

            def exps2(it):
                wait(act, A2, "scores", it)
                wait(act, A2, "shift", it)
                act.activation(prob[:, it.k, 0:P], bank[S_BANK[it.k]][:, 0:P], ACT.Exp, bias=mx[:, it.k, 1:2],
                               scale=float(P) ** -0.5, accum_out=rden[:, it.k, 1:2]).then_inc(E[A2]["probs"].sem, 1)

            def probsT_sb2(it):
                wait(act, A2, "probsT", it)
                evac(probT[:, it.k, 0:P], bank[T_BANK[it.k]][:, 0:P], A2, "probsT_sb")

            def xq_sb(it, layer):
                wait(act, layer, "xt", it)
                evac(xqT[:, it.k, :], bank[R_BANK[0]][:, 0:P], layer, "xt_sb", bias=minus_magic)

            def hq_sb(it, layer):
                wait(act, layer, "ht", it)
                evac(hqT[:, it.k, :], bank[T_BANK[it.k]][:, :], layer, "ht_sb", bias=minus_magic)

            def silu(it):
                wait(act, F0, "gate", it)
                wait(act, F0, "quant", it)
                wait(act, F0, "hid", it.back(2), 1)
                act.activation(sg[:, it.k, :], bank[S_BANK[0]][:, :], ACT.Silu, scale=qs[:, it.k, 3:4]
                               ).then_inc(E[F0]["silu"].sem, 1)

            def relu_sq(it):
                wait(act, F3, "up", it)
                wait(act, F3, "quant", it)
                wait(act, F3, "hid", it.back(2))
                act.activation(sg[:, it.k, :], bank[S_BANK[it.k]][:, :], ACT.Relu, scale=qs[:, it.k, 3:4]
                               ).then_inc(E[F3]["relu"].sem, 1)
                wait(act, F3, "relu", it)
                act.activation(hid[:, it.k, :], sg[:, it.k, :], ACT.Square).then_inc(E[F3]["sq"].sem, 1)

            def sumsq(it):
                wait(act, F3, "hid", it, 1)
                act.activation(sg[:, it.k, :], hid[:, it.k, :], ACT.Square, accum_out=hs[:, it.k, 0:1]
                               ).then_inc(E[F3]["sumsq"].sem, 1)

            def gelu2(it):
                wait(act, F2, "up", it)
                act.activation(hid[:, it.k, :], bank[S_BANK[it.k]][:, :], ACT.Gelu).then_inc(E[F2]["gelu"].sem, 1)

            def hT_sb2(it):
                wait(act, F2, "ht", it)
                evac(hid2[:, it.k, :], bank[T_BANK[it.k]][:, :], F2, "ht_sb")

            def gelu_e(it, tc):
                for ht in range(FT):
                    wait(act, MOE, "h", it, 4 * tc + ht + 1)
                    act.activation(hT[:, tc, ht, :], bank[ht][:, :], ACT.Gelu_apprx_tanh,
                                   bias=expert[:, it.k, F + ht:F + ht + 1]).then_inc(E[MOE]["gelu"].sem, 1)

            def prepare():
                act.wait_ge(loaded[0], 16)
                act.activation(tanh_g[:, :], col["gates"], ACT.Tanh).then_inc(act_const, 1)
                for n, (dst, kw) in enumerate([(kT_1, {}), (kT_3, dict(bias=col["bk_3"]))]):
                    for c in range(2):
                        act.wait_ge(prep_pe, 2 * n + c + 1)
                        act.activation(dst[:, 4 * c:4 * c + 4, :].rearrange("p b t -> p (b t)"), bank[2 * n + c][:, :],
                                       ACT.Identity if kw else ACT.Copy, **kw).then_inc(prep_act, 1)

            def route_exp():
                act.wait_ge(E[ROUTE]["lg"].sem, E[ROUTE]["lg"].at(Item(B - 1, B - 1)))
                act.activation(pr[:, :, :], lg[:, :, :], ACT.Exp).then_inc(rt_act, 1)

            def route_wT():
                act.wait_ge(rt_pe, 2)
                act.activation(w_tokT[:, :], bank[R_BANK[1]][0:B * NE, 0:P], ACT.Copy).then_inc(rt_act, 1)

            def attention(layer, pro0, pro1, epi):
                return [
                    (1, exps, layer, 0), (2, probsT_sb, layer, 3),
                    (1, exps, layer, 1), (1, probsT_sb, layer, 0), *pro0,
                    (1, exps, layer, 2), (1, probsT_sb, layer, 1), *pro1, *epi,
                    (1, exps, layer, 3), (1, probsT_sb, layer, 2)]

            stages = {
                A0: [(1, exps, A0, 0), (2, probsT_sb, A0, 3), (0, k_sb, 0),
                     (1, exps, A0, 1), (1, probsT_sb, A0, 0), (0, k_sb, 1), (0, xt_sb, A0),
                     (1, exps, A0, 2), (1, probsT_sb, A0, 1), (0, q_sb0, 0),
                     (1, exps, A0, 3), (1, probsT_sb, A0, 2), (0, q_sb0, 1)],
                F0: [(0, xq_sb, F0), (0, silu), (1, hq_sb, F0)],
                A1: attention(A1, [(0, xt_sb, A1)], [(0, q_sb, A1)], [(2, ot_sb, A1)]),
                ROUTE: [(0, xt_sb, ROUTE)],
                MOE: [(0, gelu_e, 0), (0, gelu_e, 1)],
                A2: [(2, ot_sb, A2), (0, xt_sb, A2), (1, exps2), (1, probsT_sb2)],
                F2: [(0, xt_sb, F2), (0, gelu2), (1, hT_sb2)],
                A3: attention(A3, [(0, xt_sb, A3)], [(0, q_sb, A3)], [(2, ot_sb, A3)]),
                F3: [(0, xq_sb, F3), (0, relu_sq), (1, sumsq), (1, hq_sb, F3)],
            }
            act.wait_ge(prep_dve, 1)
            act.wait_ge(kz_zero, 6)
            prepare()
            walk(act, PLAN, stages, before={(MOE, 0): route_exp, (MOE, 1): route_wT})

        @block.tensor
        def _(pe):
            def before_in_bank(layer, piece, b):
                mine = bank_of(layer, piece, b)
                here = order.index((layer, piece, b))
                return next((p for p in reversed(order[:here]) if bank_of(*p) == mine), None)

            def claim(it, layer, piece):
                found = before_in_bank(layer, piece, it.rep)
                if found is None:
                    return
                pl, pp, pb = found
                name, j = emptied[pl, pp]
                if pl != layer:
                    wait(pe, pl, name, Item(pb, pb), j)
                    if isinstance(it.b, int):
                        return
                    pl, pp, pb = before_in_bank(layer, piece, it.rep + 2)
                    pb -= 2
                    name, j = emptied[pl, pp]
                    assert pl == layer and E[layer][name].per * pb + j >= 0
                wait(pe, layer, name, Item(it.b + (pb - it.rep), pb), j)

            def bank_of(layer, piece, b):
                k = b % 2
                if layer == MOE:
                    return int(piece[2]) if piece[0] == "h" else O_BANK[int(piece[1])]
                if layer in (A0, A1, A3):
                    if piece[0] == "s":
                        return S_BANK[int(piece[1]) % 2]
                    if piece[0] == "t":
                        return T_BANK[int(piece[1]) % 2]
                    if piece.startswith("pv"):
                        return O_BANK[int(piece[2]) % 2 if layer == A0 else k]
                    return R_BANK[{"xt": 0, "k0": 0, "k1": 0, "q0": 1, "q1": 1, "v0": 0, "v1": 0, "ot0": 1, "ot1": 1,
                                   "y": 1, "q": 1, "ot": 0}[piece]]
                if layer == A2:
                    return {"xt": 6, "ot": 6, "y": 7, "s": S_BANK[k], "t": T_BANK[k], "pv": O_BANK[k]}[piece]
                if layer == F0:
                    return {"xt": 6, "gate": 0, "up": 1, "ht": T_BANK[k], "y": O_BANK[k]}[piece]
                if layer == ROUTE:
                    return {"xt": 6, "lg": S_BANK[0]}[piece]
                return {"xt": 6, "up": S_BANK[k], "ht": T_BANK[k], "y": O_BANK[k]}[piece]

            def xt(it, layer):
                wait(pe, layer, "ln" if layer not in (F0, F3) else "quant", it)
                claim(it, layer, "xt")
                src = xm if layer in (F0, F3) else xn
                pe.transpose(bank[R_BANK[0]][:, 0:P], src[:, it.k, :], ident).then_inc(E[layer]["xt"].sem, 1)

            def scores(it, layer, g):
                claim(it, layer, f"s{g}")
                out = bank[S_BANK[g % 2]]
                neg = {A0: neg0, A1: neg1, A3: None}[layer]
                if neg is not None:
                    if g == 0 and isinstance(it.b, int) and it.b == 0:
                        if layer == A0:
                            pe.wait_ge(prep_dve, 2)
                        pe.wait_ge(pool_const, 2 if layer == A0 else 5)
                    pe.matmul(out[:, :].rearrange("p (h t) -> p h t", h=GH), identb[:, :],
                              neg[:, bass.ds(it.b, 1), :].to_broadcast([P, GH, P]), start=True, stop=False)
                if layer == A0:
                    wait(pe, A0, "q_sb", it, 1 + g // 2)
                    wait(pe, A0, "k_sb", it, 2 + 2 * (g // 2))
                    for c in range(2):
                        t = 2 * g + c
                        mm_ = pe.matmul(out[:, 256 * c:256 * c + 256], qT[:, it.k, P * t:P * t + P],
                                        kz[:, it.k, 256 * t:256 * t + 256], start=False, stop=(c == 1))
                else:
                    wait(pe, layer, "q_sb", it)
                    wait(pe, layer, "kz", it)
                    mm_ = pe.matmul(out[:, :], qT[:, it.k, 0:P], kz[:, it.k, 512 * g:512 * g + 512],
                                    start=neg is None, stop=True)
                mm_.then_inc(E[layer]["scores"].sem, 1)

            def probsT(it, layer, g):
                wait(pe, layer, "probs", it, g + 1)
                claim(it, layer, f"t{g}")
                for j in range(GH):
                    mm_ = pe.transpose(bank[T_BANK[g % 2]][:, P * j:P * j + P], prob[:, g % 2, P * j:P * j + P], ident)
                mm_.then_inc(E[layer]["probsT"].sem, 1)

            def pv(it, layer, g):
                wait(pe, layer, "probsT_sb", it, g + 1)
                if layer == A0:
                    wait(pe, A0, "v_sb", it, 1 + g // 2)
                    claim(it, layer, f"pv{g}")
                elif g == 0:
                    claim(it, layer, "pv0")
                for j in range(GH):
                    h = GH * g + j
                    if layer == A0:
                        mm_ = pe.matmul(bank[O_BANK[g % 2]][:, VW0 * j:VW0 * j + VW0], probT[:, g % 2, P * j:P * j + P],
                                        va0[:, it.k, h, :], start=True, stop=True)
                    else:
                        va = va_1 if layer == A1 else va_3
                        mm_ = pe.matmul(bank[O_BANK[it.k]][:, VW * h:VW * h + VW], probT[:, g % 2, P * j:P * j + P],
                                        va[:, bass.ds(it.b, 1), h, :], start=True, stop=True)
                mm_.then_inc(E[layer]["pv"].sem, 1)

            def proj0(it, which, c):
                piece = f"{which}{c}"
                if which == "q" and c == 0:
                    wait(pe, A0, "xt_sb", it)
                if which == "v" and c == 0:
                    pe.wait_ge(ctk_loaded[it.k], 8 * it.b + 16 - 8 * it.k)
                claim(it, A0, piece)
                out = bank[bank_of(A0, piece, it.rep)]
                if which == "v":
                    mm_ = pe.matmul(out[:, :], ctk[:, it.k, :], col["wvT_0"][:, 512 * c:512 * c + 512], start=True, stop=True)
                else:
                    w = col["wkT_0" if which == "k" else "wqT_0"]
                    for t in range(4):
                        rhs = ctxT[:, bass.ds(it.b, 1), :] if which == "k" else xnT[:, it.k:it.k + 1, :]
                        mm_ = pe.matmul(out[:, P * t:P * t + P].rearrange("p (a n) -> p a n", a=1),
                                        w[:, 512 * c + P * t:512 * c + P * t + P], rhs, start=True, stop=True)
                mm_.then_inc(E[A0][which + "ps"].sem, 1)

            def ot0(it, c):
                wait(pe, A0, "norm", it, 4 * c + 4)
                piece = f"ot{c}"
                claim(it, A0, piece)
                out = bank[bank_of(A0, piece, it.rep)]
                for t in range(4):
                    mm_ = pe.transpose(out[:, P * t:P * t + P], o_n[:, it.k, 512 * c + P * t:512 * c + P * t + P], ident)
                mm_.then_inc(E[A0]["ot"].sem, 1)

            def y0(it):
                wait(pe, A0, "ot_sb", it)
                claim(it, A0, "y")
                out = bank[R_BANK[1]][:, 0:P]
                for t in range(8):
                    mm_ = pe.matmul(out, oT[:, it.k, P * t:P * t + P], col["woT_0"][:, P * t:P * t + P],
                                    start=(t == 0), stop=(t == 7))
                mm_.then_inc(E[A0]["y"].sem, 1)

            def q(it, layer):
                wait(pe, layer, "xt_sb", it)
                claim(it, layer, "q")
                pe.matmul(bank[R_BANK[1]][:, 0:P], col["wqT_1" if layer == A1 else "wqT_3"], xnT[:, it.k, :],
                          start=True, stop=True).then_inc(E[layer]["q"].sem, 1)

            def ot(it, layer):
                wait(pe, layer, "norm", it)
                claim(it, layer, "ot")
                pe.transpose(bank[R_BANK[0]][:, 0:P], o_n[:, it.k, 0:P], ident).then_inc(E[layer]["ot"].sem, 1)

            def y(it, layer):
                n = {A1: 1, A2: 2, A3: 3}[layer]
                claim(it, layer, "y")
                out = bank[R_BANK[1]][:, 0:P]
                pe.matmul(out, ones[0:1, :], row[f"bo_{n}"], start=True, stop=False)
                wait(pe, layer, "ot_sb", it)
                pe.matmul(out, oT[:, it.k, 0:P], col[f"woT_{n}"], start=False, stop=True).then_inc(E[layer]["y"].sem, 1)

            def scores2(it):
                wait(pe, A2, "xt_sb", it)
                claim(it, A2, "s")
                if it.rep == 0:
                    pe.wait_ge(pool_const, 7 + B)
                out = bank[S_BANK[it.k]][:, 0:P].rearrange("p (a n) -> p a n", a=1)
                pe.matmul(out, identb[:, :], neg2[:, bass.ds(it.b, 1), :], start=True, stop=False)
                pe.matmul(out, xnT[:, it.k, :], ctxT[:, bass.ds(it.b, 1), :], start=False, stop=True
                          ).then_inc(E[A2]["scores"].sem, 1)

            def probsT2(it):
                wait(pe, A2, "probs", it)
                claim(it, A2, "t")
                pe.transpose(bank[T_BANK[it.k]][:, 0:P], prob[:, it.k, 0:P], ident).then_inc(E[A2]["probsT"].sem, 1)

            def pv2(it):
                wait(pe, A2, "probsT_sb", it)
                claim(it, A2, "pv")
                pe.matmul(bank[O_BANK[it.k]][:, 0:P].rearrange("p (a n) -> p a n", a=1), probT[:, it.k, 0:P],
                          ctx_tok[:, bass.ds(it.b, 1), :], start=True, stop=True).then_inc(E[A2]["pv"].sem, 1)

            def up(it, layer, piece, w, lhs):
                wait(pe, layer, "xt_sb", it)
                claim(it, layer, piece)
                pe.matmul(bank[bank_of(layer, piece, it.rep)][:, :], lhs[:, it.k, :], w, start=True, stop=True
                          ).then_inc(E[layer][piece].sem, 1)

            def ht(it, layer):
                src = hid2 if layer != F2 else hid
                if layer == F3:
                    wait(pe, layer, "hq", it)
                else:
                    wait(pe, layer, "hid", it)
                claim(it, layer, "ht")
                for t in range(FT):
                    mm_ = pe.transpose(bank[T_BANK[it.k]][:, P * t:P * t + P], src[:, it.k, P * t:P * t + P], ident)
                mm_.then_inc(E[layer]["ht"].sem, 1)

            def y_ffn(it, layer, w):
                wait(pe, layer, "ht_sb", it)
                claim(it, layer, "y")
                out = bank[O_BANK[it.k]][:, 0:P]
                if layer == F2:
                    pe.matmul(out, ones[0:1, :], crow[:, :], start=True, stop=False)
                src = hid2 if layer == F2 else hqT
                for t in range(FT):
                    mm_ = pe.matmul(out, src[:, it.k, P * t:P * t + P], w[:, P * t:P * t + P],
                                    start=(t == 0 and layer != F2), stop=(t == FT - 1))
                mm_.then_inc(E[layer]["y"].sem, 1)

            def logits(it):
                wait(pe, ROUTE, "xt_sb", it)
                claim(it, ROUTE, "lg")
                pe.matmul(bank[S_BANK[0]][:, 0:NE], xnT[:, it.k, :], col["wg"], start=True, stop=True
                          ).then_inc(E[ROUTE]["logits"].sem, 1)

            def hidden(it, piece):
                tc, t = int(piece[1]), int(piece[2])
                claim(it, MOE, piece)
                if piece == "h00":
                    pe.wait_ge(expert_loaded[it.k], 8 * it.b + 16 - 8 * it.k)
                pe.matmul(bank[t][:, :], expert[:, it.k, P * t:P * t + P],
                          xnT_all[:, 4 * tc:4 * tc + 4, :].rearrange("p b t -> p (b t)"), start=True, stop=True
                          ).then_inc(E[MOE]["h"].sem, 1)

            def down(it, piece):
                tc = int(piece[1])
                claim(it, MOE, piece)
                wait(pe, MOE, "gelu", it, 4 * tc + 4)
                for tt in range(4):
                    for t in range(FT):
                        mm_ = pe.matmul(bank[O_BANK[tc]][:, P * tt:P * tt + P], hT[:, tc, t, P * tt:P * tt + P],
                                        expert[:, it.k, F + FT + P * t:F + FT + P * t + P],
                                        start=(t == 0), stop=(t == FT - 1))
                mm_.then_inc(E[MOE]["y"].sem, 1)

            def prepare():
                pe.wait_ge(loaded[0], 16)
                for n, w in enumerate(("wkT_1", "wkT_3")):
                    for c in range(2):
                        pe.matmul(bank[2 * n + c][:, :], col[w], ctxT[:, 4 * c:4 * c + 4, :].rearrange("p b t -> p (b t)"),
                                  start=True, stop=True).then_inc(prep_pe, 1)
                pe.wait_ge(rows_loaded, 16)
                for b in range(B):
                    if b >= 4:
                        pe.wait_ge(prep_dve, 2 + 2 * (b - 3))
                    out = bank[4 + b % 4][:, 0:2 * P]
                    pe.matmul(out, ones[0:1, :], row["bv_13"], start=True, stop=False)
                    pe.matmul(out, ctxT[:, b, :], col["wvT_13"], start=False, stop=True).then_inc(prep_pe, 1)
                pe.wait_ge(prep_act, 4)
                pe.wait_ge(prep_dve, 2 + 2 * B)
                pe.wait_ge(kz_zero, 6)
                pe.wait_ge(loaded[1], 16)

            def weight_sums():
                pe.wait_ge(red_dve, len(TERNARY))
                wait(pe, A0, "v_sb", Item(3, 3))
                pe.matmul(bank[R_BANK[0]][:, 0:len(TERNARY)], ones, asum[:, :], start=True, stop=True).then_inc(red_pe, 1)
                pe.wait_ge(red_dve, len(TERNARY) + 1)

            def route_places(it):
                if it.rep:
                    return
                pe.wait_ge(rt_dve, RT_CHOSEN)
                out = bank[R_BANK[0]][:, 0:B * NE]
                pe.matmul(out, utrib[:, :], chosen[:, :, :].rearrange("p b e -> p (b e)"), start=True, stop=False)
                pe.matmul(out, onesb[:, :], before_b[:, :, :].rearrange("p b e -> p (b e)"), start=False, stop=True
                          ).then_inc(rt_pe, 1)

            def route_bias():
                pe.wait_ge(rt_dve, RT_WEIGHTS)
                pe.transpose(bank[R_BANK[1]][0:B * NE, 0:P], w_tok[:, :, :].rearrange("p b e -> p (b e)"), ident
                             ).then_inc(rt_pe, 1)
                pe.wait_ge(rt_act, 2)
                pe.wait_ge(b2_loaded, 16)
                for c in range(2):
                    pe.matmul(bank[R_BANK[c]][:, :], w_tokT[:, :], b2blk[:, 512 * c:512 * c + 512], start=True, stop=True
                              ).then_inc(rt_pe, 1)

            def moe_ready():
                wait(pe, ROUTE, "copied", Item(B - 1, B - 1))

            def fold():
                pe.wait_ge(tern_dve, 3 * len(TERNARY))
                wait(pe, A2, "resid", Item(B - 2, B - 2))
                for t in range(FT):
                    mm_ = pe.matmul(bank[R_BANK[1]][0:1, 0:P], col["lnb_2"][:, t:t + 1], tern["projT"][:, P * t:P * t + P],
                                    start=(t == 0), stop=(t == FT - 1))
                mm_.then_inc(fold_pe, 1)
                pe.wait_ge(fold_dve, FT + 1)

            def attention(layer):
                return [
                    (1, scores, layer, 0), (2, probsT, layer, 3), (2, pv, layer, 2),
                    (1, scores, layer, 1), (1, probsT, layer, 0), (2, pv, layer, 3), (0, xt, layer),
                    (1, scores, layer, 2), (1, probsT, layer, 1), (0, q, layer), (2, ot, layer), (1, pv, layer, 0),
                    (1, scores, layer, 3), (2, y, layer), (1, probsT, layer, 2), (1, pv, layer, 1)]

            stages = {
                A0: [(1, scores, A0, 0), (2, probsT, A0, 3), (2, pv, A0, 2), (0, proj0, "k", 0),
                     (1, scores, A0, 1), (1, probsT, A0, 0), (2, pv, A0, 3), (0, proj0, "k", 1), (0, xt, A0),
                     (1, scores, A0, 2), (1, probsT, A0, 1), (1, pv, A0, 0), (0, proj0, "v", 0), (0, proj0, "q", 0),
                     (2, ot0, 0),
                     (1, scores, A0, 3), (1, probsT, A0, 2), (1, pv, A0, 1), (0, proj0, "v", 1), (0, proj0, "q", 1),
                     (2, ot0, 1), (2, y0)],
                F0: [(0, xt, F0), (0, up, F0, "gate", tern["gateT"][:, :], xqT), (0, up, F0, "up", tern["upT"][:, :], xqT),
                     (1, ht, F0), (1, y_ffn, F0, tern["downT"])],
                A1: attention(A1),
                ROUTE: [(1, logits), (0, xt, ROUTE)],
                MOE: [(0, hidden, "h00"), (0, hidden, "h01"), (0, hidden, "h02"), (0, hidden, "h03"), (1, down, "y1"),
                      (0, hidden, "h10"), (0, hidden, "h11"), (0, hidden, "h12"), (0, hidden, "h13"), (0, route_places),
                      (0, down, "y0")],
                A2: [(2, ot, A2), (0, xt, A2), (2, y, A2), (1, probsT2), (0, scores2), (1, pv2)],
                F2: [(0, xt, F2), (0, up, F2, "up", tern["fcT"][:, :], xnT), (1, ht, F2), (1, y_ffn, F2, projw)],
                A3: attention(A3),
                F3: [(0, xt, F3), (0, up, F3, "up", tern["w1T"][:, :], xqT), (1, ht, F3), (1, y_ffn, F3, tern["w2T"])],
            }

            def piece_name(layer, fn, args):
                if fn is xt:
                    return "xt"
                if fn in (scores, probsT, pv):
                    return {scores: "s", probsT: "t", pv: "pv"}[fn] + str(args[1])
                if fn is proj0:
                    return args[0] + str(args[1])
                if fn is ot0:
                    return f"ot{args[0]}"
                if fn is up:
                    return args[1]
                if fn in (hidden, down):
                    return args[0]
                return {y0: "y", q: "q", ot: "ot", y: "y", scores2: "s", probsT2: "t", pv2: "pv", ht: "ht",
                        y_ffn: "y", logits: "lg"}[fn]

            order = []
            for what in PLAN:
                steps = what[1] if what[0] == "peel" else [(what[1], s) for s in range(what[2], what[2] + 2 * what[3])]
                for layer, s in steps:
                    for lag, fn, *args in stages[layer]:
                        if 0 <= s - lag < B and fn is not route_places:
                            order.append((layer, piece_name(layer, fn, args), s - lag))

            def ternary_ready(n):
                return lambda: pe.wait_ge(tern_dve, 3 * n)

            prepare()
            walk(pe, PLAN, stages,
                 before={(F0, 0): ternary_ready(3), (F2, 0): fold, (MOE, 0): moe_ready, (MOE, 1): route_bias,
                         (A2, 0): lambda: pe.wait_ge(rt_dve, RT_BIAS)},
                 after={(A0, 3): weight_sums})

        @block.vector
        def _(dve):
            def chain(layer, name, it, start=0):
                ev = E[layer][name]
                count = [start]

                def do(ins, hold=True, alone=False):
                    ins.then_inc(ev.sem, 1)
                    count[0] += 1
                    if hold:
                        dve.wait_ge(ev.sem, ev.at(it, count[0]))
                    if alone:
                        dve.sem_inc(dve_waited)
                return do

            def xs(it):
                return x_sb[:, bass.ds(it.b, 1), :]

            BEFORE = {F0: A0, A1: F0, ROUTE: A1, A2: ROUTE, F2: A2, A3: F2, F3: A3}

            def ln_stats(it, layer):
                if layer == A0:
                    if it.rep == 0:
                        dve.wait_ge(loaded[5], 16)
                elif layer == A2:
                    if it.rep == 0:
                        wait(dve, MOE, "acc", Item(NE - 1, NE - 1))
                else:
                    wait(dve, BEFORE[layer], "resid", it)
                do = chain(layer, "ln", it)
                do(dve.bn_stats(stats[:, it.k, :], xs(it)), alone=True)
                do(dve.bn_aggr(mv[:, it.k, :], stats[:, it.k, :]), hold=False)

            def ln(it, layer):
                k = it.k
                wait(dve, layer, "rs", it)
                if it.rep >= 2:
                    wait(dve, layer, "xt", it.back(2))
                elif layer in BEFORE:
                    last = Item(B - 2 + k, B - 2 + k)
                    wait(dve, BEFORE[layer], "quant" if BEFORE[layer] == F0 else "xt", last)
                do = chain(layer, "ln", it, 2)
                do(dve.tensor_scalar(xn[:, k:k + 1, :], xs(it), mv[:, k, 0:1], rstd[:, k, 0:1], ALU.subtract, ALU.mult),
                   hold=layer in (F0, F3))

            def resid(it, layer):
                n = {A0: 0, A1: 1, A2: 2, A3: 3, F2: 6}[layer]
                wait(dve, layer, "y", it)
                out = bank[O_BANK[it.k] if layer == F2 else R_BANK[1]][:, 0:P].rearrange("p (a n) -> p a n", a=1)
                dve.scalar_tensor_tensor(xs(it), out, tanh_g[:, n:n + 1], xs(it), ALU.mult, ALU.add
                                         ).then_inc(E[layer]["resid"].sem, 1)

            def resid_q(it, layer):
                wait(dve, layer, "y", it)
                scale = hs[:, it.k, 7:8]
                dve.scalar_tensor_tensor(xs(it), bank[O_BANK[it.k]][:, 0:P].rearrange("p (a n) -> p a n", a=1), scale,
                                         xs(it), ALU.mult, ALU.add).then_inc(E[layer]["resid"].sem, 1)

            def shifted(it, layer, g):
                src = bank[S_BANK[g % 2]][:, :].rearrange("p (h t) -> p h t", h=GH)
                m = mx[:, g % 2, :]
                wait(dve, layer, "scores", it, g + 1)
                do = chain(layer, "shifted", it, 2 * g)
                do(dve.tensor_reduce(m, src, AX.X, ALU.max))
                ev = E[layer]["probsT"]
                if not isinstance(it.b, int) or 4 * it.b + g - 1 > 0:
                    dve.wait_ge(ev.sem, 4 * it.b + g - 1)
                do(dve.tensor_tensor(prob[:, g % 2, :].rearrange("p (h t) -> p h t", h=GH), src,
                                     m.rearrange("p (h a) -> p h a", a=1).to_broadcast([P, GH, P]), ALU.subtract),
                   hold=False)

            def v_sb(it, c):
                wait(dve, A0, "vps", it, c + 1)
                wait(dve, A0, "pv", it.back(2))
                dve.tensor_copy(va0[:, it.k, 8 * c:8 * c + 8, 0:DK0], bank[bank_of_v[c]][:, :].rearrange(
                    "p (h n) -> p h n", h=8)).then_inc(E[A0]["v_sb"].sem, 1)

            def ot_sb0(it, c):
                wait(dve, A0, "ot", it, c + 1)
                if c == 0:
                    wait(dve, A0, "y", it.back(2))
                dve.tensor_copy(oT[:, it.k, 512 * c:512 * c + 512], bank[R_BANK[1]][:, :]).then_inc(E[A0]["ot_sb"].sem, 1)

            def norm0(it, g):
                src = bank[O_BANK[g % 2]][:, 0:GH * VW0].rearrange("p (h n) -> p h n", h=GH)
                wait(dve, A0, "pv", it, g + 1)
                do = chain(A0, "norm", it, 2 * g)
                r = rden[:, it.k, GH * g:GH * g + GH].rearrange("p (h a) -> p h a", a=1)
                do(dve.reciprocal(r, src[:, :, DK0:VW0]))
                if g == 0:
                    wait(dve, A0, "ot", it.back(2))
                do(dve.tensor_tensor(o_n[:, it.k, 256 * g:256 * g + 256].rearrange("p (h n) -> p h n", h=GH),
                                     src[:, :, 0:DK0], r.to_broadcast([P, GH, DK0]), ALU.mult), hold=False)

            def norm(it, layer):
                src = bank[O_BANK[it.k]][:, 0:H * VW].rearrange("p (h n) -> p h n", h=H)
                wait(dve, layer, "pv", it)
                do = chain(layer, "norm", it)
                r = rden[:, it.k, :].rearrange("p (h a) -> p h a", a=1)
                do(dve.reciprocal(r, src[:, :, DK:VW]))
                wait(dve, layer, "ot", it.back(2))
                do(dve.tensor_tensor(o_n[:, it.k, 0:P].rearrange("p (h n) -> p h n", h=H), src[:, :, 0:DK],
                                     r.to_broadcast([P, H, DK]), ALU.mult), hold=False)

            def shift2(it):
                wait(dve, A2, "scores", it)
                wait(dve, A2, "probs", it.back(2))
                do = chain(A2, "shift", it)
                do(dve.tensor_reduce(mx[:, it.k, 0:1], bank[S_BANK[it.k]][:, 0:P], AX.X, ALU.max))
                do(dve.tensor_scalar(mx[:, it.k, 1:2], mx[:, it.k, 0:1], -float(P) ** -0.5, None, ALU.mult), hold=False)

            def norm2(it):
                wait(dve, A2, "pv", it)
                wait(dve, A2, "probs", it)
                do = chain(A2, "norm", it)
                do(dve.reciprocal(rden[:, it.k, 0:1], rden[:, it.k, 1:2]))
                wait(dve, A2, "ot", it.back(2))
                do(dve.tensor_scalar(o_n[:, it.k, 0:P], bank[O_BANK[it.k]][:, 0:P], rden[:, it.k, 0:1], None, ALU.mult),
                   hold=False)

            def quant0(it):
                k = it.k
                if it.rep == 0:
                    dve.wait_ge(red_dve, RED_DONE)
                do = chain(F0, "quant", it)
                do(dve.tensor_reduce(qs[:, k, 0:1], xn[:, k, :], AX.X, ALU.max, apply_absolute_value=True))
                do(dve.tensor_scalar(qs[:, k, 1:2], qs[:, k, 0:1], 1e-5, 1.0 / 127.0, ALU.max, ALU.mult))
                do(dve.reciprocal(qs[:, k, 2:3], qs[:, k, 1:2]))
                do(dve.tensor_scalar(qs[:, k, 3:5], wmean[:, 0:2], qs[:, k, 1:2], None, ALU.mult))
                wait(dve, F0, "xt", it.back(2))
                do(dve.tensor_scalar(xm[:, k, :], xn[:, k, :], qs[:, k, 2:3], MAGIC, ALU.mult, ALU.add))

            def hid0(it):
                k = it.k
                wait(dve, F0, "up", it)
                wait(dve, F0, "silu", it)
                do = chain(F0, "hid", it)
                do(dve.scalar_tensor_tensor(hid[:, k, :], bank[S_BANK[1]][:, :], qs[:, k, 4:5], sg[:, k, :], ALU.mult, ALU.mult))
                do(dve.tensor_reduce(hs[:, k, 0:1], hid[:, k, :], AX.X, ALU.max, apply_absolute_value=True))
                do(dve.tensor_scalar(hs[:, k, 1:2], hs[:, k, 0:1], 1e-5, 1.0 / 127.0, ALU.max, ALU.mult))
                do(dve.reciprocal(hs[:, k, 2:3], hs[:, k, 1:2]))
                do(dve.tensor_scalar(hs[:, k, 7:8], hs[:, k, 1:2], wmean[:, 2:3], tanh_g[:, 4:5], ALU.mult, ALU.mult))
                wait(dve, F0, "ht", it.back(2))
                do(dve.tensor_scalar(hid2[:, k, :], hid[:, k, :], hs[:, k, 2:3], MAGIC, ALU.mult, ALU.add))

            def rms_quant(do, v, wm, xw):
                do(dve.tensor_scalar(v[:, 5:6], v[:, 1:2], v[:, 4:5], 1e-5, ALU.mult, ALU.max))
                do(dve.reciprocal(v[:, 6:7], v[:, 5:6]))
                do(dve.tensor_scalar(v[:, 6:7], v[:, 6:7], v[:, 4:5], 127.0, ALU.mult, ALU.mult))
                do(dve.tensor_scalar(v[:, 3:4], v[:, 5:6], wm, 1.0 / 127.0, ALU.mult, ALU.mult))
                do(dve.tensor_scalar(xw, xw, v[:, 6:7], MAGIC, ALU.mult, ALU.add))

            def quant3(it):
                k = it.k
                do = chain(F3, "quant", it)
                wait(dve, F3, "xt", it.back(2))
                do(dve.tensor_tensor_reduce(xm[:, k, :], xn[:, k, :], xn[:, k, :], 1.0, 0.0, ALU.mult, ALU.add, qs[:, k, 0:1]))
                do(dve.tensor_tensor(xm[:, k, :], xn[:, k, :], col["nw1"], ALU.mult))
                do(dve.tensor_reduce(qs[:, k, 1:2], xm[:, k, :], AX.X, ALU.max, apply_absolute_value=True))
                wait(dve, F3, "rq", it)
                rms_quant(do, qs[:, k, :], wmean[:, 5:6], xm[:, k, :])

            def hid3(it):
                k = it.k
                wait(dve, F3, "sq", it)
                do = chain(F3, "hid", it)
                do(dve.tensor_scalar(hid[:, k, :], hid[:, k, :], col["act_sb"][:, 0:1], col["act_sb"][:, 1:2],
                                     ALU.mult, ALU.add))
                wait(dve, F3, "ht", it.back(2))
                do(dve.tensor_tensor(hid2[:, k, :], hid[:, k, :], col["nw2"], ALU.mult))

            def hq3(it):
                k = it.k
                do = chain(F3, "hq", it)
                do(dve.tensor_reduce(hs[:, k, 1:2], hid2[:, k, :], AX.X, ALU.max, apply_absolute_value=True))
                wait(dve, F3, "rh", it)
                rms_quant(do, hs[:, k, :], wmean[:, 6:7], hid2[:, k, :])
                do(dve.tensor_scalar(hs[:, k, 7:8], hs[:, k, 3:4], tanh_g[:, 7:8], None, ALU.mult))

            def hid2_ln(it):
                k = it.k
                wait(dve, F2, "gelu", it)
                do = chain(F2, "hid", it)
                do(dve.bn_stats(stats[:, k, :], hid[:, k, :]), alone=True)
                do(dve.bn_aggr(mv_h[:, k, :], stats[:, k, :]), hold=False)
                wait(dve, F2, "rs_hid", it)
                do(dve.tensor_scalar(hid[:, k, :], hid[:, k, :], mv_h[:, k, 0:1], rstd[:, k, 1:2], ALU.subtract, ALU.mult),
                   hold=False)

            def lg_sb(it):
                wait(dve, ROUTE, "logits", it)
                do = chain(ROUTE, "lg", it)
                src = bank[S_BANK[0]][:, 0:NE].rearrange("p (a n) -> p a n", a=1)
                do(dve.tensor_reduce(rden[:, it.k, 2:3], src, AX.X, ALU.max))
                do(dve.tensor_scalar(lg[:, bass.ds(it.b, 1), :], src, rden[:, it.k, 2:3], None, ALU.subtract))

            def acc(it, tc):
                wait(dve, MOE, "y", it, tc + 1)
                wait(dve, MOE, "acc", it.back(1), 4 * tc + 4)
                for tt in range(4):
                    b = 4 * tc + tt
                    dve.scalar_tensor_tensor(x_sb[:, b, :], bank[O_BANK[tc]][:, P * tt:P * tt + P],
                                             w_tok[:, b, bass.ds(it.b, 1)], x_sb[:, b, :], ALU.mult, ALU.add
                                             ).then_inc(E[MOE]["acc"].sem, 1)

            class Count:

                def __init__(self, s):
                    self.s, self.n = s, 0

                def do(self, ins, hold=True):
                    ins.then_inc(self.s, 1)
                    self.n += 1
                    if hold:
                        dve.wait_ge(self.s, self.n)

            rt = Count(rt_dve)

            def route():
                def bc(ap):
                    return ap.rearrange("p (b a) -> p b a", a=1).to_broadcast([P, B, NE])

                dve.wait_ge(rt_act, 1)
                rt.do(dve.tensor_reduce(psum_r[:, :], pr[:, :, :], AX.X, ALU.add))
                rt.do(dve.reciprocal(psum_r[:, :], psum_r[:, :]))
                rt.do(dve.tensor_tensor(pr[:, :, :], pr[:, :, :], bc(psum_r[:, :]), ALU.mult))
                for b in range(B):
                    rt.do(dve.max(top[:, b, :], pr[:, b, :]), hold=(b == B - 1))
                for b in range(B):
                    rt.do(dve.max_index(topi[:, b, :], top[:, b, :], pr[:, b, :]), hold=(b == B - 1))
                rt.do(dve.tensor_copy(topf[:, :, :], topi[:, :, :]), hold=False)
                rt.do(dve.tensor_tensor(gsum[:, :], top[:, :, 0], top[:, :, 1], ALU.add))
                rt.do(dve.reciprocal(gsum[:, :], gsum[:, :]), hold=False)
                eiota = col["eiota"].rearrange("p (a e) -> p a e", a=1).to_broadcast([P, B, NE])
                rt.do(dve.tensor_tensor(oh1[:, :, :], eiota, topf[:, :, 0:1].to_broadcast([P, B, NE]), ALU.is_equal), hold=False)
                rt.do(dve.tensor_tensor(oh2[:, :, :], eiota, topf[:, :, 1:2].to_broadcast([P, B, NE]), ALU.is_equal))
                rt.do(dve.tensor_tensor(chosen[:, :, :], oh1[:, :, :], oh2[:, :, :], ALU.add), hold=False)
                rt.do(dve.memset(before_b[:, 0, :], 0.0))
                for b in range(1, B):
                    rt.do(dve.tensor_tensor(before_b[:, b, :], before_b[:, b - 1, :], chosen[:, b - 1, :], ALU.add))
                assert rt.n == RT_CHOSEN, rt.n
                rt.do(dve.tensor_tensor(g12[:, :, :], top[:, :, 0:2],
                                        gsum[:, :].rearrange("p (b a) -> p b a", a=1).to_broadcast([P, B, 2]), ALU.mult))
                rt.do(dve.tensor_scalar(g12[:, :, :], g12[:, :, :], tanh_g[:, 5:6], None, ALU.mult))
                rt.do(dve.tensor_tensor(oh1[:, :, :], oh1[:, :, :], g12[:, :, 0:1].to_broadcast([P, B, NE]), ALU.mult), hold=False)
                rt.do(dve.tensor_tensor(oh2[:, :, :], oh2[:, :, :], g12[:, :, 1:2].to_broadcast([P, B, NE]), ALU.mult))
                rt.do(dve.tensor_tensor(w_tok[:, :, :], oh1[:, :, :], oh2[:, :, :], ALU.add))
                dve.wait_ge(rt_pe, 1)
                rt.do(dve.tensor_scalar(keep[:, :, :], bank[R_BANK[0]][:, 0:B * NE].rearrange("p (b e) -> p b e", b=B),
                                        float(CAP), None, ALU.is_lt))
                rt.do(dve.tensor_tensor(w_tok[:, :, :], w_tok[:, :, :], keep[:, :, :], ALU.mult))
                assert rt.n == RT_WEIGHTS, rt.n

            def route_bias():
                wait(dve, MOE, "acc", Item(0, 0), 4)
                for c in range(2):
                    dve.wait_ge(rt_pe, 3 + c)
                    xc = x_sb[:, 4 * c:4 * c + 4, :]
                    rt.do(dve.tensor_tensor(xc, xc, bank[R_BANK[c]][:, :].rearrange("p (b n) -> p b n", b=4), ALU.add))
                assert rt.n == RT_BIAS, rt.n

            def weight_sums():
                rd = Count(red_dve)
                dve.wait_ge(loaded[3], 16)
                for n, name in enumerate(TERNARY):
                    rd.do(dve.tensor_reduce(asum[:, n:n + 1], col[name], AX.X, ALU.add, apply_absolute_value=True), hold=False)
                dve.wait_ge(red_pe, 1)
                rd.do(dve.tensor_scalar(wmean[:, :], bank[R_BANK[0]][:, 0:len(TERNARY)], 1.0 / (P * F), None, ALU.mult))
                rd.do(dve.tensor_scalar(wmean[:, 0:3], wmean[:, 0:3], 1e-5, None, ALU.max), hold=False)
                rd.do(dve.tensor_scalar(wmean[:, 3:5], wmean[:, 3:5], 1e-6, None, ALU.add), hold=False)
                rd.do(dve.tensor_scalar(wmean[:, 5:7], wmean[:, 5:7], 1e-5, None, ALU.max))
                rd.do(dve.reciprocal(winv[:, :], wmean[:, :]))
                assert rd.n == RED_DONE
                tern_count = Count(tern_dve)
                for n, name in enumerate(TERNARY):
                    t = tmp_t[:, n % 2, :]
                    tern_count.do(dve.tensor_scalar(t, col[name], winv[:, n:n + 1], -1.0, ALU.mult, ALU.max))
                    tern_count.do(dve.tensor_scalar(t, t, 1.0, MAGIC, ALU.min, ALU.add))
                    tern_count.do(dve.tensor_scalar(tern[name][:, :], t, MAGIC, None, ALU.subtract), hold=False)

            def fold():
                fd = Count(fold_dve)
                dve.wait_ge(tern_dve, 3 * len(TERNARY))
                for t in range(FT):
                    fd.do(dve.tensor_scalar(projw[:, P * t:P * t + P], tern["projT"][:, P * t:P * t + P],
                                            col["lnw_2"][:, t:t + 1], None, ALU.mult), hold=False)
                dve.wait_ge(fold_pe, 1)
                fd.do(dve.tensor_copy(crow[:, :], bank[R_BANK[1]][0:1, 0:P]), hold=False)

            def prepare():
                dve.memset(minus_magic, -MAGIC).then_inc(prep_dve, 1)
                dve.wait_ge(loaded[0], 16)
                dve.wait_ge(mask0_loaded, 16)
                dve.scalar_tensor_tensor(neg0[:, :, :], mask0_u8[:, :, :], NEG,
                                         col["causal"].rearrange("p (a t) -> p a t", a=1).to_broadcast([P, B, P]),
                                         ALU.mult, ALU.min).then_inc(prep_dve, 1)
                dve.wait_ge(kz_zero, 6)
                for b in range(B):
                    dve.wait_ge(prep_pe, 4 + b + 1)
                    for n, va in enumerate((va_1, va_3)):
                        dve.tensor_copy(va[:, b, :, 0:DK], bank[4 + b % 4][:, P * n:P * n + P].rearrange(
                            "p (h n) -> p h n", h=H)).then_inc(prep_dve, 1)
                dve.wait_ge(act_const, 1)

            def attention(layer):
                return [
                    (1, shifted, layer, 0), (3, resid, layer), (0, ln_stats, layer),
                    (1, shifted, layer, 1), (0, ln, layer), (2, norm, layer),
                    (1, shifted, layer, 2), (1, shifted, layer, 3)]

            bank_of_v = {0: R_BANK[0], 1: R_BANK[0]}
            stages = {
                A0: [(1, shifted, A0, 0), (2, norm0, 2), (3, resid, A0), (0, ln_stats, A0),
                     (1, shifted, A0, 1), (0, ln, A0), (2, norm0, 3), (1, shifted, A0, 2), (1, norm0, 0), (0, v_sb, 0), (2, ot_sb0, 0),
                     (1, shifted, A0, 3), (1, norm0, 1), (0, v_sb, 1), (2, ot_sb0, 1)],
                F0: [(2, resid_q, F0), (0, ln_stats, F0), (0, ln, F0), (0, quant0), (1, hid0)],
                A1: attention(A1),
                ROUTE: [(0, ln_stats, ROUTE), (1, lg_sb), (0, ln, ROUTE)],
                MOE: [(1, acc, 1), (0, acc, 0)],
                A2: [(0, ln_stats, A2), (1, shift2), (0, ln, A2), (2, norm2), (2, resid, A2)],
                F2: [(2, resid, F2), (0, ln_stats, F2), (0, ln, F2), (1, hid2_ln)],
                A3: attention(A3),
                F3: [(2, resid_q, F3), (0, ln_stats, F3), (0, ln, F3), (0, quant3), (1, hid3), (1, hq3)],
            }
            prepare()
            walk(dve, PLAN, stages, before={(MOE, 0): route, (MOE, 1): route_bias, (F2, 0): fold},
                 after={(A0, 3): weight_sums})


def pack(arrays, pack_):
    import numpy as np
    return np.ascontiguousarray(np.concatenate([arrays[n].reshape(P, w) for n, w in pack_.items()], axis=1))


def kernel(**inputs):
    import numpy as np
    import concourse.bacc as bacc
    from concourse.bass_utils import run_bass_kernel_spmd as run

    a = {k: np.asarray(v) for k, v in inputs.items()}
    f = np.float32
    part = np.arange(P)

    def heads_T(w):
        return w.transpose(2, 0, 1).reshape(P, H * DK0)

    def tiles(w):
        return w.reshape(-1, P, w.shape[1]).transpose(1, 0, 2).reshape(P, -1)

    def everywhere(v):
        return np.broadcast_to(v.reshape(1, -1), (P, v.size))

    cols = dict(
        ctxT=a["ctx_1024"].transpose(2, 0, 1), ctx=a["ctx_1024"].transpose(1, 0, 2), x=a["x"].transpose(1, 0, 2),
        wkT_1=a["L1_xattn_w_k"].T, wkT_3=a["L3_xattn_w_k"].T,
        wvT_13=np.concatenate([a["L1_xattn_w_v"].T, a["L3_xattn_w_v"].T], axis=1),
        ident=np.eye(P, dtype=f), ones=np.ones((P, P), f),
        hmask=(part[:, None] // DK == np.arange(H)[None]).astype(f),
        bk_3=a["L3_xattn_b_k"], bq_3=a["L3_xattn_b_q"],
        gates=everywhere(np.concatenate([a["g_xattn"], a["g_ffn"]])),
        wkT_0=heads_T(a["L0_xattn_Wk"]), wqT_0=heads_T(a["L0_xattn_Wq"]), wvT_0=heads_T(a["L0_xattn_Wv"]),
        woT_0=tiles(a["L0_xattn_Wo"].T),
        causal=np.where(part[None] > part[:, None], f(NEG), f(0)), kiota=everywhere(part.astype(f)),
        utri=(part[:, None] < part[None]).astype(f), eiota=everywhere(np.arange(NE, dtype=f)), piota=part.astype(f),
        act_sb=everywhere(np.concatenate([a["L3_ffn_act_scale"], a["L3_ffn_act_bias"]])),
        lnw_2=a["L2_ffn_ln_w"].reshape(FT, P).T, lnb_2=a["L2_ffn_ln_b"].reshape(FT, P).T, wg=a["L1_ffn_Wg"],
        wqT_1=a["L1_xattn_w_q"].T, woT_1=a["L1_xattn_w_o"].T, wqT_3=a["L3_xattn_w_q"].T, woT_3=a["L3_xattn_w_o"].T,
        woT_2=a["L2_xattn_W"].T,
        gateT=a["L0_ffn_w_gate"].T, upT=a["L0_ffn_w_up"].T, downT=tiles(a["L0_ffn_w_down"].T),
        fcT=a["L2_ffn_W_fc"].T, projT=tiles(a["L2_ffn_W_proj"].T), w1T=a["L3_ffn_w1"].T, w2T=tiles(a["L3_ffn_w2"].T),
        nw1=everywhere(a["L3_ffn_norm1_w"]), nw2=everywhere(a["L3_ffn_norm2_w"]),
    )
    arrays = {f"pack{n}_d": pack(cols, p) for n, p in enumerate(PACKS)}
    row = dict(bv_13=np.concatenate([np.zeros(P, f), a["L3_xattn_b_v"]]), bo_1=a["L1_xattn_b_o"], bo_2=a["L2_xattn_b"],
               bo_3=a["L3_xattn_b_o"])
    arrays["rows_d"] = np.concatenate([row[n] for n in ROWS]).reshape(1, -1)
    arrays["mask0_d"] = np.ascontiguousarray(a["mask_BxSxS2_bf0"].transpose(1, 0, 2))
    arrays["mask1_d"] = np.ascontiguousarray(a["mask_BxSxS2_ik0"].transpose(1, 0, 2))
    arrays["lens_d"] = np.ascontiguousarray(everywhere(a["_lenS2"]))
    b2 = np.zeros((B, NE, B, P), f)
    for b in range(B):
        b2[b, :, b, :] = a["L1_ffn_b2"]
    arrays["b2blk_d"] = b2.reshape(B * NE, N)
    arrays["experts_d"] = np.ascontiguousarray(np.concatenate([
        a["L1_ffn_W1"], a["L1_ffn_b1"].reshape(NE, FT, P).transpose(0, 2, 1),
        a["L1_ffn_W2"].reshape(NE, FT, P, P).transpose(0, 2, 1, 3).reshape(NE, P, F)], axis=2))

    nc = bacc.Bacc("TRN2", target_bir_lowering=False, num_devices=1)
    args = [nc.dram_tensor(k, v.shape, mybir.dt.from_np(v.dtype), kind="ExternalInput").ap() for k, v in arrays.items()]
    out = nc.dram_tensor("out_d", (P, N), F32, kind="ExternalOutput").ap()
    n = len(PACKS)
    build(nc, args[:n], *args[n:], out)
    r = run(nc, [arrays], core_ids=[0])
    return np.ascontiguousarray(r.results[0]["out_d"].reshape(P, B, P).transpose(1, 0, 2))
```

```python
from contextlib import ExitStack

import concourse.bass as bass
from concourse import mybir

F32 = mybir.dt.float32
BF16 = mybir.dt.bfloat16
I32 = mybir.dt.int32
U8 = mybir.dt.uint8
U32 = mybir.dt.uint32
ALU = mybir.AluOpType
ACT = mybir.ActivationFunctionType
AX = mybir.AxisListType

P = 128
B = 8
N = B * P
H = 16
DK0 = 64
DK = P // H
GH = 4
G = H // GH
VW = DK + 1
VW0 = DK0 + 1
F = 512
FT = F // P
NE = 8
TOPK = 2
CAP = -(-N * TOPK * 105 // (NE * 100))
NEG = -1e30
MAGIC = 1.5 * 2 ** 23
LN_EPS = 1e-5
STATS = 6

PACK_FIRST = dict(ctxT=N, wkT_1=P, wkT_3=P, wvT_13=2 * P, ident=P, ones=P, causal=P, hmask=H, bk_3=1, bq_3=1, gates=8, x=N)
PACK_ATT0 = dict(wkT_0=H * DK0, wqT_0=H * DK0, wvT_0=H * DK0, woT_0=H * DK0)
PACK_REST = dict(kiota=P, utri=P, eiota=NE, piota=1, act_sb=2, lnw_2=FT, wg=NE, lnb_2=FT,
                 wqT_1=P, woT_1=P, wqT_3=P, woT_3=P, woT_2=P)
PACK_FFN = dict(gateT=F, upT=F, downT=F, fcT=F, projT=F, w1T=F, w2T=F, nw1=P, nw2=F)
PACK_CTX = dict(ctx=N)
PACKS = [PACK_FIRST, PACK_ATT0, PACK_REST, PACK_FFN, PACK_CTX]
ROWS = dict(bv_13=2 * P, bo_1=P, bo_2=P, bo_3=P)
EXPERT = F + FT + F
TERNARY = ["gateT", "upT", "downT", "fcT", "projT", "w1T", "w2T"]


class Item:

    def __init__(self, b, rep):
        self.b, self.rep, self.k = b, rep, rep % 2

    def back(self, n):
        return Item(self.b - n, self.rep - n) if self.rep - n >= 0 else None


class Event:

    def __init__(self, sem, per, base):
        self.sem, self.per, self.base = sem, per, base

    def at(self, item, j=None):
        return self.per * item.b + (self.base + (self.per if j is None else j))


def schedule(lags, firsts):
    out = []
    for n, (lag, first) in enumerate(zip(lags, firsts)):
        over = lags[n - 1] if n else 0
        assert first >= over and first > lag and (B - first) % 2 == 0
        for j in range(first):
            steps = [(n - 1, B + j)] if n and j < over else []
            out.append(("peel", steps + [(n, j)]))
        if first < B:
            out.append(("loop", n, first, (B - first) // 2))
    for j in range(lags[-1]):
        out.append(("peel", [(len(lags) - 1, B + j)]))
    return out


def finish(*parts):
    parts = [p for p in parts if p is not None]
    while parts:
        for p in list(parts):
            if next(p, parts) is parts:
                parts.remove(p)


def walk(eng, plan, stages, before={}, after={}):

    def step(layer, s, off, loop=None):
        for entry in stages[layer]:
            parts = []
            for lag, fn, *args in entry if isinstance(entry, list) else [entry]:
                rep = s + off - lag
                if 0 <= rep < B:
                    parts.append(fn(Item(rep if loop is None else 2 * loop + rep, rep), *args))
            finish(*parts)

    for what in plan:
        if what[0] == "peel":
            for layer, s in what[1]:
                if (layer, s) in before:
                    before[layer, s]()
                step(layer, s, 0)
                if (layer, s) in after:
                    after[layer, s]()
        else:
            _, layer, first, pairs = what
            with eng.Fori(0, pairs) as i:
                for off in range(2):
                    step(layer, first, off, i)


RED_DONE = len(TERNARY) + 5
RT_CHOSEN = 3 + 2 * B + 6 + 1 + (B - 1)
RT_WEIGHTS = RT_CHOSEN + 7
RT_BIAS = RT_WEIGHTS + 2

A0, F0, A1, ROUTE, MOE, A2, F2, A3, F3 = range(9)
LAG = [3, 3, 3, 1, 1, 3, 3, 3, 3]
KIND = ["att", "ffn", "att", "route", "moe", "att", "ffn", "att", "ffn"]
FIRST = [4, B, 4, 4, 2, 4, 4, 4, 4]
PLAN = schedule(LAG, FIRST)


def build(nc, packs, rows_d, mask0_d, mask1_d, lens_d, b2blk_d, experts_d, out_d):
    with ExitStack() as ctx:
        def sb(name, shape, dt=F32):
            return ctx.enter_context(nc.sbuf_tensor(name, shape, dt))

        def sem(name):
            return ctx.enter_context(nc.semaphore(name))

        shared = {}

        def events(layer, **per):
            out = {}
            for name, n in per.items():
                key = f"{KIND[layer]}_{name}"
                s, base = shared.get(key) or (sem(key), 0)
                out[name] = Event(s, n, base)
                shared[key] = s, base + n * B
            return out

        col = {}
        packed = []
        for n, pack in enumerate(PACKS):
            tile = sb(f"pack{n}", [P, sum(pack.values())])
            packed.append(tile)
            at = 0
            for name, w in pack.items():
                col[name] = tile[:, at:at + w]
                at += w
        rows_sb = sb("rows_sb", [1, sum(ROWS.values())])
        row = {}
        at = 0
        for name, w in ROWS.items():
            row[name] = rows_sb[0:1, at:at + w]
            at += w
        x_sb = col["x"].rearrange("p (b d) -> p b d", b=B)
        ctxT = col["ctxT"].rearrange("p (b t) -> p b t", b=B)
        ctx_tok = col["ctx"].rearrange("p (b d) -> p b d", b=B)
        ident = col["ident"]
        ones = col["ones"]
        identb = sb("identb", [P, P], BF16)
        onesb = sb("onesb", [P, P], BF16)
        utrib = sb("utrib", [P, P], BF16)
        tanh_g = sb("tanh_g", [P, 8])
        mask0_u8 = sb("mask0_u8", [P, B, P], U8)
        mask1_i32 = sb("mask1_i32", [P, B, P], I32)
        lens_i = sb("lens_i", [P, B], I32)
        lens_f = sb("lens_f", [P, B])
        qneg = sb("qneg", [P, B])
        neg0 = sb("neg0", [P, B, P], BF16)
        neg1 = sb("neg1", [P, B, P], BF16)
        neg2 = sb("neg2", [P, B, P], BF16)
        b2blk = sb("b2blk", [NE * B, N])
        kT_1 = sb("kT_1", [P, B, P])
        kT_3 = sb("kT_3", [P, B, P])
        va_1 = sb("va_1", [P, B, H, VW])
        va_3 = sb("va_3", [P, B, H, VW])

        stats = sb("stats", [P, 2, STATS])
        mv = sb("mv", [P, 2, 2])
        stats_h = sb("stats_h", [P, 2, STATS])
        mv_h = sb("mv_h", [P, 2, 2])
        rstd = sb("rstd", [P, 2, 4])
        xn = sb("xn", [P, 2, P])
        xnT = sb("xnT", [P, 2, P])
        qT = sb("qT", [P, 2, H * DK0])
        ctk = sb("ctk", [P, 2, P])
        kz = sb("kz", [P, 2, 2 * H * DK0])
        va0 = sb("va0", [P, 2, H, VW0])
        prob = sb("prob", [P, 2, F])
        probT = sb("probT", [P, 2, F])
        mx = sb("mx", [P, 2, GH])
        rden = sb("rden", [P, 2, H])
        o_n = sb("o_n", [P, 2, H * DK0])
        oT = sb("oT", [P, 2, H * DK0])

        minus_half = sb("minus_half", [P, 1])[:, 0:1]
        minus_magic = sb("minus_magic", [P, 1])[:, 0:1]
        xm = sb("xm", [P, 2, P])
        xqT = sb("xqT", [P, 2, P], BF16)
        qs = sb("qs", [P, 2, 8])
        hs = sb("hs", [P, 2, 8])
        hid = sb("hid", [P, 2, F])
        hid2 = sb("hid2", [P, 2, F])
        sg = sb("sg", [P, 2, F])
        hqT = sb("hqT", [P, 2, F], BF16)
        tern = {n: sb(f"t_{n}", [P, F], F32 if n in ("fcT", "projT") else BF16) for n in TERNARY}
        tmp_t = sb("tmp_t", [P, 2, F])
        asum = sb("asum", [P, len(TERNARY)])
        wmean = sb("wmean", [P, len(TERNARY)])
        winv = sb("winv", [P, len(TERNARY)])
        projw = sb("projw", [P, F])
        crow = sb("crow", [1, P])

        xnT_all = sb("xnT_all", [P, B, P])
        lg = sb("lg", [P, B, NE])
        pr = sb("pr", [P, B, NE])
        psum_r = sb("psum_r", [P, B])
        top = sb("top", [P, B, NE])
        topi = sb("topi", [P, B, NE], U32)
        topf = sb("topf", [P, B, NE])
        gsum = sb("gsum", [P, B])
        g12 = sb("g12", [P, B, 2])
        oh1 = sb("oh1", [P, B, NE])
        oh2 = sb("oh2", [P, B, NE])
        chosen = sb("chosen", [P, B, NE], BF16)
        before_b = sb("before_b", [P, B, NE], BF16)
        keep = sb("keep", [P, B, NE])
        w_tok = sb("w_tok", [P, B, NE])
        w_tokT = sb("w_tokT", [B * NE, P])
        expert = sb("expert", [P, 2, EXPERT])
        hT = kz[:, :, :].rearrange("p k (t n) -> p k t n", t=FT)

        bank = [ctx.enter_context(nc.psum_tensor(f"bank{i}", [P, 512], F32)) for i in range(8)]
        S_BANK, T_BANK, O_BANK, R_BANK = (0, 1), (2, 3), (4, 5), (6, 7)

        loaded = [sem(f"loaded{n}") for n in range(len(PACKS) + 1)]
        rows_loaded, mask0_loaded, mask1_loaded = sem("rows_loaded"), sem("mask0_loaded"), sem("mask1_loaded")
        lens_loaded, b2_loaded = sem("lens_loaded"), sem("b2_loaded")
        ctk_loaded = [sem(f"ctk_loaded{k}") for k in range(2)]
        expert_loaded = [sem(f"expert_loaded{k}") for k in range(2)]
        stored = sem("stored")
        pool_const = sem("pool_const")
        tern_dve = sem("tern_dve")
        prep_pe = sem("prep_pe")
        prep_act = sem("prep_act")
        prep_dve = sem("prep_dve")
        act_const = sem("act_const")
        kz_zero = sem("kz_zero")
        pool_waited, dve_waited = sem("pool_waited"), sem("dve_waited")
        red_dve = sem("red_dve")
        red_pe = sem("red_pe")
        fold_dve = sem("fold_dve")
        fold_pe = sem("fold_pe")
        rt_dve = sem("rt_dve")
        rt_act = sem("rt_act")
        rt_pe = sem("rt_pe")

        att = dict(ln=3, rs=2, xt=1, xt_sb=1, scores=G, shifted=2 * G, probs=G, probsT=G, probsT_sb=G, pv=G, y=1, resid=1)
        ffn = dict(ln=3, rs=2, xt=1, xt_sb=1, ht=1, ht_sb=1, y=1, resid=1)
        E = {
            A0: events(A0, **att, kps=2, k_sb=4, qps=2, q_sb=2, vps=2, v_sb=2, norm=2 * G, ot=2, ot_sb=2),
            F0: events(F0, **ffn, gate=1, up=1, silu=1, quant=5, hid=6),
            A1: events(A1, **att, q=1, q_sb=1, kz=1, norm=2, ot=1, ot_sb=1),
            ROUTE: events(ROUTE, ln=3, rs=2, xt=1, xt_sb=1, copied=1, logits=1, lg=2),
            MOE: events(MOE, h=8, gelu=8, y=2, acc=8),
            A2: events(A2, ln=3, rs=2, xt=1, xt_sb=1, scores=1, shift=2, probs=1, probsT=1, probsT_sb=1, pv=1,
                       norm=2, ot=1, ot_sb=1, y=1, resid=1),
            F2: events(F2, **ffn, up=1, gelu=1, hid=3, rs_hid=2),
            A3: events(A3, **att, q=1, q_sb=1, kz=1, norm=2, ot=1, ot_sb=1),
            F3: events(F3, **ffn, quant=8, rq=2, up=1, relu=1, sq=1, biased=1, sumsq=1, hw=1, rh=2, hq=7),
        }
        emptied = {
            (A0, "xt"): ("xt_sb", 1), (A0, "k0"): ("k_sb", 2), (A0, "k1"): ("k_sb", 4), (A0, "q0"): ("q_sb", 1),
            (A0, "q1"): ("q_sb", 2), (A0, "v0"): ("v_sb", 1), (A0, "v1"): ("v_sb", 2), (A0, "ot0"): ("ot_sb", 1),
            (A0, "ot1"): ("ot_sb", 2), (A0, "y"): ("resid", 1),
            (A2, "xt"): ("xt_sb", 1), (A2, "s"): ("probs", 1), (A2, "t"): ("probsT_sb", 1), (A2, "pv"): ("norm", 2),
            (A2, "ot"): ("ot_sb", 1), (A2, "y"): ("resid", 1),
            (F0, "xt"): ("xt_sb", 1), (F0, "gate"): ("silu", 1), (F0, "up"): ("hid", 1), (F0, "ht"): ("ht_sb", 1),
            (F0, "y"): ("resid", 1),
            (F3, "xt"): ("xt_sb", 1), (F3, "up"): ("relu", 1), (F3, "ht"): ("ht_sb", 1), (F3, "y"): ("resid", 1),
            (F2, "xt"): ("xt_sb", 1), (F2, "up"): ("gelu", 1), (F2, "ht"): ("ht_sb", 1), (F2, "y"): ("resid", 1),
            (ROUTE, "xt"): ("xt_sb", 1), (ROUTE, "lg"): ("lg", 2),
        }
        for a in (A0, A1, A3):
            for g in range(G):
                emptied[a, f"s{g}"] = ("shifted", 2 * g + 2)
                emptied[a, f"t{g}"] = ("probsT_sb", g + 1)
                emptied[a, f"pv{g}"] = ("norm", 2 * g + 2 if a == A0 else 2)
        for a in (A1, A3):
            emptied[a, "xt"] = ("xt_sb", 1)
            emptied[a, "q"] = ("q_sb", 1)
            emptied[a, "ot"] = ("ot_sb", 1)
            emptied[a, "y"] = ("resid", 1)
        for tc in range(2):
            for ht in range(FT):
                emptied[MOE, f"h{tc}{ht}"] = ("gelu", 4 * tc + ht + 1)
            emptied[MOE, f"y{tc}"] = ("acc", 4 * tc + 4)

        def wait(eng, layer, name, item, j=None):
            if item is not None:
                ev = E[layer][name]
                eng.wait_ge(ev.sem, ev.at(item, j))

        block = ctx.enter_context(nc.Block())

        @block.sync
        def _(sp):
            cut = sum(PACK_FIRST.values()) - N
            sp.dma_start(packed[0][:, 0:cut], packs[0][:, 0:cut]).then_inc(loaded[0], 16)
            sp.dma_start(packed[0][:, cut:], packs[0][:, cut:]).then_inc(loaded[5], 16)
            sp.dma_start(rows_sb[:, :], rows_d).then_inc(rows_loaded, 16)
            sp.dma_start(mask0_u8[:, :, :], mask0_d).then_inc(mask0_loaded, 16)
            sp.dma_start(packed[1][:, :], packs[1]).then_inc(loaded[1], 16)
            sp.dma_start(packed[2][:, :], packs[2]).then_inc(loaded[2], 16)

            def load_ctk(it):
                wait(sp, A0, "vps", it.back(2))
                sp.dma_start(ctk[:, it.k, :], packs[0][:, 0:N].rearrange("p (b t) -> p b t", b=B)[:, bass.ds(it.b, 1), :]
                             ).then_inc(ctk_loaded[it.k], 16)

            def load_expert(it):
                wait(sp, MOE, "y", it.back(2))
                sp.dma_start(expert[:, it.k, :], experts_d[bass.ds(it.b, 1)].rearrange("a p n -> p (a n)")
                             ).then_inc(expert_loaded[it.k], 16)

            def rest():
                sp.dma_start(packed[3][:, :], packs[3]).then_inc(loaded[3], 16)
                sp.dma_start(mask1_i32[:, :, :], mask1_d).then_inc(mask1_loaded, 16)
                sp.dma_start(lens_i[:, :], lens_d).then_inc(lens_loaded, 16)
                sp.dma_start(b2blk[:, :], b2blk_d).then_inc(b2_loaded, 16)
                sp.dma_start(packed[4][:, :], packs[4]).then_inc(loaded[4], 16)

            stages = {n: [] for n in range(len(LAG))}
            stages[A0] = [(0, load_ctk)]
            stages[MOE] = [(0, load_expert)]
            walk(sp, PLAN, stages, after={(A0, 0): rest})
            wait(sp, F3, "resid", Item(B - 1, B - 1))
            sp.dma_start(out_d, col["x"]).then_inc(stored, 16)
            sp.wait_ge(stored, 16)

        @block.gpsimd
        def _(pool):
            pool.memset(minus_half, -0.5).then_inc(pool_const, 1)
            for k in range(2):
                pool.memset(kz[:, k, :], 0.0).then_inc(kz_zero, 1)
                pool.memset(va0[:, k, :, DK0:VW0], 1.0).then_inc(kz_zero, 1)
            for va in (va_1, va_3):
                pool.memset(va[:, :, :, DK:VW], 1.0).then_inc(kz_zero, 1)
            pool.wait_ge(loaded[0], 16)
            pool.tensor_copy(identb[:, :], ident).then_inc(pool_const, 1)
            pool.tensor_copy(onesb[:, :], ones).then_inc(pool_const, 1)
            def masks():
                pool.wait_ge(loaded[2], 16)
                pool.tensor_copy(utrib[:, :], col["utri"]).then_inc(pool_const, 1)
                pool.wait_ge(mask1_loaded, 16)
                pool.tensor_scalar(neg1[:, :, :], mask1_i32[:, :, :], 0.0, NEG, ALU.is_equal, ALU.mult).then_inc(pool_const, 1)
                pool.wait_ge(lens_loaded, 16)
                pool.tensor_copy(lens_f[:, :], lens_i[:, :]).then_inc(pool_const, 1)
                pool.wait_ge(pool_const, 6)
                pool.tensor_scalar(qneg[:, :], lens_f[:, :], col["piota"], NEG, ALU.is_le, ALU.mult).then_inc(pool_const, 1)
                pool.wait_ge(pool_const, 7)
                for b in range(B):
                    pool.tensor_scalar(neg2[:, b, :], col["kiota"], lens_f[:, b:b + 1], qneg[:, b:b + 1], ALU.is_ge,
                                       ALU.mult).then_inc(pool_const, 1)

            def inverse_root(it, layer, name, out, src, scale, eps):
                ev = E[layer][name]
                pool.tensor_scalar(out, src, scale, eps, ALU.mult, ALU.add).then_inc(ev.sem, 1)
                pool.wait_ge(ev.sem, ev.at(it, 1))
                pool.tensor_tensor(out, out, minus_half, ALU.pow).then_inc(ev.sem, 1)

            def rs(it, layer):
                wait(pool, layer, "ln", it, 2)
                if not isinstance(it.b, int):
                    pool.sem_inc(pool_waited)
                inverse_root(it, layer, "rs", rstd[:, it.k, 0:1], mv[:, it.k, 1:2], 1.0, LN_EPS)

            def rs_hid(it):
                wait(pool, F2, "hid", it, 2)
                if not isinstance(it.b, int):
                    pool.sem_inc(pool_waited)
                inverse_root(it, F2, "rs_hid", rstd[:, it.k, 1:2], mv_h[:, it.k, 1:2], 1.0, LN_EPS)

            def rms(it, src, j, v, n, name):
                wait(pool, F3, src, it, j)
                if not isinstance(it.b, int):
                    pool.sem_inc(pool_waited)
                inverse_root(it, F3, name, v[:, it.k, 4:5], v[:, it.k, 0:1], 1.0 / n, 1e-8)

            def weigh(it):
                wait(pool, F3, "biased", it)
                wait(pool, F3, "ht", it.back(2))
                pool.tensor_tensor(hid2[:, it.k, :], hid[:, it.k, :], col["nw2"], ALU.mult).then_inc(E[F3]["hw"].sem, 1)

            def mask_keys(it, layer, kT):
                wait(pool, layer, "scores", it.back(2))
                pool.tensor_tensor(kz[:, it.k, :].rearrange("p (h t) -> p h t", h=H),
                                   kT[:, bass.ds(it.b, 1), :].to_broadcast([P, H, P]),
                                   col["hmask"].rearrange("p (h a) -> p h a", a=1).to_broadcast([P, H, P]),
                                   ALU.mult).then_inc(E[layer]["kz"].sem, 1)

            def copy_xnT(it):
                wait(pool, ROUTE, "xt_sb", it)
                pool.tensor_copy(xnT_all[:, bass.ds(it.b, 1), :], xnT[:, it.k:it.k + 1, :]).then_inc(E[ROUTE]["copied"].sem, 1)

            def keys_ready():
                pool.wait_ge(prep_act, 4)
                wait(pool, A0, "scores", Item(B - 1, B - 1))

            stages = {n: [] for n in range(len(LAG))}
            for layer in (A0, F0, A1, ROUTE, A2, F2, A3, F3):
                stages[layer] = [(0, rs, layer)]
            stages[A1] += [(0, mask_keys, A1, kT_1)]
            stages[A3] += [(0, mask_keys, A3, kT_3)]
            stages[ROUTE] += [(1, copy_xnT)]
            stages[F2] += [(2, rs_hid)]
            stages[F3] += [(0, rms, "quant", 1, qs, P, "rq"), (1, weigh), (1, rms, "sumsq", 1, hs, F, "rh")]
            walk(pool, PLAN, stages, before={(A1, 0): keys_ready}, after={(A0, 1): masks})

        @block.scalar
        def _(act):
            def evac(dst, src, layer, name, **kw):
                act.activation(dst, src, ACT.Identity if kw else ACT.Copy, **kw).then_inc(E[layer][name].sem, 1)

            def xt_sb(it, layer):
                wait(act, layer, "xt", it)
                if layer == ROUTE:
                    wait(act, ROUTE, "copied", it.back(2))
                evac(xnT[:, it.k, :], bank[R_BANK[0]][:, 0:P], layer, "xt_sb")

            def exps(it, layer, g):
                wait(act, layer, "shifted", it, 2 * g + 2)
                act.activation(prob[:, g % 2, :], prob[:, g % 2, :], ACT.Exp,
                               scale=float(DK0 if layer == A0 else DK) ** -0.5).then_inc(E[layer]["probs"].sem, 1)

            def probsT_sb(it, layer, g):
                wait(act, layer, "probsT", it, g + 1)
                evac(probT[:, g % 2, :], bank[T_BANK[g % 2]][:, :], layer, "probsT_sb")

            def k_sb(it, c):
                wait(act, A0, "kps", it, c + 1)
                kv = kz[:, it.k, :].rearrange("p (t a n) -> p t a n", t=8, a=2)
                src = bank[R_BANK[0]][:, :].rearrange("p (t n) -> p t n", t=4)
                for a in range(2):
                    evac(kv[64 * a:64 * a + 64, 4 * c:4 * c + 4, a, :], src[64 * a:64 * a + 64], A0, "k_sb")

            def q_sb0(it, c):
                wait(act, A0, "qps", it, c + 1)
                evac(qT[:, it.k, 512 * c:512 * c + 512], bank[R_BANK[1]][:, :], A0, "q_sb")

            def q_sb(it, layer):
                wait(act, layer, "q", it)
                if layer == A3:
                    evac(qT[:, it.k, 0:P], bank[R_BANK[1]][:, 0:P], layer, "q_sb", bias=col["bq_3"])
                else:
                    evac(qT[:, it.k, 0:P], bank[R_BANK[1]][:, 0:P], layer, "q_sb")

            def ot_sb(it, layer):
                wait(act, layer, "ot", it)
                evac(oT[:, it.k, 0:P], bank[R_BANK[0]][:, 0:P], layer, "ot_sb")

            def exps2(it):
                wait(act, A2, "scores", it)
                wait(act, A2, "shift", it)
                act.activation(prob[:, it.k, 0:P], bank[S_BANK[it.k]][:, 0:P], ACT.Exp, bias=mx[:, it.k, 1:2],
                               scale=float(P) ** -0.5, accum_out=rden[:, it.k, 1:2]).then_inc(E[A2]["probs"].sem, 1)

            def probsT_sb2(it):
                wait(act, A2, "probsT", it)
                evac(probT[:, it.k, 0:P], bank[T_BANK[it.k]][:, 0:P], A2, "probsT_sb")

            def xq_sb(it, layer):
                wait(act, layer, "xt", it)
                evac(xqT[:, it.k, :], bank[R_BANK[0]][:, 0:P], layer, "xt_sb", bias=minus_magic)

            def hq_sb(it, layer):
                wait(act, layer, "ht", it)
                evac(hqT[:, it.k, :], bank[T_BANK[it.k]][:, :], layer, "ht_sb", bias=minus_magic)

            def silu(it):
                wait(act, F0, "gate", it)
                wait(act, F0, "quant", it)
                wait(act, F0, "hid", it.back(2), 1)
                act.activation(sg[:, it.k, :], bank[S_BANK[it.k]][:, :], ACT.Silu, scale=qs[:, it.k, 3:4]
                               ).then_inc(E[F0]["silu"].sem, 1)

            def hid3(it):
                k = it.k
                wait(act, F3, "up", it)
                wait(act, F3, "quant", it)
                act.activation(sg[:, k, :], bank[S_BANK[k]][:, :], ACT.Relu, scale=qs[:, k, 3:4]
                               ).then_inc(E[F3]["relu"].sem, 1)
                wait(act, F3, "relu", it)
                act.activation(sg[:, k, :], sg[:, k, :], ACT.Square).then_inc(E[F3]["sq"].sem, 1)
                wait(act, F3, "hw", it.back(2))
                wait(act, F3, "sq", it)
                act.activation(hid[:, k, :], sg[:, k, :], ACT.Identity, bias=col["act_sb"][:, 1:2],
                               scale=col["act_sb"][:, 0:1]).then_inc(E[F3]["biased"].sem, 1)
                wait(act, F3, "rh", it.back(2))
                wait(act, F3, "biased", it)
                act.activation(sg[:, k, :], hid[:, k, :], ACT.Square, accum_out=hs[:, k, 0:1]
                               ).then_inc(E[F3]["sumsq"].sem, 1)

            def gelu2(it):
                wait(act, F2, "up", it)
                act.activation(hid[:, it.k, :], bank[S_BANK[it.k]][:, :], ACT.Gelu).then_inc(E[F2]["gelu"].sem, 1)

            def hT_sb2(it):
                wait(act, F2, "ht", it)
                evac(hid2[:, it.k, :], bank[T_BANK[it.k]][:, :], F2, "ht_sb")

            def gelu_e(it, tc):
                for ht in range(FT):
                    wait(act, MOE, "h", it, 4 * tc + ht + 1)
                    act.activation(hT[:, tc, ht, :], bank[ht][:, :], ACT.Gelu_apprx_tanh,
                                   bias=expert[:, it.k, F + ht:F + ht + 1]).then_inc(E[MOE]["gelu"].sem, 1)

            def prepare():
                act.wait_ge(loaded[0], 16)
                act.activation(tanh_g[:, :], col["gates"], ACT.Tanh).then_inc(act_const, 1)
                for n, (dst, kw) in enumerate([(kT_1, {}), (kT_3, dict(bias=col["bk_3"]))]):
                    for c in range(2):
                        act.wait_ge(prep_pe, 2 * n + c + 1)
                        act.activation(dst[:, 4 * c:4 * c + 4, :].rearrange("p b t -> p (b t)"), bank[2 * n + c][:, :],
                                       ACT.Identity if kw else ACT.Copy, **kw).then_inc(prep_act, 1)

            def route_exp():
                act.wait_ge(E[ROUTE]["lg"].sem, E[ROUTE]["lg"].at(Item(B - 1, B - 1)))
                act.activation(pr[:, :, :], lg[:, :, :], ACT.Exp).then_inc(rt_act, 1)

            def route_wT():
                act.wait_ge(rt_pe, 2)
                act.activation(w_tokT[:, :], bank[R_BANK[1]][0:B * NE, 0:P], ACT.Copy).then_inc(rt_act, 1)

            def attention(layer):
                return [
                    (2, exps, layer, 3), (2, probsT_sb, layer, 2),
                    (3, ot_sb, layer), (1, exps, layer, 0), (2, probsT_sb, layer, 3),
                    (1, exps, layer, 1), (1, probsT_sb, layer, 0), (0, xt_sb, layer),
                    (1, exps, layer, 2), (1, probsT_sb, layer, 1), (0, q_sb, layer)]

            stages = {
                A0: [(2, exps, A0, 3), (2, probsT_sb, A0, 2), (0, k_sb, 0),
                     (1, exps, A0, 0), (2, probsT_sb, A0, 3), (0, k_sb, 1),
                     (0, xt_sb, A0), (1, exps, A0, 1), (1, probsT_sb, A0, 0), (0, q_sb0, 0),
                     (1, exps, A0, 2), (1, probsT_sb, A0, 1), (0, q_sb0, 1)],
                F0: [(1, xq_sb, F0), (3, hq_sb, F0), (1, silu)],
                A1: attention(A1),
                ROUTE: [(0, xt_sb, ROUTE)],
                MOE: [(0, gelu_e, 0), (0, gelu_e, 1)],
                A2: [(1, xt_sb, A2), (2, exps2), (3, ot_sb, A2), (2, probsT_sb2)],
                F2: [(1, xt_sb, F2), (3, hT_sb2), (1, gelu2)],
                A3: attention(A3),
                F3: [(1, xq_sb, F3), (3, hq_sb, F3), (1, hid3)],
            }
            act.wait_ge(prep_dve, 1)
            act.wait_ge(kz_zero, 6)
            prepare()
            walk(act, PLAN, stages, before={(MOE, 0): route_exp, (MOE, 1): route_wT})

        @block.tensor
        def _(pe):
            def before_in_bank(layer, piece, b):
                mine = bank_of(layer, piece, b)
                here = order.index((layer, piece, b))
                return next((p for p in reversed(order[:here]) if bank_of(*p) == mine), None)

            def claim(it, layer, piece):
                found = before_in_bank(layer, piece, it.rep)
                if found is None:
                    return
                pl, pp, pb = found
                name, j = emptied[pl, pp]
                if pl != layer:
                    wait(pe, pl, name, Item(pb, pb), j)
                    if isinstance(it.b, int):
                        return
                    pl, pp, pb = before_in_bank(layer, piece, it.rep + 2)
                    pb -= 2
                    name, j = emptied[pl, pp]
                    assert pl == layer and E[layer][name].at(Item(pb, pb), j) > 0
                wait(pe, layer, name, Item(it.b + (pb - it.rep), pb), j)

            def bank_of(layer, piece, b):
                k = b % 2
                if layer == MOE:
                    return int(piece[2]) if piece[0] == "h" else O_BANK[int(piece[1])]
                if layer in (A0, A1, A3):
                    if piece[0] == "s":
                        return S_BANK[int(piece[1]) % 2]
                    if piece[0] == "t":
                        return T_BANK[int(piece[1]) % 2]
                    if piece.startswith("pv"):
                        return O_BANK[int(piece[2]) % 2 if layer == A0 else k]
                    return R_BANK[{"xt": 0, "k0": 0, "k1": 0, "q0": 1, "q1": 1, "v0": 0, "v1": 0, "ot0": 1, "ot1": 1,
                                   "y": 1, "q": 1, "ot": 0}[piece]]
                if layer == A2:
                    return {"xt": 6, "ot": 6, "y": 7, "s": S_BANK[k], "t": T_BANK[k], "pv": O_BANK[k]}[piece]
                if layer == F0:
                    return {"xt": 6, "gate": S_BANK[k], "up": O_BANK[k], "ht": T_BANK[k], "y": 7}[piece]
                if layer == ROUTE:
                    return {"xt": 6, "lg": S_BANK[0]}[piece]
                return {"xt": 6, "up": S_BANK[k], "ht": T_BANK[k], "y": O_BANK[k]}[piece]

            def xt(it, layer):
                wait(pe, layer, "ln" if layer not in (F0, F3) else "quant", it)
                claim(it, layer, "xt")
                src = xm if layer in (F0, F3) else xn
                pe.transpose(bank[R_BANK[0]][:, 0:P], src[:, it.k, :], ident).then_inc(E[layer]["xt"].sem, 1)

            def scores(it, layer, g):
                claim(it, layer, f"s{g}")
                out = bank[S_BANK[g % 2]]
                neg = {A0: neg0, A1: neg1, A3: None}[layer]
                if neg is not None:
                    if g == 0 and isinstance(it.b, int) and it.b == 0:
                        if layer == A0:
                            pe.wait_ge(prep_dve, 2)
                        pe.wait_ge(pool_const, 2 if layer == A0 else 5)
                    pe.matmul(out[:, :].rearrange("p (h t) -> p h t", h=GH), identb[:, :],
                              neg[:, bass.ds(it.b, 1), :].to_broadcast([P, GH, P]), start=True, stop=False)
                if layer == A0:
                    wait(pe, A0, "q_sb", it, 1 + g // 2)
                    wait(pe, A0, "k_sb", it, 2 + 2 * (g // 2))
                    for c in range(2):
                        t = 2 * g + c
                        mm_ = pe.matmul(out[:, 256 * c:256 * c + 256], qT[:, it.k, P * t:P * t + P],
                                        kz[:, it.k, 256 * t:256 * t + 256], start=False, stop=(c == 1))
                else:
                    wait(pe, layer, "q_sb", it)
                    wait(pe, layer, "kz", it)
                    mm_ = pe.matmul(out[:, :], qT[:, it.k, 0:P], kz[:, it.k, 512 * g:512 * g + 512],
                                    start=neg is None, stop=True)
                mm_.then_inc(E[layer]["scores"].sem, 1)

            def probsT(it, layer, g):
                wait(pe, layer, "probs", it, g + 1)
                claim(it, layer, f"t{g}")
                for j in range(GH):
                    mm_ = pe.transpose(bank[T_BANK[g % 2]][:, P * j:P * j + P], prob[:, g % 2, P * j:P * j + P], ident)
                mm_.then_inc(E[layer]["probsT"].sem, 1)

            def pv(it, layer, g):
                wait(pe, layer, "probsT_sb", it, g + 1)
                if layer == A0:
                    wait(pe, A0, "v_sb", it, 1 + g // 2)
                    claim(it, layer, f"pv{g}")
                elif g == 0:
                    claim(it, layer, "pv0")
                for j in range(GH):
                    h = GH * g + j
                    if layer == A0:
                        mm_ = pe.matmul(bank[O_BANK[g % 2]][:, VW0 * j:VW0 * j + VW0], probT[:, g % 2, P * j:P * j + P],
                                        va0[:, it.k, h, :], start=True, stop=True)
                    else:
                        va = va_1 if layer == A1 else va_3
                        mm_ = pe.matmul(bank[O_BANK[it.k]][:, VW * h:VW * h + VW], probT[:, g % 2, P * j:P * j + P],
                                        va[:, bass.ds(it.b, 1), h, :], start=True, stop=True)
                mm_.then_inc(E[layer]["pv"].sem, 1)

            def proj0(it, which, c):
                piece = f"{which}{c}"
                if which == "q" and c == 0:
                    wait(pe, A0, "xt_sb", it)
                if which == "v" and c == 0:
                    pe.wait_ge(ctk_loaded[it.k], 8 * it.b + 16 - 8 * it.k)
                claim(it, A0, piece)
                out = bank[bank_of(A0, piece, it.rep)]
                if which == "v":
                    mm_ = pe.matmul(out[:, :], ctk[:, it.k, :], col["wvT_0"][:, 512 * c:512 * c + 512], start=True, stop=True)
                else:
                    w = col["wkT_0" if which == "k" else "wqT_0"]
                    for t in range(4):
                        rhs = ctxT[:, bass.ds(it.b, 1), :] if which == "k" else xnT[:, it.k:it.k + 1, :]
                        mm_ = pe.matmul(out[:, P * t:P * t + P].rearrange("p (a n) -> p a n", a=1),
                                        w[:, 512 * c + P * t:512 * c + P * t + P], rhs, start=True, stop=True)
                mm_.then_inc(E[A0][which + "ps"].sem, 1)

            def ot0(it, c):
                wait(pe, A0, "norm", it, 4 * c + 4)
                piece = f"ot{c}"
                claim(it, A0, piece)
                out = bank[bank_of(A0, piece, it.rep)]
                for t in range(4):
                    mm_ = pe.transpose(out[:, P * t:P * t + P], o_n[:, it.k, 512 * c + P * t:512 * c + P * t + P], ident)
                mm_.then_inc(E[A0]["ot"].sem, 1)

            def y0(it):
                wait(pe, A0, "ot_sb", it)
                claim(it, A0, "y")
                out = bank[R_BANK[1]][:, 0:P]
                for t in range(8):
                    mm_ = pe.matmul(out, oT[:, it.k, P * t:P * t + P], col["woT_0"][:, P * t:P * t + P],
                                    start=(t == 0), stop=(t == 7))
                mm_.then_inc(E[A0]["y"].sem, 1)

            def q(it, layer):
                wait(pe, layer, "xt_sb", it)
                claim(it, layer, "q")
                pe.matmul(bank[R_BANK[1]][:, 0:P], col["wqT_1" if layer == A1 else "wqT_3"], xnT[:, it.k, :],
                          start=True, stop=True).then_inc(E[layer]["q"].sem, 1)

            def ot(it, layer):
                wait(pe, layer, "norm", it)
                claim(it, layer, "ot")
                pe.transpose(bank[R_BANK[0]][:, 0:P], o_n[:, it.k, 0:P], ident).then_inc(E[layer]["ot"].sem, 1)

            def y(it, layer):
                n = {A1: 1, A2: 2, A3: 3}[layer]
                claim(it, layer, "y")
                out = bank[R_BANK[1]][:, 0:P]
                pe.matmul(out, ones[0:1, :], row[f"bo_{n}"], start=True, stop=False)
                wait(pe, layer, "ot_sb", it)
                pe.matmul(out, oT[:, it.k, 0:P], col[f"woT_{n}"], start=False, stop=True).then_inc(E[layer]["y"].sem, 1)

            def scores2(it):
                wait(pe, A2, "xt_sb", it)
                claim(it, A2, "s")
                if it.rep == 0:
                    pe.wait_ge(pool_const, 7 + B)
                out = bank[S_BANK[it.k]][:, 0:P].rearrange("p (a n) -> p a n", a=1)
                pe.matmul(out, identb[:, :], neg2[:, bass.ds(it.b, 1), :], start=True, stop=False)
                pe.matmul(out, xnT[:, it.k, :], ctxT[:, bass.ds(it.b, 1), :], start=False, stop=True
                          ).then_inc(E[A2]["scores"].sem, 1)

            def probsT2(it):
                wait(pe, A2, "probs", it)
                claim(it, A2, "t")
                pe.transpose(bank[T_BANK[it.k]][:, 0:P], prob[:, it.k, 0:P], ident).then_inc(E[A2]["probsT"].sem, 1)

            def pv2(it):
                wait(pe, A2, "probsT_sb", it)
                claim(it, A2, "pv")
                pe.matmul(bank[O_BANK[it.k]][:, 0:P].rearrange("p (a n) -> p a n", a=1), probT[:, it.k, 0:P],
                          ctx_tok[:, bass.ds(it.b, 1), :], start=True, stop=True).then_inc(E[A2]["pv"].sem, 1)

            def up(it, layer, piece, w, lhs):
                wait(pe, layer, "xt_sb", it)
                claim(it, layer, piece)
                pe.matmul(bank[bank_of(layer, piece, it.rep)][:, :], lhs[:, it.k, :], w, start=True, stop=True
                          ).then_inc(E[layer][piece].sem, 1)

            def ht(it, layer):
                src = hid2 if layer != F2 else hid
                if layer == F3:
                    wait(pe, layer, "hq", it)
                else:
                    wait(pe, layer, "hid", it)
                claim(it, layer, "ht")
                for t in range(FT):
                    mm_ = pe.transpose(bank[T_BANK[it.k]][:, P * t:P * t + P], src[:, it.k, P * t:P * t + P], ident)
                mm_.then_inc(E[layer]["ht"].sem, 1)

            def y_ffn(it, layer, w):
                wait(pe, layer, "ht_sb", it)
                claim(it, layer, "y")
                out = bank[bank_of(layer, "y", it.rep)][:, 0:P]
                if layer == F2:
                    pe.matmul(out, ones[0:1, :], crow[:, :], start=True, stop=False)
                src = hid2 if layer == F2 else hqT
                for t in range(FT):
                    mm_ = pe.matmul(out, src[:, it.k, P * t:P * t + P], w[:, P * t:P * t + P],
                                    start=(t == 0 and layer != F2), stop=(t == FT - 1))
                mm_.then_inc(E[layer]["y"].sem, 1)

            def logits(it):
                wait(pe, ROUTE, "xt_sb", it)
                claim(it, ROUTE, "lg")
                pe.matmul(bank[S_BANK[0]][:, 0:NE], xnT[:, it.k, :], col["wg"], start=True, stop=True
                          ).then_inc(E[ROUTE]["logits"].sem, 1)

            def hidden(it, piece):
                tc, t = int(piece[1]), int(piece[2])
                claim(it, MOE, piece)
                if piece == "h00":
                    pe.wait_ge(expert_loaded[it.k], 8 * it.b + 16 - 8 * it.k)
                pe.matmul(bank[t][:, :], expert[:, it.k, P * t:P * t + P],
                          xnT_all[:, 4 * tc:4 * tc + 4, :].rearrange("p b t -> p (b t)"), start=True, stop=True
                          ).then_inc(E[MOE]["h"].sem, 1)

            def down(it, piece):
                tc = int(piece[1])
                claim(it, MOE, piece)
                wait(pe, MOE, "gelu", it, 4 * tc + 4)
                for tt in range(4):
                    for t in range(FT):
                        mm_ = pe.matmul(bank[O_BANK[tc]][:, P * tt:P * tt + P], hT[:, tc, t, P * tt:P * tt + P],
                                        expert[:, it.k, F + FT + P * t:F + FT + P * t + P],
                                        start=(t == 0), stop=(t == FT - 1))
                mm_.then_inc(E[MOE]["y"].sem, 1)

            def prepare():
                pe.wait_ge(loaded[0], 16)
                for n, w in enumerate(("wkT_1", "wkT_3")):
                    for c in range(2):
                        pe.matmul(bank[2 * n + c][:, :], col[w], ctxT[:, 4 * c:4 * c + 4, :].rearrange("p b t -> p (b t)"),
                                  start=True, stop=True).then_inc(prep_pe, 1)
                pe.wait_ge(rows_loaded, 16)
                for b in range(B):
                    if b >= 4:
                        pe.wait_ge(prep_dve, 2 + 2 * (b - 3))
                    out = bank[4 + b % 4][:, 0:2 * P]
                    pe.matmul(out, ones[0:1, :], row["bv_13"], start=True, stop=False)
                    pe.matmul(out, ctxT[:, b, :], col["wvT_13"], start=False, stop=True).then_inc(prep_pe, 1)
                pe.wait_ge(prep_act, 4)
                pe.wait_ge(prep_dve, 2 + 2 * B)
                pe.wait_ge(kz_zero, 6)
                pe.wait_ge(loaded[1], 16)

            def weight_sums():
                pe.wait_ge(red_dve, len(TERNARY))
                wait(pe, A0, "v_sb", Item(3, 3))
                pe.matmul(bank[R_BANK[0]][:, 0:len(TERNARY)], ones, asum[:, :], start=True, stop=True).then_inc(red_pe, 1)
                pe.wait_ge(red_dve, len(TERNARY) + 1)

            def route_places(it):
                if it.rep:
                    return
                pe.wait_ge(rt_dve, RT_CHOSEN)
                out = bank[R_BANK[0]][:, 0:B * NE]
                pe.matmul(out, utrib[:, :], chosen[:, :, :].rearrange("p b e -> p (b e)"), start=True, stop=False)
                pe.matmul(out, onesb[:, :], before_b[:, :, :].rearrange("p b e -> p (b e)"), start=False, stop=True
                          ).then_inc(rt_pe, 1)

            def route_bias():
                pe.wait_ge(rt_dve, RT_WEIGHTS)
                pe.transpose(bank[R_BANK[1]][0:B * NE, 0:P], w_tok[:, :, :].rearrange("p b e -> p (b e)"), ident
                             ).then_inc(rt_pe, 1)
                pe.wait_ge(rt_act, 2)
                pe.wait_ge(b2_loaded, 16)
                for c in range(2):
                    pe.matmul(bank[R_BANK[c]][:, :], w_tokT[:, :], b2blk[:, 512 * c:512 * c + 512], start=True, stop=True
                              ).then_inc(rt_pe, 1)

            def moe_ready():
                wait(pe, ROUTE, "copied", Item(B - 1, B - 1))

            def fold():
                pe.wait_ge(tern_dve, 3 * len(TERNARY))
                wait(pe, A2, "resid", Item(B - 3, B - 3))
                for t in range(FT):
                    mm_ = pe.matmul(bank[R_BANK[1]][0:1, 0:P], col["lnb_2"][:, t:t + 1], tern["projT"][:, P * t:P * t + P],
                                    start=(t == 0), stop=(t == FT - 1))
                mm_.then_inc(fold_pe, 1)
                pe.wait_ge(fold_dve, FT + 1)

            def attention(layer):
                return [
                    (1, scores, layer, 0), (2, probsT, layer, 2), (2, pv, layer, 1), (3, ot, layer),
                    (1, scores, layer, 1), (2, probsT, layer, 3), (2, pv, layer, 2), (3, y, layer),
                    (1, scores, layer, 2), (1, probsT, layer, 0), (2, pv, layer, 3), (0, xt, layer),
                    (1, scores, layer, 3), (1, probsT, layer, 1), (0, q, layer), (1, pv, layer, 0)]

            stages = {
                A0: [(1, scores, A0, 0), (0, proj0, "k", 0), (2, probsT, A0, 2), (3, ot0, 1), (2, pv, A0, 1),
                     (1, scores, A0, 1), (0, proj0, "k", 1), (2, probsT, A0, 3), (3, y0), (2, pv, A0, 2), (0, xt, A0),
                     (2, ot0, 0),
                     (1, scores, A0, 2), (0, proj0, "v", 0), (1, probsT, A0, 0), (0, proj0, "q", 0), (2, pv, A0, 3),
                     (1, scores, A0, 3), (0, proj0, "v", 1), (1, probsT, A0, 1), (0, proj0, "q", 1), (1, pv, A0, 0)],
                F0: [(1, xt, F0), (3, ht, F0), (1, up, F0, "gate", tern["gateT"][:, :], xqT),
                     (1, up, F0, "up", tern["upT"][:, :], xqT), (3, y_ffn, F0, tern["downT"])],
                A1: attention(A1),
                ROUTE: [(1, logits), (0, xt, ROUTE)],
                MOE: [(0, hidden, "h00"), (0, hidden, "h01"), (0, hidden, "h02"), (0, hidden, "h03"), (1, down, "y1"),
                      (0, hidden, "h10"), (0, hidden, "h11"), (0, hidden, "h12"), (0, hidden, "h13"), (0, route_places),
                      (0, down, "y0")],
                A2: [(1, xt, A2), (3, ot, A2), (2, probsT2), (1, scores2), (3, y, A2), (2, pv2)],
                F2: [(1, xt, F2), (3, ht, F2), (1, up, F2, "up", tern["fcT"][:, :], xnT), (3, y_ffn, F2, projw)],
                A3: attention(A3),
                F3: [(1, xt, F3), (3, ht, F3), (1, up, F3, "up", tern["w1T"][:, :], xqT), (3, y_ffn, F3, tern["w2T"])],
            }

            def piece_name(layer, fn, args):
                if fn is xt:
                    return "xt"
                if fn in (scores, probsT, pv):
                    return {scores: "s", probsT: "t", pv: "pv"}[fn] + str(args[1])
                if fn is proj0:
                    return args[0] + str(args[1])
                if fn is ot0:
                    return f"ot{args[0]}"
                if fn is up:
                    return args[1]
                if fn in (hidden, down):
                    return args[0]
                return {y0: "y", q: "q", ot: "ot", y: "y", scores2: "s", probsT2: "t", pv2: "pv", ht: "ht",
                        y_ffn: "y", logits: "lg"}[fn]

            order = []
            for what in PLAN:
                steps = what[1] if what[0] == "peel" else [(what[1], s) for s in range(what[2], what[2] + 2 * what[3])]
                for layer, s in steps:
                    for lag, fn, *args in stages[layer]:
                        if 0 <= s - lag < B and fn is not route_places:
                            order.append((layer, piece_name(layer, fn, args), s - lag))

            def ternary_ready(n):
                return lambda: pe.wait_ge(tern_dve, 3 * n)

            prepare()
            walk(pe, PLAN, stages,
                 before={(F0, 0): ternary_ready(3), (F2, 0): fold, (MOE, 0): moe_ready, (MOE, 1): route_bias,
                         (A2, 0): lambda: pe.wait_ge(rt_dve, RT_BIAS)},
                 after={(A0, 3): weight_sums})

        @block.vector
        def _(dve):
            def chain(layer, name, it, start=0):
                ev = E[layer][name]
                count = [start]

                def do(ins, hold=True, alone=False):
                    ins.then_inc(ev.sem, 1)
                    count[0] += 1
                    yield
                    if hold:
                        dve.wait_ge(ev.sem, ev.at(it, count[0]))
                    if alone and not isinstance(it.b, int):
                        dve.sem_inc(dve_waited)
                return do

            def xs(it):
                return x_sb[:, bass.ds(it.b, 1), :]

            BEFORE = {F0: A0, A1: F0, ROUTE: A1, A2: ROUTE, F2: A2, A3: F2, F3: A3}

            def ln_stats(it, layer):
                if layer == A0:
                    if it.rep == 0:
                        dve.wait_ge(loaded[5], 16)
                elif layer == A2:
                    if it.rep == 0:
                        wait(dve, MOE, "acc", Item(NE - 1, NE - 1))
                else:
                    wait(dve, BEFORE[layer], "resid", it)
                do = chain(layer, "ln", it)
                yield from do(dve.bn_stats(stats[:, it.k, :], xs(it)), alone=True)
                yield from do(dve.bn_aggr(mv[:, it.k, :], stats[:, it.k, :]), hold=False)

            def ln(it, layer):
                k = it.k
                wait(dve, layer, "rs", it)
                if it.rep >= 2:
                    wait(dve, layer, "xt", it.back(2))
                elif layer in BEFORE:
                    last = Item(B - 2 + k, B - 2 + k)
                    wait(dve, BEFORE[layer], "xt", last)
                do = chain(layer, "ln", it, 2)
                yield from do(dve.tensor_scalar(xn[:, k:k + 1, :], xs(it), mv[:, k, 0:1], rstd[:, k, 0:1], ALU.subtract, ALU.mult),
                   hold=layer in (F0, F3))

            def resid(it, layer):
                n = {A0: 0, A1: 1, A2: 2, A3: 3, F2: 6}[layer]
                wait(dve, layer, "y", it)
                out = bank[O_BANK[it.k] if layer == F2 else R_BANK[1]][:, 0:P].rearrange("p (a n) -> p a n", a=1)
                dve.scalar_tensor_tensor(xs(it), out, tanh_g[:, n:n + 1], xs(it), ALU.mult, ALU.add
                                         ).then_inc(E[layer]["resid"].sem, 1)

            def resid_q(it, layer):
                wait(dve, layer, "y", it)
                scale = hs[:, it.k, 7:8]
                out = bank[R_BANK[1] if layer == F0 else O_BANK[it.k]][:, 0:P].rearrange("p (a n) -> p a n", a=1)
                dve.scalar_tensor_tensor(xs(it), out, scale, xs(it), ALU.mult, ALU.add).then_inc(E[layer]["resid"].sem, 1)

            def shifted(it, layer, g):
                src = bank[S_BANK[g % 2]][:, :].rearrange("p (h t) -> p h t", h=GH)
                m = mx[:, g % 2, :]
                wait(dve, layer, "scores", it, g + 1)
                do = chain(layer, "shifted", it, 2 * g)
                yield from do(dve.tensor_reduce(m, src, AX.X, ALU.max))
                if g >= 2 or it.rep >= 1:
                    wait(dve, layer, "probsT", it, g - 1)
                yield from do(dve.tensor_tensor(prob[:, g % 2, :].rearrange("p (h t) -> p h t", h=GH), src,
                                     m.rearrange("p (h a) -> p h a", a=1).to_broadcast([P, GH, P]), ALU.subtract),
                   hold=False)

            def v_sb(it, c):
                wait(dve, A0, "vps", it, c + 1)
                wait(dve, A0, "pv", it.back(2), 2 * c + 2)
                dve.tensor_copy(va0[:, it.k, 8 * c:8 * c + 8, 0:DK0], bank[bank_of_v[c]][:, :].rearrange(
                    "p (h n) -> p h n", h=8)).then_inc(E[A0]["v_sb"].sem, 1)

            def ot_sb0(it, c):
                wait(dve, A0, "ot", it, c + 1)
                if c == 0:
                    wait(dve, A0, "y", it.back(2))
                dve.tensor_copy(oT[:, it.k, 512 * c:512 * c + 512], bank[R_BANK[1]][:, :]).then_inc(E[A0]["ot_sb"].sem, 1)

            def norm0(it, g):
                src = bank[O_BANK[g % 2]][:, 0:GH * VW0].rearrange("p (h n) -> p h n", h=GH)
                wait(dve, A0, "pv", it, g + 1)
                do = chain(A0, "norm", it, 2 * g)
                r = rden[:, it.k, GH * g:GH * g + GH].rearrange("p (h a) -> p h a", a=1)
                yield from do(dve.reciprocal(r, src[:, :, DK0:VW0]))
                if g == 0:
                    wait(dve, A0, "ot", it.back(2))
                yield from do(dve.tensor_tensor(o_n[:, it.k, 256 * g:256 * g + 256].rearrange("p (h n) -> p h n", h=GH),
                                     src[:, :, 0:DK0], r.to_broadcast([P, GH, DK0]), ALU.mult), hold=False)

            def norm(it, layer):
                src = bank[O_BANK[it.k]][:, 0:H * VW].rearrange("p (h n) -> p h n", h=H)
                wait(dve, layer, "pv", it)
                do = chain(layer, "norm", it)
                r = rden[:, it.k, :].rearrange("p (h a) -> p h a", a=1)
                yield from do(dve.reciprocal(r, src[:, :, DK:VW]))
                wait(dve, layer, "ot", it.back(2))
                yield from do(dve.tensor_tensor(o_n[:, it.k, 0:P].rearrange("p (h n) -> p h n", h=H), src[:, :, 0:DK],
                                     r.to_broadcast([P, H, DK]), ALU.mult), hold=False)

            def shift2(it):
                wait(dve, A2, "scores", it)
                wait(dve, A2, "probs", it.back(2))
                do = chain(A2, "shift", it)
                yield from do(dve.tensor_reduce(mx[:, it.k, 0:1], bank[S_BANK[it.k]][:, 0:P], AX.X, ALU.max))
                yield from do(dve.tensor_scalar(mx[:, it.k, 1:2], mx[:, it.k, 0:1], -float(P) ** -0.5, None, ALU.mult), hold=False)

            def norm2(it):
                wait(dve, A2, "pv", it)
                wait(dve, A2, "probs", it)
                do = chain(A2, "norm", it)
                yield from do(dve.reciprocal(rden[:, it.k, 0:1], rden[:, it.k, 1:2]))
                wait(dve, A2, "ot", it.back(2))
                yield from do(dve.tensor_scalar(o_n[:, it.k, 0:P], bank[O_BANK[it.k]][:, 0:P], rden[:, it.k, 0:1], None, ALU.mult),
                   hold=False)

            def quant0(it):
                k = it.k
                if it.rep == 0:
                    dve.wait_ge(red_dve, RED_DONE)
                do = chain(F0, "quant", it)
                wait(dve, F0, "silu", it.back(2))
                yield from do(dve.tensor_reduce(qs[:, k, 0:1], xn[:, k, :], AX.X, ALU.max, apply_absolute_value=True))
                yield from do(dve.tensor_scalar(qs[:, k, 1:2], qs[:, k, 0:1], 1e-5, 1.0 / 127.0, ALU.max, ALU.mult))
                yield from do(dve.reciprocal(qs[:, k, 2:3], qs[:, k, 1:2]))
                yield from do(dve.tensor_scalar(qs[:, k, 3:5], wmean[:, 0:2], qs[:, k, 1:2], None, ALU.mult))
                wait(dve, F0, "xt", it.back(2))
                yield from do(dve.tensor_scalar(xm[:, k, :], xn[:, k, :], qs[:, k, 2:3], MAGIC, ALU.mult, ALU.add))

            def hid0(it):
                k = it.k
                wait(dve, F0, "up", it)
                wait(dve, F0, "silu", it)
                do = chain(F0, "hid", it)
                yield from do(dve.scalar_tensor_tensor(hid[:, k, :], bank[O_BANK[k]][:, :], qs[:, k, 4:5], sg[:, k, :], ALU.mult, ALU.mult))
                yield from do(dve.tensor_reduce(hs[:, k, 0:1], hid[:, k, :], AX.X, ALU.max, apply_absolute_value=True))
                yield from do(dve.tensor_scalar(hs[:, k, 1:2], hs[:, k, 0:1], 1e-5, 1.0 / 127.0, ALU.max, ALU.mult))
                yield from do(dve.reciprocal(hs[:, k, 2:3], hs[:, k, 1:2]))
                yield from do(dve.tensor_scalar(hs[:, k, 7:8], hs[:, k, 1:2], wmean[:, 2:3], tanh_g[:, 4:5], ALU.mult, ALU.mult))
                wait(dve, F0, "ht", it.back(2))
                yield from do(dve.tensor_scalar(hid2[:, k, :], hid[:, k, :], hs[:, k, 2:3], MAGIC, ALU.mult, ALU.add))

            def rms_quant(do, v, wm, xw):
                yield from do(dve.tensor_scalar(v[:, 5:6], v[:, 1:2], v[:, 4:5], 1e-5, ALU.mult, ALU.max))
                yield from do(dve.reciprocal(v[:, 6:7], v[:, 5:6]))
                yield from do(dve.tensor_scalar(v[:, 6:7], v[:, 6:7], v[:, 4:5], 127.0, ALU.mult, ALU.mult))
                yield from do(dve.tensor_scalar(v[:, 3:4], v[:, 5:6], wm, 1.0 / 127.0, ALU.mult, ALU.mult))
                yield from do(dve.tensor_scalar(xw, xw, v[:, 6:7], MAGIC, ALU.mult, ALU.add))

            def quant3(it):
                k = it.k
                do = chain(F3, "quant", it)
                wait(dve, F3, "xt", it.back(2))
                wait(dve, F3, "relu", it.back(2))
                yield from do(dve.tensor_tensor_reduce(xm[:, k, :], xn[:, k, :], xn[:, k, :], 1.0, 0.0, ALU.mult, ALU.add, qs[:, k, 0:1]))
                yield from do(dve.tensor_tensor(xm[:, k, :], xn[:, k, :], col["nw1"], ALU.mult))
                yield from do(dve.tensor_reduce(qs[:, k, 1:2], xm[:, k, :], AX.X, ALU.max, apply_absolute_value=True))
                wait(dve, F3, "rq", it)
                yield from rms_quant(do, qs[:, k, :], wmean[:, 5:6], xm[:, k, :])

            def ln_whole(it, layer):
                yield from ln_stats(it, layer)
                yield from ln(it, layer)

            def ln_quant(it, layer):
                yield from ln_whole(it, layer)
                yield from (quant0 if layer == F0 else quant3)(it)

            def hq3(it):
                k = it.k
                do = chain(F3, "hq", it)
                wait(dve, F3, "hw", it)
                yield from do(dve.tensor_reduce(hs[:, k, 1:2], hid2[:, k, :], AX.X, ALU.max, apply_absolute_value=True))
                wait(dve, F3, "rh", it)
                yield from rms_quant(do, hs[:, k, :], wmean[:, 6:7], hid2[:, k, :])
                yield from do(dve.tensor_scalar(hs[:, k, 7:8], hs[:, k, 3:4], tanh_g[:, 7:8], None, ALU.mult))

            def hid2_ln(it):
                k = it.k
                wait(dve, F2, "gelu", it)
                do = chain(F2, "hid", it)
                yield from do(dve.bn_stats(stats_h[:, k, :], hid[:, k, :]), alone=True)
                yield from do(dve.bn_aggr(mv_h[:, k, :], stats_h[:, k, :]), hold=False)
                wait(dve, F2, "rs_hid", it)
                yield from do(dve.tensor_scalar(hid[:, k, :], hid[:, k, :], mv_h[:, k, 0:1], rstd[:, k, 1:2], ALU.subtract, ALU.mult),
                   hold=False)

            def lg_sb(it):
                wait(dve, ROUTE, "logits", it)
                do = chain(ROUTE, "lg", it)
                src = bank[S_BANK[0]][:, 0:NE].rearrange("p (a n) -> p a n", a=1)
                yield from do(dve.tensor_reduce(rden[:, it.k, 2:3], src, AX.X, ALU.max))
                yield from do(dve.tensor_scalar(lg[:, bass.ds(it.b, 1), :], src, rden[:, it.k, 2:3], None, ALU.subtract))

            def acc(it, tc):
                wait(dve, MOE, "y", it, tc + 1)
                wait(dve, MOE, "acc", it.back(1), 4 * tc + 4)
                for tt in range(4):
                    b = 4 * tc + tt
                    dve.scalar_tensor_tensor(x_sb[:, b, :], bank[O_BANK[tc]][:, P * tt:P * tt + P],
                                             w_tok[:, b, bass.ds(it.b, 1)], x_sb[:, b, :], ALU.mult, ALU.add
                                             ).then_inc(E[MOE]["acc"].sem, 1)

            class Count:

                def __init__(self, s):
                    self.s, self.n = s, 0

                def do(self, ins, hold=True):
                    ins.then_inc(self.s, 1)
                    self.n += 1
                    if hold:
                        dve.wait_ge(self.s, self.n)

            rt = Count(rt_dve)

            def route():
                def bc(ap):
                    return ap.rearrange("p (b a) -> p b a", a=1).to_broadcast([P, B, NE])

                dve.wait_ge(rt_act, 1)
                rt.do(dve.tensor_reduce(psum_r[:, :], pr[:, :, :], AX.X, ALU.add))
                rt.do(dve.reciprocal(psum_r[:, :], psum_r[:, :]))
                rt.do(dve.tensor_tensor(pr[:, :, :], pr[:, :, :], bc(psum_r[:, :]), ALU.mult))
                for b in range(B):
                    rt.do(dve.max(top[:, b, :], pr[:, b, :]), hold=(b == B - 1))
                for b in range(B):
                    rt.do(dve.max_index(topi[:, b, :], top[:, b, :], pr[:, b, :]), hold=(b == B - 1))
                rt.do(dve.tensor_copy(topf[:, :, :], topi[:, :, :]), hold=False)
                rt.do(dve.tensor_tensor(gsum[:, :], top[:, :, 0], top[:, :, 1], ALU.add))
                rt.do(dve.reciprocal(gsum[:, :], gsum[:, :]), hold=False)
                eiota = col["eiota"].rearrange("p (a e) -> p a e", a=1).to_broadcast([P, B, NE])
                rt.do(dve.tensor_tensor(oh1[:, :, :], eiota, topf[:, :, 0:1].to_broadcast([P, B, NE]), ALU.is_equal), hold=False)
                rt.do(dve.tensor_tensor(oh2[:, :, :], eiota, topf[:, :, 1:2].to_broadcast([P, B, NE]), ALU.is_equal))
                rt.do(dve.tensor_tensor(chosen[:, :, :], oh1[:, :, :], oh2[:, :, :], ALU.add), hold=False)
                rt.do(dve.memset(before_b[:, 0, :], 0.0))
                for b in range(1, B):
                    rt.do(dve.tensor_tensor(before_b[:, b, :], before_b[:, b - 1, :], chosen[:, b - 1, :], ALU.add))
                assert rt.n == RT_CHOSEN, rt.n
                rt.do(dve.tensor_tensor(g12[:, :, :], top[:, :, 0:2],
                                        gsum[:, :].rearrange("p (b a) -> p b a", a=1).to_broadcast([P, B, 2]), ALU.mult))
                rt.do(dve.tensor_scalar(g12[:, :, :], g12[:, :, :], tanh_g[:, 5:6], None, ALU.mult))
                rt.do(dve.tensor_tensor(oh1[:, :, :], oh1[:, :, :], g12[:, :, 0:1].to_broadcast([P, B, NE]), ALU.mult), hold=False)
                rt.do(dve.tensor_tensor(oh2[:, :, :], oh2[:, :, :], g12[:, :, 1:2].to_broadcast([P, B, NE]), ALU.mult))
                rt.do(dve.tensor_tensor(w_tok[:, :, :], oh1[:, :, :], oh2[:, :, :], ALU.add))
                dve.wait_ge(rt_pe, 1)
                rt.do(dve.tensor_scalar(keep[:, :, :], bank[R_BANK[0]][:, 0:B * NE].rearrange("p (b e) -> p b e", b=B),
                                        float(CAP), None, ALU.is_lt))
                rt.do(dve.tensor_tensor(w_tok[:, :, :], w_tok[:, :, :], keep[:, :, :], ALU.mult))
                assert rt.n == RT_WEIGHTS, rt.n

            def route_bias():
                wait(dve, MOE, "acc", Item(0, 0), 4)
                for c in range(2):
                    dve.wait_ge(rt_pe, 3 + c)
                    xc = x_sb[:, 4 * c:4 * c + 4, :]
                    rt.do(dve.tensor_tensor(xc, xc, bank[R_BANK[c]][:, :].rearrange("p (b n) -> p b n", b=4), ALU.add))
                assert rt.n == RT_BIAS, rt.n

            def weight_sums():
                rd = Count(red_dve)
                dve.wait_ge(loaded[3], 16)
                for n, name in enumerate(TERNARY):
                    rd.do(dve.tensor_reduce(asum[:, n:n + 1], col[name], AX.X, ALU.add, apply_absolute_value=True), hold=False)
                dve.wait_ge(red_pe, 1)
                rd.do(dve.tensor_scalar(wmean[:, :], bank[R_BANK[0]][:, 0:len(TERNARY)], 1.0 / (P * F), None, ALU.mult))
                rd.do(dve.tensor_scalar(wmean[:, 0:3], wmean[:, 0:3], 1e-5, None, ALU.max), hold=False)
                rd.do(dve.tensor_scalar(wmean[:, 3:5], wmean[:, 3:5], 1e-6, None, ALU.add), hold=False)
                rd.do(dve.tensor_scalar(wmean[:, 5:7], wmean[:, 5:7], 1e-5, None, ALU.max))
                rd.do(dve.reciprocal(winv[:, :], wmean[:, :]))
                assert rd.n == RED_DONE
                tern_count = Count(tern_dve)
                for n, name in enumerate(TERNARY):
                    t = tmp_t[:, n % 2, :]
                    tern_count.do(dve.tensor_scalar(t, col[name], winv[:, n:n + 1], -1.0, ALU.mult, ALU.max))
                    tern_count.do(dve.tensor_scalar(t, t, 1.0, MAGIC, ALU.min, ALU.add))
                    tern_count.do(dve.tensor_scalar(tern[name][:, :], t, MAGIC, None, ALU.subtract), hold=False)

            def fold():
                fd = Count(fold_dve)
                dve.wait_ge(tern_dve, 3 * len(TERNARY))
                for t in range(FT):
                    fd.do(dve.tensor_scalar(projw[:, P * t:P * t + P], tern["projT"][:, P * t:P * t + P],
                                            col["lnw_2"][:, t:t + 1], None, ALU.mult), hold=False)
                dve.wait_ge(fold_pe, 1)
                fd.do(dve.tensor_copy(crow[:, :], bank[R_BANK[1]][0:1, 0:P]), hold=False)

            def prepare():
                dve.memset(minus_magic, -MAGIC).then_inc(prep_dve, 1)
                dve.wait_ge(loaded[0], 16)
                dve.wait_ge(mask0_loaded, 16)
                dve.scalar_tensor_tensor(neg0[:, :, :], mask0_u8[:, :, :], NEG,
                                         col["causal"].rearrange("p (a t) -> p a t", a=1).to_broadcast([P, B, P]),
                                         ALU.mult, ALU.min).then_inc(prep_dve, 1)
                dve.wait_ge(kz_zero, 6)
                for b in range(B):
                    dve.wait_ge(prep_pe, 4 + b + 1)
                    for n, va in enumerate((va_1, va_3)):
                        dve.tensor_copy(va[:, b, :, 0:DK], bank[4 + b % 4][:, P * n:P * n + P].rearrange(
                            "p (h n) -> p h n", h=H)).then_inc(prep_dve, 1)
                dve.wait_ge(act_const, 1)

            def attention(layer):
                return [
                    [(1, shifted, layer, 0), (0, ln_stats, layer)],
                    [(1, shifted, layer, 1), (0, ln, layer)], (3, resid, layer),
                    (1, shifted, layer, 2),
                    [(1, shifted, layer, 3), (2, norm, layer)]]

            bank_of_v = {0: R_BANK[0], 1: R_BANK[0]}
            stages = {
                A0: [[(1, shifted, A0, 0), (0, ln_stats, A0)], (2, norm0, 1), (3, ot_sb0, 1),
                     [(1, shifted, A0, 1), (0, ln, A0)], (3, resid, A0), (2, norm0, 2), (2, ot_sb0, 0),
                     (1, shifted, A0, 2), (0, v_sb, 0), (2, norm0, 3),
                     (1, shifted, A0, 3), (0, v_sb, 1), (1, norm0, 0)],
                F0: [[(0, ln_quant, F0), (2, hid0)], (3, resid_q, F0)],
                A1: attention(A1),
                ROUTE: [[(0, ln_whole, ROUTE), (1, lg_sb)]],
                MOE: [(1, acc, 1), (0, acc, 0)],
                A2: [[(3, norm2), (2, shift2), (0, ln_whole, A2)], (3, resid, A2)],
                F2: [[(0, ln_whole, F2), (2, hid2_ln)], (3, resid, F2)],
                A3: attention(A3),
                F3: [[(0, ln_quant, F3), (2, hq3)], (3, resid_q, F3)],
            }
            prepare()
            walk(dve, PLAN, stages, before={(MOE, 0): route, (MOE, 1): route_bias, (F2, 0): fold},
                 after={(A0, 3): weight_sums})


def pack(arrays, pack_):
    import numpy as np
    return np.ascontiguousarray(np.concatenate([arrays[n].reshape(P, w) for n, w in pack_.items()], axis=1))


def kernel(**inputs):
    import numpy as np
    import concourse.bacc as bacc
    from concourse.bass_utils import run_bass_kernel_spmd as run

    a = {k: np.asarray(v) for k, v in inputs.items()}
    f = np.float32
    part = np.arange(P)

    def heads_T(w):
        return w.transpose(2, 0, 1).reshape(P, H * DK0)

    def tiles(w):
        return w.reshape(-1, P, w.shape[1]).transpose(1, 0, 2).reshape(P, -1)

    def everywhere(v):
        return np.broadcast_to(v.reshape(1, -1), (P, v.size))

    cols = dict(
        ctxT=a["ctx_1024"].transpose(2, 0, 1), ctx=a["ctx_1024"].transpose(1, 0, 2), x=a["x"].transpose(1, 0, 2),
        wkT_1=a["L1_xattn_w_k"].T, wkT_3=a["L3_xattn_w_k"].T,
        wvT_13=np.concatenate([a["L1_xattn_w_v"].T, a["L3_xattn_w_v"].T], axis=1),
        ident=np.eye(P, dtype=f), ones=np.ones((P, P), f),
        hmask=(part[:, None] // DK == np.arange(H)[None]).astype(f),
        bk_3=a["L3_xattn_b_k"], bq_3=a["L3_xattn_b_q"],
        gates=everywhere(np.concatenate([a["g_xattn"], a["g_ffn"]])),
        wkT_0=heads_T(a["L0_xattn_Wk"]), wqT_0=heads_T(a["L0_xattn_Wq"]), wvT_0=heads_T(a["L0_xattn_Wv"]),
        woT_0=tiles(a["L0_xattn_Wo"].T),
        causal=np.where(part[None] > part[:, None], f(NEG), f(0)), kiota=everywhere(part.astype(f)),
        utri=(part[:, None] < part[None]).astype(f), eiota=everywhere(np.arange(NE, dtype=f)), piota=part.astype(f),
        act_sb=everywhere(np.concatenate([a["L3_ffn_act_scale"], a["L3_ffn_act_bias"]])),
        lnw_2=a["L2_ffn_ln_w"].reshape(FT, P).T, lnb_2=a["L2_ffn_ln_b"].reshape(FT, P).T, wg=a["L1_ffn_Wg"],
        wqT_1=a["L1_xattn_w_q"].T, woT_1=a["L1_xattn_w_o"].T, wqT_3=a["L3_xattn_w_q"].T, woT_3=a["L3_xattn_w_o"].T,
        woT_2=a["L2_xattn_W"].T,
        gateT=a["L0_ffn_w_gate"].T, upT=a["L0_ffn_w_up"].T, downT=tiles(a["L0_ffn_w_down"].T),
        fcT=a["L2_ffn_W_fc"].T, projT=tiles(a["L2_ffn_W_proj"].T), w1T=a["L3_ffn_w1"].T, w2T=tiles(a["L3_ffn_w2"].T),
        nw1=everywhere(a["L3_ffn_norm1_w"]), nw2=everywhere(a["L3_ffn_norm2_w"]),
    )
    arrays = {f"pack{n}_d": pack(cols, p) for n, p in enumerate(PACKS)}
    row = dict(bv_13=np.concatenate([np.zeros(P, f), a["L3_xattn_b_v"]]), bo_1=a["L1_xattn_b_o"], bo_2=a["L2_xattn_b"],
               bo_3=a["L3_xattn_b_o"])
    arrays["rows_d"] = np.concatenate([row[n] for n in ROWS]).reshape(1, -1)
    arrays["mask0_d"] = np.ascontiguousarray(a["mask_BxSxS2_bf0"].transpose(1, 0, 2))
    arrays["mask1_d"] = np.ascontiguousarray(a["mask_BxSxS2_ik0"].transpose(1, 0, 2))
    arrays["lens_d"] = np.ascontiguousarray(everywhere(a["_lenS2"]))
    b2 = np.zeros((B, NE, B, P), f)
    for b in range(B):
        b2[b, :, b, :] = a["L1_ffn_b2"]
    arrays["b2blk_d"] = b2.reshape(B * NE, N)
    arrays["experts_d"] = np.ascontiguousarray(np.concatenate([
        a["L1_ffn_W1"], a["L1_ffn_b1"].reshape(NE, FT, P).transpose(0, 2, 1),
        a["L1_ffn_W2"].reshape(NE, FT, P, P).transpose(0, 2, 1, 3).reshape(NE, P, F)], axis=2))

    nc = bacc.Bacc("TRN2", target_bir_lowering=False, num_devices=1)
    args = [nc.dram_tensor(k, v.shape, mybir.dt.from_np(v.dtype), kind="ExternalInput").ap() for k, v in arrays.items()]
    out = nc.dram_tensor("out_d", (P, N), F32, kind="ExternalOutput").ap()
    n = len(PACKS)
    build(nc, args[:n], *args[n:], out)
    r = run(nc, [arrays], core_ids=[0])
    return np.ascontiguousarray(r.results[0]["out_d"].reshape(P, B, P).transpose(1, 0, 2))
```

```python
from contextlib import ExitStack

import concourse.bass as bass
from concourse import mybir

F32 = mybir.dt.float32
BF16 = mybir.dt.bfloat16
I32 = mybir.dt.int32
U8 = mybir.dt.uint8
U32 = mybir.dt.uint32
ALU = mybir.AluOpType
ACT = mybir.ActivationFunctionType
AX = mybir.AxisListType

P = 128
B = 8
N = B * P
H = 16
DK0 = 64
DK = P // H
GH = 4
G = H // GH
VW = DK + 1
VW0 = DK0 + 1
F = 512
FT = F // P
NE = 8
TOPK = 2
CAP = -(-N * TOPK * 105 // (NE * 100))
NEG = -1e30
MAGIC = 1.5 * 2 ** 23
LN_EPS = 1e-5
STATS = 6
SLOTS = 4

PACK_FIRST = dict(ctxT=N, wkT_1=P, wkT_3=P, wvT_13=2 * P, ident=P, ones=P, causal=P, hmask=H, bk_3=1, bq_3=1, gates=8, x=N)
PACK_ATT0 = dict(wkT_0=H * DK0, wqT_0=H * DK0, wvT_0=H * DK0, woT_0=H * DK0)
PACK_REST = dict(kiota=P, utri=P, eiota=NE, piota=1, act_sb=2, lnw_2=FT, wg=NE, lnb_2=FT,
                 wqT_1=P, woT_1=P, wqT_3=P, woT_3=P, woT_2=P)
PACK_FFN = dict(gateT=F, upT=F, downT=F, fcT=F, projT=F, w1T=F, w2T=F, nw1=P, nw2=F)
PACK_CTX = dict(ctx=N)
PACKS = [PACK_FIRST, PACK_ATT0, PACK_REST, PACK_FFN, PACK_CTX]
ROWS = dict(bv_3=P, bo_1=P, bo_2=P, bo_3=P)
EXPERT = F + FT + F
TERNARY = ["gateT", "upT", "downT", "fcT", "projT", "w1T", "w2T"]


class Item:

    def __init__(self, b, rep):
        self.b, self.rep, self.k = b, rep, rep % 2

    def back(self, n):
        return Item(self.b - n, self.rep - n) if self.rep - n >= 0 else None


class Event:

    def __init__(self, sem, per, base):
        self.sem, self.per, self.base = sem, per, base

    def at(self, item, j=None):
        return self.per * item.b + (self.base + (self.per if j is None else j))


def steps_of(offsets):
    last = max(at + B + LAG[n] for n, at in offsets.items())
    return [("steps", [(n, t - at) for n, at in offsets.items() if 0 <= t - at < B + LAG[n]]) for t in range(last)]


def turns(*parts):
    parts = list(parts)
    while parts:
        for p in list(parts):
            if next(p, parts) is parts:
                parts.remove(p)
            else:
                yield


def walk(eng, plan, stages, before={}, after={}, run=lambda layer, fn, it, *args: fn(it, *args)):

    def stage(layer, s, loop, lag, fn, *args):
        rep = s - lag
        if 0 <= rep < B:
            held = run(layer, fn, Item(rep if loop is None else 2 * loop + rep, rep), *args)
            if held is None:
                yield
            else:
                yield from held

    def slot(layer, s, entries, loop=None):
        for entry in entries:
            if entry is None:
                yield
                continue
            for_turns = entry if isinstance(entry, list) else [entry]
            yield from turns(*[stage(layer, s, loop, *e) for e in for_turns])

    def single(layer, s, loop=None):
        for n in range(SLOTS):
            for _ in slot(layer, s, stages[layer][n], loop):
                pass

    for what in plan:
        if what[0] == "steps":
            for at in what[1]:
                before.get(at, lambda: None)()
            for n in range(SLOTS):
                for _ in turns(*[slot(layer, s, stages[layer][n]) for layer, s in what[1] if layer in stages]):
                    pass
            for at in what[1]:
                after.get(at, lambda: None)()
        elif what[1] in stages:
            _, layer, first, passes = what
            if eng is None:
                for s in range(first, first + 2 * passes):
                    single(layer, s)
            else:
                with eng.Fori(0, passes) as i:
                    for s in range(first, first + 2):
                        single(layer, s, i)


RED_DONE = len(TERNARY) + 6
RT_CHOSEN = 3 + 2 * B + 6 + 1 + (B - 1)
RT_WEIGHTS = RT_CHOSEN + 7
RT_BIAS = RT_WEIGHTS + 2

A0, F0, A1, ROUTE, MOE, A2, F2, A3, F3 = range(9)
LAG = [3, 2, 3, 1, 1, 3, 2, 3, 2]
KIND = ["att", "ffn", "att", "route", "moe", "att", "ffn", "att", "ffn"]
SIDE = [0, 1, 0, 1, None, 0, 1, 0, 1]
PLAN = (steps_of({F0: 4, A0: 0, A1: 8, ROUTE: 12})
        + [("steps", [(MOE, 0)]), ("steps", [(MOE, 1)]), ("loop", MOE, 2, (NE - 2) // 2), ("steps", [(MOE, NE)])]
        + steps_of({A2: 0, F2: 4, A3: 8, F3: 12}))


def build(nc, packs, rows_d, mask0_d, mask1_d, lens_d, b2blk_d, experts_d, out_d):
    with ExitStack() as ctx:
        def sb(name, shape, dt=F32):
            return ctx.enter_context(nc.sbuf_tensor(name, shape, dt))

        def sem(name):
            return ctx.enter_context(nc.semaphore(name))

        shared = {}

        def events(layer, **per):
            out = {}
            for name, n in per.items():
                key = f"{KIND[layer]}_{name}"
                s, base = shared.get(key) or (sem(key), 0)
                out[name] = Event(s, n, base)
                shared[key] = s, base + n * B
            return out

        col = {}
        packed = []
        for n, pack in enumerate(PACKS):
            tile = sb(f"pack{n}", [P, sum(pack.values())])
            packed.append(tile)
            at = 0
            for name, w in pack.items():
                col[name] = tile[:, at:at + w]
                at += w
        rows_sb = sb("rows_sb", [1, sum(ROWS.values())])
        row = {}
        at = 0
        for name, w in ROWS.items():
            row[name] = rows_sb[0:1, at:at + w]
            at += w
        x_sb = col["x"].rearrange("p (b d) -> p b d", b=B)
        ctxT = col["ctxT"].rearrange("p (b t) -> p b t", b=B)
        ctx_tok = col["ctx"].rearrange("p (b d) -> p b d", b=B)
        ident = col["ident"]
        ones = col["ones"]
        identb = sb("identb", [P, P], BF16)
        onesb = sb("onesb", [P, P], BF16)
        utrib = sb("utrib", [P, P], BF16)
        tanh_g = sb("tanh_g", [P, 8])
        mask0_u8 = sb("mask0_u8", [P, B, P], U8)
        mask1_i32 = sb("mask1_i32", [P, B, P], I32)
        lens_i = sb("lens_i", [P, B], I32)
        lens_f = sb("lens_f", [P, B])
        qneg = sb("qneg", [P, B])
        neg0 = sb("neg0", [P, B, P], BF16)
        neg1 = sb("neg1", [P, B, P], BF16)
        neg2 = sb("neg2", [P, B, P], BF16)
        b2blk = sb("b2blk", [NE * B, N])
        kT_1 = sb("kT_1", [P, B, P])
        kT_3 = sb("kT_3", [P, B, P])
        va_1 = sb("va_1", [P, B, H, VW])
        va_3 = sb("va_3", [P, B, H, VW])

        stats = [sb(f"stats{n}", [P, 2, STATS]) for n in range(2)]
        mv = [sb(f"mv{n}", [P, 2, 2]) for n in range(2)]
        stats_h = sb("stats_h", [P, 2, STATS])
        mv_h = sb("mv_h", [P, 2, 2])
        rstd = [sb(f"rstd{n}", [P, 2, 4]) for n in range(2)]
        xn = [sb(f"xn{n}", [P, 2, P]) for n in range(2)]
        xnT = [sb(f"xnT{n}", [P, 2, P]) for n in range(2)]
        qT = sb("qT", [P, 2, H * DK0])
        kz = sb("kz", [P, 2, 2 * H * DK0])
        va0 = sb("va0", [P, 2, H, VW0])
        prob = sb("prob", [P, 2, F])
        probT = sb("probT", [P, 2, F])
        mx = sb("mx", [P, 2, GH])
        rden = sb("rden", [P, 2, H])
        o_n = sb("o_n", [P, 2, H * DK0])
        oT = sb("oT", [P, 2, H * DK0])

        minus_half = sb("minus_half", [P, 1])[:, 0:1]
        minus_magic = sb("minus_magic", [P, 1])[:, 0:1]
        xm = sb("xm", [P, 2, P])
        xqT = sb("xqT", [P, 2, P], BF16)
        qs = sb("qs", [P, 2, 8])
        hs = sb("hs", [P, 2, 8])
        hid = sb("hid", [P, 2, F])
        hid2 = sb("hid2", [P, 2, F])
        sg = sb("sg", [P, 2, F])
        hqT = sb("hqT", [P, 2, F], BF16)
        tern = {n: sb(f"t_{n}", [P, F], F32 if n in ("fcT", "projT") else BF16) for n in TERNARY}
        tmp_t = sb("tmp_t", [P, 2, F])
        asum = sb("asum", [P, len(TERNARY)])
        wmean = sb("wmean", [P, len(TERNARY)])
        winv = sb("winv", [P, len(TERNARY)])
        projw = sb("projw", [P, F])
        crow = sb("crow", [1, P])

        xnT_all = sb("xnT_all", [P, B, P])
        lg_max = sb("lg_max", [P, 2])
        lg = sb("lg", [P, B, NE])
        pr = sb("pr", [P, B, NE])
        psum_r = sb("psum_r", [P, B])
        top = sb("top", [P, B, NE])
        topi = sb("topi", [P, B, NE], U32)
        topf = sb("topf", [P, B, NE])
        gsum = sb("gsum", [P, B])
        g12 = sb("g12", [P, B, 2])
        oh1 = sb("oh1", [P, B, NE])
        oh2 = sb("oh2", [P, B, NE])
        chosen = sb("chosen", [P, B, NE], BF16)
        before_b = sb("before_b", [P, B, NE], BF16)
        keep = sb("keep", [P, B, NE])
        w_tok = sb("w_tok", [P, B, NE])
        w_tokT = sb("w_tokT", [B * NE, P])
        expert = sb("expert", [P, 2, EXPERT])
        hT = kz[:, :, :].rearrange("p k (t n) -> p k t n", t=FT)

        bank = [ctx.enter_context(nc.psum_tensor(f"bank{i}", [P, 512], F32)) for i in range(8)]
        S_BANK, T_BANK, O_BANK, R_BANK = (0, 1), (2, 3), (4, 5), (6, 7)

        loaded = [sem(f"loaded{n}") for n in range(len(PACKS) + 1)]
        rows_loaded, mask0_loaded, mask1_loaded = sem("rows_loaded"), sem("mask0_loaded"), sem("mask1_loaded")
        lens_loaded, b2_loaded = sem("lens_loaded"), sem("b2_loaded")
        expert_loaded = [sem(f"expert_loaded{k}") for k in range(2)]
        stored = sem("stored")
        pool_const = sem("pool_const")
        tern_dve = sem("tern_dve")
        kv_pe = sem("kv_pe")
        kv_act = sem("kv_act")
        prep_dve = sem("prep_dve")
        gates_ready = sem("gates_ready")
        cleared = sem("cleared")
        wsum_dve = sem("wsum_dve")
        wsum_pe = sem("wsum_pe")
        fold_dve = sem("fold_dve")
        fold_pe = sem("fold_pe")
        route_dve = sem("route_dve")
        route_act = sem("route_act")
        route_pe = sem("route_pe")

        att = dict(ln=3, rs=2, xt=1, xt_sb=1, scores=G, shifted=2 * G, probs=G, probsT=G, probsT_sb=G, pv=G, y=1, resid=1)
        ffn = dict(ln=3, rs=2, xt=1, xt_sb=1, ht=1, ht_sb=1, y=1, resid=1)
        E = {
            A0: events(A0, **att, kps=2, k_sb=4, qps=2, q_sb=2, vps=2, v_sb=2, norm=2 * G, ot=2, ot_sb=2),
            F0: events(F0, **ffn, gate=1, up=1, tanh=1, gate_sb=1, up_sb=1, quant=5, hid=7),
            A1: events(A1, **att, q=1, q_sb=1, kz=2, norm=2, ot=1, ot_sb=1),
            ROUTE: events(ROUTE, ln=3, rs=2, xt=1, xt_sb=1, copied=1, logits=1, lg=2),
            MOE: events(MOE, h=8, gelu=8, y=2, acc=8),
            A2: events(A2, ln=3, rs=2, xt=1, xt_sb=1, scores=1, shift=2, probs=1, probsT=1, probsT_sb=1, pv=1,
                       norm=2, ot=1, ot_sb=1, y=1, resid=1),
            F2: events(F2, **ffn, up=1, gelu=1, hid=3, rs_hid=2),
            A3: events(A3, **att, q=1, q_sb=1, kz=2, norm=2, ot=1, ot_sb=1),
            F3: events(F3, **ffn, quant=8, rq=2, up=1, relu=1, squared=1, biased=1, sumsq=1, hw=1, rh=2, hq=7),
        }
        emptied = {
            (A0, "xt"): ("xt_sb", 1), (A0, "k0"): ("k_sb", 2), (A0, "k1"): ("k_sb", 4), (A0, "q0"): ("q_sb", 1),
            (A0, "q1"): ("q_sb", 2), (A0, "v0"): ("v_sb", 1), (A0, "v1"): ("v_sb", 2), (A0, "ot0"): ("ot_sb", 1),
            (A0, "ot1"): ("ot_sb", 2), (A0, "y"): ("resid", 1),
            (A2, "xt"): ("xt_sb", 1), (A2, "s"): ("probs", 1), (A2, "t"): ("probsT_sb", 1), (A2, "pv"): ("norm", 2),
            (A2, "ot"): ("ot_sb", 1), (A2, "y"): ("resid", 1),
            (F0, "xt"): ("xt_sb", 1), (F0, "gate"): ("gate_sb", 1), (F0, "up"): ("up_sb", 1), (F0, "ht"): ("ht_sb", 1),
            (F0, "y"): ("resid", 1),
            (F3, "xt"): ("xt_sb", 1), (F3, "up"): ("relu", 1), (F3, "ht"): ("ht_sb", 1), (F3, "y"): ("resid", 1),
            (F2, "xt"): ("xt_sb", 1), (F2, "up"): ("gelu", 1), (F2, "ht"): ("ht_sb", 1), (F2, "y"): ("resid", 1),
            (ROUTE, "xt"): ("xt_sb", 1), (ROUTE, "lg"): ("lg", 2),
        }
        for a in (A0, A1, A3):
            for g in range(G):
                emptied[a, f"s{g}"] = ("shifted", 2 * g + 2)
                emptied[a, f"t{g}"] = ("probsT_sb", g + 1)
                emptied[a, f"pv{g}"] = ("norm", 2 * g + 2 if a == A0 else 2)
        for a in (A1, A3):
            emptied[a, "xt"] = ("xt_sb", 1)
            emptied[a, "q"] = ("q_sb", 1)
            emptied[a, "ot"] = ("ot_sb", 1)
            emptied[a, "y"] = ("resid", 1)
        for tc in range(2):
            for ht in range(FT):
                emptied[MOE, f"h{tc}{ht}"] = ("gelu", 4 * tc + ht + 1)
            emptied[MOE, f"y{tc}"] = ("acc", 4 * tc + 4)

        def wait(eng, layer, name, item, j=None):
            if item is not None:
                ev = E[layer][name]
                eng.wait_ge(ev.sem, ev.at(item, j))

        bank_of_up = {F0: T_BANK[1], F2: T_BANK[1], F3: T_BANK[1]}
        bank_of_ht = {F0: T_BANK[1], F2: T_BANK[0], F3: T_BANK[0]}
        bank_of_y = {F0: R_BANK[0], F2: R_BANK[1], F3: R_BANK[1]}

        block = ctx.enter_context(nc.Block())

        @block.sync
        def _(sp):
            cut = sum(PACK_FIRST.values()) - N
            sp.dma_start(packed[0][:, 0:cut], packs[0][:, 0:cut]).then_inc(loaded[0], 16)
            sp.dma_start(packed[0][:, cut:], packs[0][:, cut:]).then_inc(loaded[5], 16)
            sp.dma_start(rows_sb[:, :], rows_d).then_inc(rows_loaded, 16)
            sp.dma_start(mask0_u8[:, :, :], mask0_d).then_inc(mask0_loaded, 16)
            sp.dma_start(packed[1][:, :], packs[1]).then_inc(loaded[1], 16)
            sp.dma_start(packed[2][:, :], packs[2]).then_inc(loaded[2], 16)

            def load_expert(it):
                wait(sp, MOE, "y", it.back(2))
                sp.dma_start(expert[:, it.k, :], experts_d[bass.ds(it.b, 1)].rearrange("a p n -> p (a n)")
                             ).then_inc(expert_loaded[it.k], 16)

            sp.dma_start(packed[3][:, :], packs[3]).then_inc(loaded[3], 16)
            sp.dma_start(mask1_i32[:, :, :], mask1_d).then_inc(mask1_loaded, 16)
            sp.dma_start(lens_i[:, :], lens_d).then_inc(lens_loaded, 16)
            sp.dma_start(b2blk[:, :], b2blk_d).then_inc(b2_loaded, 16)
            sp.dma_start(packed[4][:, :], packs[4]).then_inc(loaded[4], 16)

            walk(sp, PLAN, {MOE: [[(0, load_expert)], [], [], []]})
            wait(sp, F3, "resid", Item(B - 1, B - 1))
            sp.dma_start(out_d, col["x"]).then_inc(stored, 16)
            sp.wait_ge(stored, 16)

        @block.gpsimd
        def _(pool):
            pool.memset(minus_half, -0.5).then_inc(pool_const, 1)
            for k in range(2):
                pool.memset(kz[:, k, :], 0.0).then_inc(cleared, 1)
                pool.memset(va0[:, k, :, DK0:VW0], 1.0).then_inc(cleared, 1)
            for va in (va_1, va_3):
                pool.memset(va[:, :, :, DK:VW], 1.0).then_inc(cleared, 1)
            pool.wait_ge(loaded[0], 16)
            pool.tensor_copy(identb[:, :], ident).then_inc(pool_const, 1)
            pool.tensor_copy(onesb[:, :], ones).then_inc(pool_const, 1)
            def masks():
                pool.wait_ge(loaded[2], 16)
                pool.tensor_copy(utrib[:, :], col["utri"]).then_inc(pool_const, 1)
                pool.wait_ge(mask1_loaded, 16)
                pool.tensor_scalar(neg1[:, :, :], mask1_i32[:, :, :], 0.0, NEG, ALU.is_equal, ALU.mult).then_inc(pool_const, 1)
                pool.wait_ge(lens_loaded, 16)
                pool.tensor_copy(lens_f[:, :], lens_i[:, :]).then_inc(pool_const, 1)
                pool.wait_ge(pool_const, 6)
                pool.tensor_scalar(qneg[:, :], lens_f[:, :], col["piota"], NEG, ALU.is_le, ALU.mult).then_inc(pool_const, 1)
                pool.wait_ge(pool_const, 7)
                for b in range(B):
                    pool.tensor_scalar(neg2[:, b, :], col["kiota"], lens_f[:, b:b + 1], qneg[:, b:b + 1], ALU.is_ge,
                                       ALU.mult).then_inc(pool_const, 1)

            def inverse_root(it, layer, name, out, src, scale, eps):
                ev = E[layer][name]
                pool.tensor_scalar(out, src, scale, eps, ALU.mult, ALU.add).then_inc(ev.sem, 1)
                pool.wait_ge(ev.sem, ev.at(it, 1))
                pool.tensor_tensor(out, out, minus_half, ALU.pow).then_inc(ev.sem, 1)

            def rs(it, layer):
                wait(pool, layer, "ln", it, 2)
                inverse_root(it, layer, "rs", rstd[SIDE[layer]][:, it.k, 0:1], mv[SIDE[layer]][:, it.k, 1:2], 1.0, LN_EPS)

            def rs_hid(it):
                wait(pool, F2, "hid", it, 2)
                inverse_root(it, F2, "rs_hid", rstd[1][:, it.k, 1:2], mv_h[:, it.k, 1:2], 1.0, LN_EPS)

            def rms(it, src, j, v, n, name):
                wait(pool, F3, src, it, j)
                inverse_root(it, F3, name, v[:, it.k, 4:5], v[:, it.k, 0:1], 1.0 / n, 1e-8)

            def weigh(it):
                wait(pool, F3, "biased", it)
                wait(pool, F3, "ht", it.back(2))
                pool.tensor_tensor(hid2[:, it.k, :], hid[:, it.k, :], col["nw2"], ALU.mult).then_inc(E[F3]["hw"].sem, 1)

            def mask_keys(it, layer, kT, half):
                if it.rep == 0 and half == 0:
                    pool.wait_ge(kv_act, 2 if layer == A1 else 6)
                if it.rep >= 2:
                    wait(pool, layer, "scores", it.back(2))
                elif layer == A1:
                    wait(pool, A0, "scores", Item(B - 2 + it.k, B - 2 + it.k))
                heads = H // 2
                pool.tensor_tensor(kz[:, it.k, 1024 * half:1024 * half + 1024].rearrange("p (h t) -> p h t", h=heads),
                                   kT[:, bass.ds(it.b, 1), :].to_broadcast([P, heads, P]),
                                   col["hmask"][:, heads * half:heads * half + heads].rearrange(
                                       "p (h a) -> p h a", a=1).to_broadcast([P, heads, P]),
                                   ALU.mult).then_inc(E[layer]["kz"].sem, 1)

            def copy_xnT(it):
                wait(pool, ROUTE, "xt_sb", it)
                pool.tensor_copy(xnT_all[:, bass.ds(it.b, 1), :], xnT[1][:, it.k:it.k + 1, :]).then_inc(E[ROUTE]["copied"].sem, 1)

            stages = {
                A0: [[(0, rs, A0)], [], [], []],
                F0: [[(0, rs, F0)], [], [], []],
                A1: [[(0, rs, A1)], [(0, mask_keys, A1, kT_1, 0)], [(0, mask_keys, A1, kT_1, 1)], []],
                ROUTE: [[(0, rs, ROUTE)], [], [], [(0, copy_xnT)]],
                A2: [[(0, rs, A2)], [], [], []],
                F2: [[(0, rs, F2)], [], [(1, rs_hid)], []],
                A3: [[(0, rs, A3)], [(0, mask_keys, A3, kT_3, 0)], [(0, mask_keys, A3, kT_3, 1)], []],
                F3: [[(0, rs, F3)], [(0, rms, "quant", 1, qs, P, "rq")], [(1, weigh), (1, rms, "sumsq", 1, hs, F, "rh")], []],
            }
            walk(pool, PLAN, stages, after={(A0, 1): masks})

        @block.scalar
        def _(act):
            def evac(dst, src, layer, name, **kw):
                act.activation(dst, src, ACT.Identity if kw else ACT.Copy, **kw).then_inc(E[layer][name].sem, 1)

            def xt_sb(it, layer):
                wait(act, layer, "xt", it)
                if layer == ROUTE:
                    wait(act, ROUTE, "copied", it.back(2))
                evac(xnT[SIDE[layer]][:, it.k, :], bank[R_BANK[0]][:, 0:P], layer, "xt_sb")

            def exps(it, layer, g):
                wait(act, layer, "shifted", it, 2 * g + 2)
                act.activation(prob[:, g % 2, :], prob[:, g % 2, :], ACT.Exp,
                               scale=float(DK0 if layer == A0 else DK) ** -0.5).then_inc(E[layer]["probs"].sem, 1)

            def probsT_sb(it, layer, g):
                wait(act, layer, "probsT", it, g + 1)
                evac(probT[:, g % 2, :], bank[T_BANK[g % 2]][:, :], layer, "probsT_sb")

            def k_sb(it, c):
                wait(act, A0, "kps", it, c + 1)
                kv = kz[:, it.k, :].rearrange("p (t a n) -> p t a n", t=8, a=2)
                src = bank[R_BANK[0]][:, :].rearrange("p (t n) -> p t n", t=4)
                for a in range(2):
                    evac(kv[64 * a:64 * a + 64, 4 * c:4 * c + 4, a, :], src[64 * a:64 * a + 64], A0, "k_sb")

            def q_sb0(it, c):
                wait(act, A0, "qps", it, c + 1)
                evac(qT[:, it.k, 512 * c:512 * c + 512], bank[R_BANK[1]][:, :], A0, "q_sb")

            def q_sb(it, layer):
                wait(act, layer, "q", it)
                if layer == A3:
                    evac(qT[:, it.k, 0:P], bank[R_BANK[1]][:, 0:P], layer, "q_sb", bias=col["bq_3"])
                else:
                    evac(qT[:, it.k, 0:P], bank[R_BANK[1]][:, 0:P], layer, "q_sb")

            def ot_sb(it, layer):
                wait(act, layer, "ot", it)
                evac(oT[:, it.k, 0:P], bank[R_BANK[0]][:, 0:P], layer, "ot_sb")

            def exps2(it):
                wait(act, A2, "scores", it)
                wait(act, A2, "shift", it)
                act.activation(prob[:, it.k, 0:P], bank[S_BANK[it.k]][:, 0:P], ACT.Exp, bias=mx[:, it.k, 1:2],
                               scale=float(P) ** -0.5, accum_out=rden[:, it.k, 1:2]).then_inc(E[A2]["probs"].sem, 1)

            def probsT_sb2(it):
                wait(act, A2, "probsT", it)
                evac(probT[:, it.k, 0:P], bank[O_BANK[1 - it.k]][:, 0:P], A2, "probsT_sb")

            def xq_sb(it, layer):
                wait(act, layer, "xt", it)
                evac(xqT[:, it.k, :], bank[R_BANK[0]][:, 0:P], layer, "xt_sb", bias=minus_magic)

            def hq_sb(it, layer):
                wait(act, layer, "ht", it)
                evac(hqT[:, it.k, :], bank[bank_of_ht[layer]][:, :], layer, "ht_sb", bias=minus_magic)

            def half_gate(it):
                wait(act, F0, "gate", it)
                wait(act, F0, "quant", it)
                wait(act, F0, "hid", it.back(2))
                act.activation(sg[:, it.k, :], bank[T_BANK[0]][:, :], ACT.Tanh, scale=qs[:, it.k, 3:4]
                               ).then_inc(E[F0]["tanh"].sem, 1)
                evac(hid[:, it.k, :], bank[T_BANK[0]][:, :], F0, "gate_sb", scale=qs[:, it.k, 3:4])

            def up_sb(it):
                wait(act, F0, "up", it)
                wait(act, F0, "ht", it.back(2))
                evac(hid2[:, it.k, :], bank[bank_of_up[F0]][:, :], F0, "up_sb", scale=qs[:, it.k, 4:5])

            def relu3(it):
                k = it.k
                wait(act, F3, "up", it)
                wait(act, F3, "quant", it)
                act.activation(sg[:, k, :], bank[bank_of_up[F3]][:, :], ACT.Relu, scale=qs[:, k, 3:4]
                               ).then_inc(E[F3]["relu"].sem, 1)
                wait(act, F3, "relu", it)
                act.activation(sg[:, k, :], sg[:, k, :], ACT.Square).then_inc(E[F3]["squared"].sem, 1)

            def hid3(it):
                k = it.k
                wait(act, F3, "hw", it.back(2))
                wait(act, F3, "squared", it)
                act.activation(hid[:, k, :], sg[:, k, :], ACT.Identity, bias=col["act_sb"][:, 1:2],
                               scale=col["act_sb"][:, 0:1]).then_inc(E[F3]["biased"].sem, 1)
                wait(act, F3, "rh", it.back(2))
                wait(act, F3, "biased", it)
                act.activation(sg[:, k, :], hid[:, k, :], ACT.Square, accum_out=hs[:, k, 0:1]
                               ).then_inc(E[F3]["sumsq"].sem, 1)

            def gelu2(it):
                wait(act, F2, "up", it)
                act.activation(hid[:, it.k, :], bank[bank_of_up[F2]][:, :], ACT.Gelu).then_inc(E[F2]["gelu"].sem, 1)

            def hT_sb2(it):
                wait(act, F2, "ht", it)
                evac(hid2[:, it.k, :], bank[bank_of_ht[F2]][:, :], F2, "ht_sb")

            def gelu_e(it, tc):
                for ht in range(FT):
                    wait(act, MOE, "h", it, 4 * tc + ht + 1)
                    act.activation(hT[:, tc, ht, :], bank[ht][:, :], ACT.Gelu_apprx_tanh,
                                   bias=expert[:, it.k, F + ht:F + ht + 1]).then_inc(E[MOE]["gelu"].sem, 1)

            def kv_sb(n, c):
                kT, va = ((kT_1, va_1), (kT_3, va_3))[n]
                kw = dict(bias=col["bk_3"]) if n else {}
                half = slice(4 * (c % 2), 4 * (c % 2) + 4)
                act.wait_ge(kv_pe, 4 * n + c + 1)
                if c < 2:
                    act.activation(kT[:, half, :].rearrange("p b t -> p (b t)"), bank[c][:, :],
                                   ACT.Identity if kw else ACT.Copy, **kw).then_inc(kv_act, 1)
                else:
                    act.activation(va[:, half, :, 0:DK], bank[c][:, :].rearrange("p (b h n) -> p b h n", b=4, h=H),
                                   ACT.Copy).then_inc(kv_act, 1)

            def kv3_sb(it, c):
                if it.rep == 0:
                    kv_sb(1, c)

            def prepare():
                act.wait_ge(loaded[0], 16)
                act.activation(tanh_g[:, :], col["gates"], ACT.Tanh).then_inc(gates_ready, 1)
                for c in range(4):
                    kv_sb(0, c)

            def route_exp():
                act.wait_ge(E[ROUTE]["lg"].sem, E[ROUTE]["lg"].at(Item(B - 1, B - 1)))
                act.activation(pr[:, :, :], lg[:, :, :], ACT.Exp).then_inc(route_act, 1)

            def route_wT():
                act.wait_ge(route_pe, 2)
                act.activation(w_tokT[:, :], bank[R_BANK[1]][0:B * NE, 0:P], ACT.Copy).then_inc(route_act, 1)

            def attention(layer):
                return [
                    [(2, exps, layer, 3), (2, probsT_sb, layer, 2)],
                    [(3, ot_sb, layer), (1, exps, layer, 0), (2, probsT_sb, layer, 3)],
                    [(1, exps, layer, 1), (1, probsT_sb, layer, 0), (0, xt_sb, layer)],
                    [(1, exps, layer, 2), (1, probsT_sb, layer, 1), (0, q_sb, layer)]]

            stages = {
                A0: [[(2, exps, A0, 3), (2, probsT_sb, A0, 2), (0, k_sb, 0), (0, kv3_sb, 0)],
                     [(1, exps, A0, 0), (2, probsT_sb, A0, 3), (0, k_sb, 1), (0, kv3_sb, 1)],
                     [(0, xt_sb, A0), (1, exps, A0, 1), (1, probsT_sb, A0, 0), (0, q_sb0, 0), (0, kv3_sb, 2)],
                     [(1, exps, A0, 2), (1, probsT_sb, A0, 1), (0, q_sb0, 1), (0, kv3_sb, 3)]],
                F0: [[(1, up_sb)], [], [None, None, (0, xq_sb, F0), (1, hq_sb, F0)], [None, (0, half_gate)]],
                A1: attention(A1),
                ROUTE: [[], [], [(0, xt_sb, ROUTE)], []],
                MOE: [[(0, gelu_e, 0), (0, gelu_e, 1)], [], [], []],
                A2: [[(1, xt_sb, A2), (2, exps2)], [], [(3, ot_sb, A2), (2, probsT_sb2)], []],
                F2: [[], [(1, gelu2), (2, hT_sb2)], [], [(0, xt_sb, F2)]],
                A3: attention(A3),
                F3: [[(1, relu3)], [(1, hid3), None, (2, hq_sb, F3)], [], [None, None, (0, xq_sb, F3)]],
            }
            act.wait_ge(prep_dve, 1)
            act.wait_ge(cleared, 6)
            prepare()
            walk(act, PLAN, stages, before={(MOE, 0): route_exp, (MOE, 1): route_wT})

        @block.tensor
        def _(pe):
            def before_in_bank(layer, piece, b):
                mine = bank_of(layer, piece, b)
                here = order.index((layer, piece, b))
                return next((p for p in reversed(order[:here]) if bank_of(*p) == mine), None)

            def claim(it, layer, piece):
                found = before_in_bank(layer, piece, it.rep)
                if found is None:
                    return
                pl, pp, pb = found
                name, j = emptied[pl, pp]
                if pl != layer:
                    wait(pe, pl, name, Item(pb, pb), j)
                    if isinstance(it.b, int):
                        return
                    pl, pp, pb = before_in_bank(layer, piece, it.rep + 2)
                    pb -= 2
                    name, j = emptied[pl, pp]
                    assert pl == layer and E[layer][name].at(Item(pb, pb), j) > 0
                wait(pe, layer, name, Item(it.b + (pb - it.rep), pb), j)

            def bank_of(layer, piece, b):
                k = b % 2
                if layer == MOE:
                    return int(piece[2]) if piece[0] == "h" else O_BANK[int(piece[1])]
                if layer in (A0, A1, A3):
                    if piece[0] == "s":
                        return S_BANK[int(piece[1]) % 2]
                    if piece[0] == "t":
                        return T_BANK[int(piece[1]) % 2]
                    if piece.startswith("pv"):
                        return O_BANK[int(piece[2]) % 2 if layer == A0 else k]
                    return R_BANK[{"xt": 0, "k0": 0, "k1": 0, "q0": 1, "q1": 1, "v0": 0, "v1": 0, "ot0": 1, "ot1": 1,
                                   "y": 1, "q": 1, "ot": 0}[piece]]
                if layer == A2:
                    return {"xt": 6, "ot": 6, "y": 7, "s": S_BANK[k], "t": O_BANK[1 - k], "pv": O_BANK[k]}[piece]
                if layer == ROUTE:
                    return {"xt": R_BANK[0], "lg": T_BANK[1]}[piece]
                return {"xt": R_BANK[0], "gate": T_BANK[0], "up": bank_of_up[layer], "ht": bank_of_ht[layer],
                        "y": bank_of_y[layer]}[piece]

            def xt(it, layer):
                wait(pe, layer, "ln" if layer not in (F0, F3) else "quant", it)
                claim(it, layer, "xt")
                src = xm if layer in (F0, F3) else xn[SIDE[layer]]
                pe.transpose(bank[R_BANK[0]][:, 0:P], src[:, it.k, :], ident).then_inc(E[layer]["xt"].sem, 1)

            def scores(it, layer, g):
                claim(it, layer, f"s{g}")
                out = bank[S_BANK[g % 2]]
                neg = {A0: neg0, A1: neg1, A3: None}[layer]
                if neg is not None:
                    if g == 0 and it.rep == 0:
                        if layer == A0:
                            pe.wait_ge(prep_dve, 2)
                        pe.wait_ge(pool_const, 2 if layer == A0 else 5)
                    pe.matmul(out[:, :].rearrange("p (h t) -> p h t", h=GH), identb[:, :],
                              neg[:, bass.ds(it.b, 1), :].to_broadcast([P, GH, P]), start=True, stop=False)
                if layer == A0:
                    wait(pe, A0, "q_sb", it, 1 + g // 2)
                    wait(pe, A0, "k_sb", it, 2 + 2 * (g // 2))
                    for c in range(2):
                        t = 2 * g + c
                        mm_ = pe.matmul(out[:, 256 * c:256 * c + 256], qT[:, it.k, P * t:P * t + P],
                                        kz[:, it.k, 256 * t:256 * t + 256], start=False, stop=(c == 1))
                else:
                    wait(pe, layer, "q_sb", it)
                    wait(pe, layer, "kz", it, 1 + g // 2)
                    mm_ = pe.matmul(out[:, :], qT[:, it.k, 0:P], kz[:, it.k, 512 * g:512 * g + 512],
                                    start=neg is None, stop=True)
                mm_.then_inc(E[layer]["scores"].sem, 1)

            def probsT(it, layer, g):
                wait(pe, layer, "probs", it, g + 1)
                claim(it, layer, f"t{g}")
                for j in range(GH):
                    mm_ = pe.transpose(bank[T_BANK[g % 2]][:, P * j:P * j + P], prob[:, g % 2, P * j:P * j + P], ident)
                mm_.then_inc(E[layer]["probsT"].sem, 1)

            def pv(it, layer, g):
                wait(pe, layer, "probsT_sb", it, g + 1)
                if layer == A0:
                    wait(pe, A0, "v_sb", it, 1 + g // 2)
                    claim(it, layer, f"pv{g}")
                elif g == 0:
                    claim(it, layer, "pv0")
                for j in range(GH):
                    h = GH * g + j
                    if layer == A0:
                        mm_ = pe.matmul(bank[O_BANK[g % 2]][:, VW0 * j:VW0 * j + VW0], probT[:, g % 2, P * j:P * j + P],
                                        va0[:, it.k, h, :], start=True, stop=True)
                    else:
                        va = va_1 if layer == A1 else va_3
                        mm_ = pe.matmul(bank[O_BANK[it.k]][:, VW * h:VW * h + VW], probT[:, g % 2, P * j:P * j + P],
                                        va[:, bass.ds(it.b, 1), h, :], start=True, stop=True)
                mm_.then_inc(E[layer]["pv"].sem, 1)

            def proj0(it, which, c):
                piece = f"{which}{c}"
                if which == "q" and c == 0:
                    wait(pe, A0, "xt_sb", it)
                claim(it, A0, piece)
                out = bank[bank_of(A0, piece, it.rep)]
                if which == "v":
                    mm_ = pe.matmul(out[:, :], ctxT[:, it.b, :], col["wvT_0"][:, 512 * c:512 * c + 512], start=True, stop=True)
                else:
                    w = col["wkT_0" if which == "k" else "wqT_0"]
                    for t in range(4):
                        rhs = ctxT[:, bass.ds(it.b, 1), :] if which == "k" else xnT[0][:, it.k:it.k + 1, :]
                        mm_ = pe.matmul(out[:, P * t:P * t + P].rearrange("p (a n) -> p a n", a=1),
                                        w[:, 512 * c + P * t:512 * c + P * t + P], rhs, start=True, stop=True)
                mm_.then_inc(E[A0][which + "ps"].sem, 1)

            def ot0(it, c):
                wait(pe, A0, "norm", it, 4 * c + 4)
                piece = f"ot{c}"
                claim(it, A0, piece)
                out = bank[bank_of(A0, piece, it.rep)]
                for t in range(4):
                    mm_ = pe.transpose(out[:, P * t:P * t + P], o_n[:, it.k, 512 * c + P * t:512 * c + P * t + P], ident)
                mm_.then_inc(E[A0]["ot"].sem, 1)

            def y0(it):
                wait(pe, A0, "ot_sb", it)
                claim(it, A0, "y")
                out = bank[R_BANK[1]][:, 0:P]
                for t in range(8):
                    mm_ = pe.matmul(out, oT[:, it.k, P * t:P * t + P], col["woT_0"][:, P * t:P * t + P],
                                    start=(t == 0), stop=(t == 7))
                mm_.then_inc(E[A0]["y"].sem, 1)

            def q(it, layer):
                wait(pe, layer, "xt_sb", it)
                claim(it, layer, "q")
                pe.matmul(bank[R_BANK[1]][:, 0:P], col["wqT_1" if layer == A1 else "wqT_3"], xnT[0][:, it.k, :],
                          start=True, stop=True).then_inc(E[layer]["q"].sem, 1)

            def ot(it, layer):
                wait(pe, layer, "norm", it)
                claim(it, layer, "ot")
                pe.transpose(bank[R_BANK[0]][:, 0:P], o_n[:, it.k, 0:P], ident).then_inc(E[layer]["ot"].sem, 1)

            def y(it, layer):
                n = {A1: 1, A2: 2, A3: 3}[layer]
                claim(it, layer, "y")
                out = bank[R_BANK[1]][:, 0:P]
                pe.matmul(out, ones[0:1, :], row[f"bo_{n}"], start=True, stop=False)
                wait(pe, layer, "ot_sb", it)
                pe.matmul(out, oT[:, it.k, 0:P], col[f"woT_{n}"], start=False, stop=True).then_inc(E[layer]["y"].sem, 1)

            def scores2(it):
                wait(pe, A2, "xt_sb", it)
                claim(it, A2, "s")
                if it.rep == 0:
                    pe.wait_ge(pool_const, 7 + B)
                out = bank[S_BANK[it.k]][:, 0:P].rearrange("p (a n) -> p a n", a=1)
                pe.matmul(out, identb[:, :], neg2[:, bass.ds(it.b, 1), :], start=True, stop=False)
                pe.matmul(out, xnT[0][:, it.k, :], ctxT[:, bass.ds(it.b, 1), :], start=False, stop=True
                          ).then_inc(E[A2]["scores"].sem, 1)

            def probsT2(it):
                wait(pe, A2, "probs", it)
                claim(it, A2, "t")
                pe.transpose(bank[O_BANK[1 - it.k]][:, 0:P], prob[:, it.k, 0:P], ident).then_inc(E[A2]["probsT"].sem, 1)

            def pv2(it):
                wait(pe, A2, "probsT_sb", it)
                claim(it, A2, "pv")
                pe.matmul(bank[O_BANK[it.k]][:, 0:P].rearrange("p (a n) -> p a n", a=1), probT[:, it.k, 0:P],
                          ctx_tok[:, bass.ds(it.b, 1), :], start=True, stop=True).then_inc(E[A2]["pv"].sem, 1)

            def up(it, layer, piece, w, lhs):
                wait(pe, layer, "xt_sb", it)
                claim(it, layer, piece)
                pe.matmul(bank[bank_of(layer, piece, it.rep)][:, :], lhs[:, it.k, :], w, start=True, stop=True
                          ).then_inc(E[layer][piece].sem, 1)

            def ht(it, layer):
                src = hid2 if layer != F2 else hid
                if layer == F3:
                    wait(pe, layer, "hq", it)
                else:
                    wait(pe, layer, "hid", it)
                claim(it, layer, "ht")
                for t in range(FT):
                    mm_ = pe.transpose(bank[bank_of_ht[layer]][:, P * t:P * t + P], src[:, it.k, P * t:P * t + P], ident)
                mm_.then_inc(E[layer]["ht"].sem, 1)

            def y_ffn(it, layer, w):
                wait(pe, layer, "ht_sb", it)
                claim(it, layer, "y")
                out = bank[bank_of(layer, "y", it.rep)][:, 0:P]
                if layer == F2:
                    pe.matmul(out, ones[0:1, :], crow[:, :], start=True, stop=False)
                src = hid2 if layer == F2 else hqT
                for t in range(FT):
                    mm_ = pe.matmul(out, src[:, it.k, P * t:P * t + P], w[:, P * t:P * t + P],
                                    start=(t == 0 and layer != F2), stop=(t == FT - 1))
                mm_.then_inc(E[layer]["y"].sem, 1)

            def logits(it):
                wait(pe, ROUTE, "xt_sb", it)
                claim(it, ROUTE, "lg")
                pe.matmul(bank[T_BANK[1]][:, 0:NE], xnT[1][:, it.k, :], col["wg"], start=True, stop=True
                          ).then_inc(E[ROUTE]["logits"].sem, 1)

            def hidden(it, piece):
                tc, t = int(piece[1]), int(piece[2])
                claim(it, MOE, piece)
                if piece == "h00":
                    pe.wait_ge(expert_loaded[it.k], 8 * it.b + 16 - 8 * it.k)
                pe.matmul(bank[t][:, :], expert[:, it.k, P * t:P * t + P],
                          xnT_all[:, 4 * tc:4 * tc + 4, :].rearrange("p b t -> p (b t)"), start=True, stop=True
                          ).then_inc(E[MOE]["h"].sem, 1)

            def down(it, piece):
                tc = int(piece[1])
                claim(it, MOE, piece)
                wait(pe, MOE, "gelu", it, 4 * tc + 4)
                for tt in range(4):
                    for t in range(FT):
                        mm_ = pe.matmul(bank[O_BANK[tc]][:, P * tt:P * tt + P], hT[:, tc, t, P * tt:P * tt + P],
                                        expert[:, it.k, F + FT + P * t:F + FT + P * t + P],
                                        start=(t == 0), stop=(t == FT - 1))
                mm_.then_inc(E[MOE]["y"].sem, 1)

            def kv(n, c):
                first = 4 * (c % 2)
                out = bank[c]
                if c < 2:
                    mm_ = pe.matmul(out[:, :], col["wkT_3" if n else "wkT_1"],
                                    ctxT[:, first:first + 4, :].rearrange("p b t -> p (b t)"), start=True, stop=True)
                else:
                    if n:
                        pe.matmul(out[:, :].rearrange("p (b n) -> p b n", b=4), ones[0:1, :],
                                  row["bv_3"].rearrange("p (a n) -> p a n", a=1).to_broadcast([1, 4, P]), start=True, stop=False)
                    for b in range(4):
                        mm_ = pe.matmul(out[:, P * b:P * b + P], ctxT[:, first + b, :], col["wvT_13"][:, P * n:P * n + P],
                                        start=not n, stop=(not n or b == 3))
                mm_.then_inc(kv_pe, 1)

            def kv3(it, c):
                if it.rep == 0:
                    pe.wait_ge(kv_act, c + 1)
                    if c == 2:
                        pe.wait_ge(rows_loaded, 16)
                    kv(1, c)

            def prepare():
                pe.wait_ge(loaded[0], 16)
                for c in range(4):
                    kv(0, c)
                pe.wait_ge(loaded[1], 16)

            def banks_free():
                pe.wait_ge(kv_act, 8)

            def weight_sums():
                pe.wait_ge(wsum_dve, len(TERNARY))
                wait(pe, A0, "v_sb", Item(2, 2))
                pe.matmul(bank[R_BANK[0]][:, 0:len(TERNARY)], ones, asum[:, :], start=True, stop=True).then_inc(wsum_pe, 1)
                pe.wait_ge(wsum_dve, len(TERNARY) + 1)

            def route_places(it):
                if it.rep:
                    return
                pe.wait_ge(route_dve, RT_CHOSEN)
                out = bank[R_BANK[0]][:, 0:B * NE]
                pe.matmul(out, utrib[:, :], chosen[:, :, :].rearrange("p b e -> p (b e)"), start=True, stop=False)
                pe.matmul(out, onesb[:, :], before_b[:, :, :].rearrange("p b e -> p (b e)"), start=False, stop=True
                          ).then_inc(route_pe, 1)

            def route_bias():
                pe.wait_ge(route_dve, RT_WEIGHTS)
                pe.transpose(bank[R_BANK[1]][0:B * NE, 0:P], w_tok[:, :, :].rearrange("p b e -> p (b e)"), ident
                             ).then_inc(route_pe, 1)
                pe.wait_ge(route_act, 2)
                pe.wait_ge(b2_loaded, 16)
                for c in range(2):
                    pe.matmul(bank[R_BANK[c]][:, :], w_tokT[:, :], b2blk[:, 512 * c:512 * c + 512], start=True, stop=True
                              ).then_inc(route_pe, 1)

            def moe_ready():
                wait(pe, ROUTE, "copied", Item(B - 1, B - 1))

            def fold():
                pe.wait_ge(tern_dve, 3 * len(TERNARY))
                pe.wait_ge(route_dve, RT_BIAS)
                for t in range(FT):
                    mm_ = pe.matmul(bank[R_BANK[1]][0:1, 0:P], col["lnb_2"][:, t:t + 1], tern["projT"][:, P * t:P * t + P],
                                    start=(t == 0), stop=(t == FT - 1))
                mm_.then_inc(fold_pe, 1)

            def attention(layer):
                return [
                    [(1, scores, layer, 0), (2, probsT, layer, 2), (2, pv, layer, 1), (3, ot, layer)],
                    [(1, scores, layer, 1), (2, probsT, layer, 3), (2, pv, layer, 2), (3, y, layer)],
                    [(1, scores, layer, 2), (1, probsT, layer, 0), (2, pv, layer, 3), (0, xt, layer)],
                    [(1, scores, layer, 3), (1, probsT, layer, 1), (0, q, layer), (1, pv, layer, 0)]]

            stages = {
                A0: [[(1, scores, A0, 0), (2, probsT, A0, 2), (3, ot0, 1), (2, pv, A0, 1), (0, proj0, "k", 0), (0, kv3, 0)],
                     [(1, scores, A0, 1), (2, probsT, A0, 3), (0, proj0, "k", 1), (3, y0), (2, pv, A0, 2), (0, xt, A0),
                      (2, ot0, 0), (0, kv3, 1)],
                     [(1, scores, A0, 2), (1, probsT, A0, 0), (0, proj0, "v", 0), (0, proj0, "q", 0), (2, pv, A0, 3), (0, kv3, 2)],
                     [(1, scores, A0, 3), (1, probsT, A0, 1), (0, proj0, "v", 1), (0, proj0, "q", 1), (1, pv, A0, 0), (0, kv3, 3)]],
                F0: [[(2, y_ffn, F0, tern["downT"]), (1, up, F0, "up", tern["upT"][:, :], xqT)], [],
                     [None, None, (0, xt, F0), (1, ht, F0)],
                     [None, (0, up, F0, "gate", tern["gateT"][:, :], xqT)]],
                A1: attention(A1),
                ROUTE: [[(1, logits)], [], [(0, xt, ROUTE)], []],
                MOE: [[(0, hidden, "h00"), (0, hidden, "h01"), (0, hidden, "h02"), (0, hidden, "h03"), (1, down, "y1"),
                       (0, hidden, "h10"), (0, hidden, "h11"), (0, hidden, "h12"), (0, hidden, "h13"),
                       (0, route_places), (0, down, "y0")], [], [], []],
                A2: [[(1, xt, A2)], [(3, ot, A2), (2, probsT2)], [(1, scores2)], [(2, pv2), (3, y, A2)]],
                F2: [[(1, up, F2, "up", tern["fcT"][:, :], xnT[1])], [(2, ht, F2)], [None, None, (2, y_ffn, F2, projw)], [(0, xt, F2)]],
                A3: attention(A3),
                F3: [[(1, up, F3, "up", tern["w1T"][:, :], xqT)], [None, None, (2, ht, F3)], [None, None, (2, y_ffn, F3, tern["w2T"])],
                     [None, None, (0, xt, F3)]],
            }

            def piece_name(layer, fn, args):
                if fn is xt:
                    return "xt"
                if fn in (scores, probsT, pv):
                    return {scores: "s", probsT: "t", pv: "pv"}[fn] + str(args[1])
                if fn is proj0:
                    return args[0] + str(args[1])
                if fn is ot0:
                    return f"ot{args[0]}"
                if fn is up:
                    return args[1]
                if fn in (hidden, down):
                    return args[0]
                return {y0: "y", q: "q", ot: "ot", y: "y", scores2: "s", probsT2: "t", pv2: "pv", ht: "ht",
                        y_ffn: "y", logits: "lg"}[fn]

            order = []

            def note(layer, fn, it, *args):
                if fn not in (route_places, kv3):
                    order.append((layer, piece_name(layer, fn, (it, *args)[1:]), it.rep))

            walk(None, PLAN, stages, run=note)

            def ternary_ready(n):
                return lambda: pe.wait_ge(tern_dve, 3 * n)

            prepare()
            walk(pe, PLAN, stages,
                 before={(A0, 3): weight_sums, (F0, 0): ternary_ready(3), (MOE, 0): moe_ready, (MOE, 1): route_bias,
                         (A0, 1): banks_free, (A2, 0): fold,
                         (F2, 0): lambda: pe.wait_ge(fold_dve, FT + 1)})

        @block.vector
        def _(dve):
            def chain(layer, name, it, start=0):
                ev = E[layer][name]
                count = [start]

                def do(ins, hold=True):
                    ins.then_inc(ev.sem, 1)
                    count[0] += 1
                    yield
                    if hold:
                        dve.wait_ge(ev.sem, ev.at(it, count[0]))
                return do

            def xs(it):
                return x_sb[:, bass.ds(it.b, 1), :]

            PREVIOUS = {A1: A0, ROUTE: F0, A2: A1, F2: ROUTE, A3: A2, F3: F2}
            BEFORE = {F0: A0, A1: F0, ROUTE: A1, A2: ROUTE, F2: A2, A3: F2, F3: A3}

            def ln_stats(it, layer):
                if layer == A0:
                    if it.rep == 0:
                        dve.wait_ge(loaded[5], 16)
                elif layer == A2:
                    wait(dve, MOE, "acc", Item(NE - 1, NE - 1), 4 if it.rep < 4 else 8)
                else:
                    wait(dve, BEFORE[layer], "resid", it)
                do = chain(layer, "ln", it)
                z = SIDE[layer]
                yield from do(dve.bn_stats(stats[z][:, it.k, :], xs(it)))
                yield from do(dve.bn_aggr(mv[z][:, it.k, :], stats[z][:, it.k, :]), hold=False)

            def ln(it, layer):
                k = it.k
                wait(dve, layer, "rs", it)
                if it.rep >= 2:
                    wait(dve, layer, "xt", it.back(2))
                elif layer in PREVIOUS:
                    last = Item(B - 2 + k, B - 2 + k)
                    wait(dve, PREVIOUS[layer], "xt", last)
                do = chain(layer, "ln", it, 2)
                z = SIDE[layer]
                yield from do(dve.tensor_scalar(xn[z][:, k:k + 1, :], xs(it), mv[z][:, k, 0:1], rstd[z][:, k, 0:1], ALU.subtract, ALU.mult),
                   hold=layer in (F0, F3))

            def resid(it, layer):
                n = {A0: 0, A1: 1, A2: 2, A3: 3, F2: 6}[layer]
                wait(dve, layer, "y", it)
                out = bank[bank_of_y.get(layer, R_BANK[1])][:, 0:P].rearrange("p (a n) -> p a n", a=1)
                dve.scalar_tensor_tensor(xs(it), out, tanh_g[:, n:n + 1], xs(it), ALU.mult, ALU.add
                                         ).then_inc(E[layer]["resid"].sem, 1)

            def resid_q(it, layer):
                wait(dve, layer, "y", it)
                scale = hs[:, it.k, 7:8]
                out = bank[bank_of_y[layer]][:, 0:P].rearrange("p (a n) -> p a n", a=1)
                dve.scalar_tensor_tensor(xs(it), out, scale, xs(it), ALU.mult, ALU.add).then_inc(E[layer]["resid"].sem, 1)

            def shifted(it, layer, g):
                src = bank[S_BANK[g % 2]][:, :].rearrange("p (h t) -> p h t", h=GH)
                m = mx[:, g % 2, :]
                wait(dve, layer, "scores", it, g + 1)
                do = chain(layer, "shifted", it, 2 * g)
                yield from do(dve.tensor_reduce(m, src, AX.X, ALU.max))
                if g >= 2 or it.rep >= 1:
                    wait(dve, layer, "probsT", it, g - 1)
                elif layer == A3:
                    wait(dve, A2, "probsT", Item(B - 2 + g, B - 2 + g))
                yield from do(dve.tensor_tensor(prob[:, g % 2, :].rearrange("p (h t) -> p h t", h=GH), src,
                                     m.rearrange("p (h a) -> p h a", a=1).to_broadcast([P, GH, P]), ALU.subtract),
                   hold=False)

            def v_sb(it, c):
                wait(dve, A0, "vps", it, c + 1)
                wait(dve, A0, "pv", it.back(2), 2 * c + 2)
                dve.tensor_copy(va0[:, it.k, 8 * c:8 * c + 8, 0:DK0], bank[R_BANK[0]][:, :].rearrange(
                    "p (h n) -> p h n", h=8)).then_inc(E[A0]["v_sb"].sem, 1)

            def ot_sb0(it, c):
                wait(dve, A0, "ot", it, c + 1)
                if c == 0:
                    wait(dve, A0, "y", it.back(2))
                dve.tensor_copy(oT[:, it.k, 512 * c:512 * c + 512], bank[R_BANK[1]][:, :]).then_inc(E[A0]["ot_sb"].sem, 1)

            def norm0(it, g):
                src = bank[O_BANK[g % 2]][:, 0:GH * VW0].rearrange("p (h n) -> p h n", h=GH)
                wait(dve, A0, "pv", it, g + 1)
                do = chain(A0, "norm", it, 2 * g)
                r = rden[:, it.k, GH * g:GH * g + GH].rearrange("p (h a) -> p h a", a=1)
                yield from do(dve.reciprocal(r, src[:, :, DK0:VW0]))
                if g == 0:
                    wait(dve, A0, "ot", it.back(2))
                yield from do(dve.tensor_tensor(o_n[:, it.k, 256 * g:256 * g + 256].rearrange("p (h n) -> p h n", h=GH),
                                     src[:, :, 0:DK0], r.to_broadcast([P, GH, DK0]), ALU.mult), hold=False)

            def norm(it, layer):
                src = bank[O_BANK[it.k]][:, 0:H * VW].rearrange("p (h n) -> p h n", h=H)
                wait(dve, layer, "pv", it)
                do = chain(layer, "norm", it)
                r = rden[:, it.k, :].rearrange("p (h a) -> p h a", a=1)
                yield from do(dve.reciprocal(r, src[:, :, DK:VW]))
                wait(dve, layer, "ot", it.back(2))
                yield from do(dve.tensor_tensor(o_n[:, it.k, 0:P].rearrange("p (h n) -> p h n", h=H), src[:, :, 0:DK],
                                     r.to_broadcast([P, H, DK]), ALU.mult), hold=False)

            def shift2(it):
                wait(dve, A2, "scores", it)
                wait(dve, A2, "probs", it.back(2))
                do = chain(A2, "shift", it)
                yield from do(dve.tensor_reduce(mx[:, it.k, 0:1], bank[S_BANK[it.k]][:, 0:P], AX.X, ALU.max))
                yield from do(dve.tensor_scalar(mx[:, it.k, 1:2], mx[:, it.k, 0:1], -float(P) ** -0.5, None, ALU.mult), hold=False)

            def norm2(it):
                wait(dve, A2, "pv", it)
                wait(dve, A2, "probs", it)
                do = chain(A2, "norm", it)
                yield from do(dve.reciprocal(rden[:, it.k, 0:1], rden[:, it.k, 1:2]))
                wait(dve, A2, "ot", it.back(2))
                yield from do(dve.tensor_scalar(o_n[:, it.k, 0:P], bank[O_BANK[it.k]][:, 0:P], rden[:, it.k, 0:1], None, ALU.mult),
                   hold=False)

            def quant0(it):
                k = it.k
                if it.rep == 0:
                    dve.wait_ge(wsum_dve, RED_DONE)
                do = chain(F0, "quant", it)
                wait(dve, F0, "up_sb", it.back(2))
                yield from do(dve.tensor_reduce(qs[:, k, 0:1], xn[1][:, k, :], AX.X, ALU.max, apply_absolute_value=True))
                yield from do(dve.tensor_scalar(qs[:, k, 1:2], qs[:, k, 0:1], 1e-5, 1.0 / 127.0, ALU.max, ALU.mult))
                yield from do(dve.reciprocal(qs[:, k, 2:3], qs[:, k, 1:2]))
                yield from do(dve.tensor_scalar(qs[:, k, 3:5], wmean[:, 0:2], qs[:, k, 1:2], None, ALU.mult))
                wait(dve, F0, "xt", it.back(2))
                yield from do(dve.tensor_scalar(xm[:, k, :], xn[1][:, k, :], qs[:, k, 2:3], MAGIC, ALU.mult, ALU.add))

            def hid0(it):
                k = it.k
                wait(dve, F0, "up_sb", it)
                do = chain(F0, "hid", it)
                yield from do(dve.scalar_tensor_tensor(hid[:, k, :], sg[:, k, :], 1.0, hid[:, k, :], ALU.add, ALU.mult))
                yield from do(dve.tensor_tensor(hid[:, k, :], hid[:, k, :], hid2[:, k, :], ALU.mult))
                yield from do(dve.tensor_reduce(hs[:, k, 0:1], hid[:, k, :], AX.X, ALU.max, apply_absolute_value=True))
                yield from do(dve.tensor_scalar(hs[:, k, 1:2], hs[:, k, 0:1], 1e-5, 1.0 / 127.0, ALU.max, ALU.mult))
                yield from do(dve.reciprocal(hs[:, k, 2:3], hs[:, k, 1:2]))
                yield from do(dve.tensor_scalar(hs[:, k, 7:8], hs[:, k, 1:2], wmean[:, 2:3], tanh_g[:, 4:5], ALU.mult, ALU.mult))
                yield from do(dve.tensor_scalar(hid2[:, k, :], hid[:, k, :], hs[:, k, 2:3], MAGIC, ALU.mult, ALU.add))

            def rms_quant(do, v, wm, xw):
                yield from do(dve.tensor_scalar(v[:, 5:6], v[:, 1:2], v[:, 4:5], 1e-5, ALU.mult, ALU.max))
                yield from do(dve.reciprocal(v[:, 6:7], v[:, 5:6]))
                yield from do(dve.tensor_scalar(v[:, 6:7], v[:, 6:7], v[:, 4:5], 127.0, ALU.mult, ALU.mult))
                yield from do(dve.tensor_scalar(v[:, 3:4], v[:, 5:6], wm, 1.0 / 127.0, ALU.mult, ALU.mult))
                yield from do(dve.tensor_scalar(xw, xw, v[:, 6:7], MAGIC, ALU.mult, ALU.add))

            def quant3(it):
                k = it.k
                do = chain(F3, "quant", it)
                wait(dve, F3, "xt", it.back(2))
                wait(dve, F3, "relu", it.back(2))
                yield from do(dve.tensor_tensor_reduce(xm[:, k, :], xn[1][:, k, :], xn[1][:, k, :], 1.0, 0.0, ALU.mult, ALU.add, qs[:, k, 0:1]))
                yield from do(dve.tensor_tensor(xm[:, k, :], xn[1][:, k, :], col["nw1"], ALU.mult))
                yield from do(dve.tensor_reduce(qs[:, k, 1:2], xm[:, k, :], AX.X, ALU.max, apply_absolute_value=True))

            def scale3(it):
                do = chain(F3, "quant", it, 3)
                k = it.k
                wait(dve, F3, "rq", it)
                yield from rms_quant(do, qs[:, k, :], wmean[:, 5:6], xm[:, k, :])

            def ln_quant(it, layer):
                yield from ln(it, layer)
                yield from (quant0 if layer == F0 else quant3)(it)

            def hq3(it):
                k = it.k
                do = chain(F3, "hq", it)
                wait(dve, F3, "hw", it)
                yield from do(dve.tensor_reduce(hs[:, k, 1:2], hid2[:, k, :], AX.X, ALU.max, apply_absolute_value=True))
                wait(dve, F3, "rh", it)
                yield from rms_quant(do, hs[:, k, :], wmean[:, 6:7], hid2[:, k, :])
                yield from do(dve.tensor_scalar(hs[:, k, 7:8], hs[:, k, 3:4], tanh_g[:, 7:8], None, ALU.mult))

            def hid2_stats(it):
                k = it.k
                wait(dve, F2, "gelu", it)
                do = chain(F2, "hid", it)
                yield from do(dve.bn_stats(stats_h[:, k, :], hid[:, k, :]))
                yield from do(dve.bn_aggr(mv_h[:, k, :], stats_h[:, k, :]), hold=False)

            def hid2_ln(it):
                k = it.k
                do = chain(F2, "hid", it, 2)
                wait(dve, F2, "rs_hid", it)
                yield from do(dve.tensor_scalar(hid[:, k, :], hid[:, k, :], mv_h[:, k, 0:1], rstd[1][:, k, 1:2], ALU.subtract, ALU.mult),
                   hold=False)

            def lg_sb(it):
                wait(dve, ROUTE, "logits", it)
                do = chain(ROUTE, "lg", it)
                src = bank[T_BANK[1]][:, 0:NE].rearrange("p (a n) -> p a n", a=1)
                yield from do(dve.tensor_reduce(lg_max[:, it.k:it.k + 1], src, AX.X, ALU.max))
                yield from do(dve.tensor_scalar(lg[:, bass.ds(it.b, 1), :], src, lg_max[:, it.k:it.k + 1], None, ALU.subtract))

            def acc(it, tc):
                wait(dve, MOE, "y", it, tc + 1)
                wait(dve, MOE, "acc", it.back(1), 4 * tc + 4)
                for tt in range(4):
                    b = 4 * tc + tt
                    dve.scalar_tensor_tensor(x_sb[:, b, :], bank[O_BANK[tc]][:, P * tt:P * tt + P],
                                             w_tok[:, b, bass.ds(it.b, 1)], x_sb[:, b, :], ALU.mult, ALU.add
                                             ).then_inc(E[MOE]["acc"].sem, 1)

            class Count:

                def __init__(self, s):
                    self.s, self.n = s, 0

                def do(self, ins, hold=True):
                    ins.then_inc(self.s, 1)
                    self.n += 1
                    if hold:
                        dve.wait_ge(self.s, self.n)

            rt = Count(route_dve)

            def route():
                def bc(ap):
                    return ap.rearrange("p (b a) -> p b a", a=1).to_broadcast([P, B, NE])

                dve.wait_ge(route_act, 1)
                rt.do(dve.tensor_reduce(psum_r[:, :], pr[:, :, :], AX.X, ALU.add))
                rt.do(dve.reciprocal(psum_r[:, :], psum_r[:, :]))
                rt.do(dve.tensor_tensor(pr[:, :, :], pr[:, :, :], bc(psum_r[:, :]), ALU.mult))
                for b in range(B):
                    rt.do(dve.max(top[:, b, :], pr[:, b, :]), hold=(b == B - 1))
                for b in range(B):
                    rt.do(dve.max_index(topi[:, b, :], top[:, b, :], pr[:, b, :]), hold=(b == B - 1))
                rt.do(dve.tensor_copy(topf[:, :, :], topi[:, :, :]), hold=False)
                rt.do(dve.tensor_tensor(gsum[:, :], top[:, :, 0], top[:, :, 1], ALU.add))
                rt.do(dve.reciprocal(gsum[:, :], gsum[:, :]), hold=False)
                eiota = col["eiota"].rearrange("p (a e) -> p a e", a=1).to_broadcast([P, B, NE])
                rt.do(dve.tensor_tensor(oh1[:, :, :], eiota, topf[:, :, 0:1].to_broadcast([P, B, NE]), ALU.is_equal), hold=False)
                rt.do(dve.tensor_tensor(oh2[:, :, :], eiota, topf[:, :, 1:2].to_broadcast([P, B, NE]), ALU.is_equal))
                rt.do(dve.tensor_tensor(chosen[:, :, :], oh1[:, :, :], oh2[:, :, :], ALU.add), hold=False)
                rt.do(dve.memset(before_b[:, 0, :], 0.0))
                for b in range(1, B):
                    rt.do(dve.tensor_tensor(before_b[:, b, :], before_b[:, b - 1, :], chosen[:, b - 1, :], ALU.add))
                assert rt.n == RT_CHOSEN, rt.n
                rt.do(dve.tensor_tensor(g12[:, :, :], top[:, :, 0:2],
                                        gsum[:, :].rearrange("p (b a) -> p b a", a=1).to_broadcast([P, B, 2]), ALU.mult))
                rt.do(dve.tensor_scalar(g12[:, :, :], g12[:, :, :], tanh_g[:, 5:6], None, ALU.mult))
                rt.do(dve.tensor_tensor(oh1[:, :, :], oh1[:, :, :], g12[:, :, 0:1].to_broadcast([P, B, NE]), ALU.mult), hold=False)
                rt.do(dve.tensor_tensor(oh2[:, :, :], oh2[:, :, :], g12[:, :, 1:2].to_broadcast([P, B, NE]), ALU.mult))
                rt.do(dve.tensor_tensor(w_tok[:, :, :], oh1[:, :, :], oh2[:, :, :], ALU.add))
                dve.wait_ge(route_pe, 1)
                rt.do(dve.tensor_scalar(keep[:, :, :], bank[R_BANK[0]][:, 0:B * NE].rearrange("p (b e) -> p b e", b=B),
                                        float(CAP), None, ALU.is_lt))
                rt.do(dve.tensor_tensor(w_tok[:, :, :], w_tok[:, :, :], keep[:, :, :], ALU.mult))
                assert rt.n == RT_WEIGHTS, rt.n

            def route_bias():
                wait(dve, MOE, "acc", Item(0, 0), 4)
                for c in range(2):
                    dve.wait_ge(route_pe, 3 + c)
                    xc = x_sb[:, 4 * c:4 * c + 4, :]
                    rt.do(dve.tensor_tensor(xc, xc, bank[R_BANK[c]][:, :].rearrange("p (b n) -> p b n", b=4), ALU.add))
                assert rt.n == RT_BIAS, rt.n

            sums, ternary = Count(wsum_dve), Count(tern_dve)

            def weights(it):
                for n in {1: range(0, 4), 2: range(4, 7)}.get(it.rep, ()):
                    dve.wait_ge(loaded[3], 16)
                    sums.do(dve.tensor_reduce(asum[:, n:n + 1], col[TERNARY[n]], AX.X, ALU.add, apply_absolute_value=True),
                            hold=False)
                    yield
                for n in {3: range(0, 3), 4: [3], 5: [4], 6: [5], 7: [6]}.get(it.rep, ()):
                    t = tmp_t[:, n % 2, :]
                    ternary.do(dve.tensor_scalar(t, col[TERNARY[n]], winv[:, n:n + 1], -1.0, ALU.mult, ALU.max), hold=False)
                    yield
                    dve.wait_ge(tern_dve, ternary.n)
                    ternary.do(dve.tensor_scalar(t, t, 1.0, MAGIC, ALU.min, ALU.add), hold=False)
                    yield
                    dve.wait_ge(tern_dve, ternary.n)
                    ternary.do(dve.tensor_scalar(tern[TERNARY[n]][:, :], t, MAGIC, None, ALU.subtract), hold=False)
                    yield

            def means():
                dve.wait_ge(wsum_pe, 1)
                sums.do(dve.tensor_scalar(wmean[:, :], bank[R_BANK[0]][:, 0:len(TERNARY)], 1.0 / (P * F), None, ALU.mult))
                sums.do(dve.tensor_scalar(wmean[:, 0:3], wmean[:, 0:3], 1e-5, None, ALU.max), hold=False)
                sums.do(dve.tensor_scalar(wmean[:, 3:5], wmean[:, 3:5], 1e-6, None, ALU.add), hold=False)
                sums.do(dve.tensor_scalar(wmean[:, 5:7], wmean[:, 5:7], 1e-5, None, ALU.max))
                sums.do(dve.reciprocal(winv[:, :], wmean[:, :]))
                sums.do(dve.tensor_scalar(wmean[:, 0:1], wmean[:, 0:1], 0.5, None, ALU.mult))
                assert sums.n == RED_DONE

            def fold():
                fd = Count(fold_dve)
                dve.wait_ge(tern_dve, 3 * len(TERNARY))
                for t in range(FT):
                    fd.do(dve.tensor_scalar(projw[:, P * t:P * t + P], tern["projT"][:, P * t:P * t + P],
                                            col["lnw_2"][:, t:t + 1], None, ALU.mult), hold=False)
                dve.wait_ge(fold_pe, 1)
                fd.do(dve.tensor_copy(crow[:, :], bank[R_BANK[1]][0:1, 0:P]), hold=False)

            def prepare():
                dve.memset(minus_magic, -MAGIC).then_inc(prep_dve, 1)
                dve.wait_ge(loaded[0], 16)
                dve.wait_ge(mask0_loaded, 16)
                dve.scalar_tensor_tensor(neg0[:, :, :], mask0_u8[:, :, :], NEG,
                                         col["causal"].rearrange("p (a t) -> p a t", a=1).to_broadcast([P, B, P]),
                                         ALU.mult, ALU.min).then_inc(prep_dve, 1)
                dve.wait_ge(cleared, 6)
                dve.wait_ge(gates_ready, 1)

            def attention(layer):
                return [
                    [[(1, shifted, layer, 0), (0, ln_stats, layer)]],
                    [[(1, shifted, layer, 1), (0, ln, layer)], (3, resid, layer)],
                    [(1, shifted, layer, 2)],
                    [[(1, shifted, layer, 3), (2, norm, layer)]]]

            stages = {
                A0: [[[(1, shifted, A0, 0), (0, ln_stats, A0)], (2, norm0, 1), (3, ot_sb0, 1)],
                     [[(1, shifted, A0, 1), (0, ln, A0), (0, weights)], (3, resid, A0), (2, norm0, 2), (2, ot_sb0, 0)],
                     [(1, shifted, A0, 2), (0, v_sb, 0), (2, norm0, 3)],
                     [(1, shifted, A0, 3), (0, v_sb, 1), (1, norm0, 0)]],
                F0: [[(2, resid_q, F0), (0, ln_stats, F0)], [[(1, hid0), (0, ln_quant, F0)]], [], []],
                A1: attention(A1),
                ROUTE: [[(1, lg_sb), (0, ln_stats, ROUTE)], [(0, ln, ROUTE)], [], []],
                MOE: [[(1, acc, 1), (0, acc, 0)], [], [], []],
                A2: [[[(3, norm2), (0, ln_stats, A2)]], [(0, ln, A2)], [], [(1, shift2), (3, resid, A2)]],
                F2: [[(0, ln_stats, F2)], [(0, ln, F2)], [[(1, hid2_stats), (2, resid, F2)]], [(1, hid2_ln)]],
                A3: attention(A3),
                F3: [[(0, ln_stats, F3)], [(0, ln_quant, F3)], [(0, scale3), (2, resid_q, F3)], [(1, hq3)]],
            }
            prepare()
            walk(dve, PLAN, stages, before={(A0, 3): means, (MOE, 0): route, (MOE, 1): route_bias, (A2, 0): fold})


def pack(arrays, pack_):
    import numpy as np
    return np.ascontiguousarray(np.concatenate([arrays[n].reshape(P, w) for n, w in pack_.items()], axis=1))


def kernel(**inputs):
    import numpy as np
    import concourse.bacc as bacc
    from concourse.bass_utils import run_bass_kernel_spmd as run

    a = {k: np.asarray(v) for k, v in inputs.items()}
    f = np.float32
    part = np.arange(P)

    def heads_T(w):
        return w.transpose(2, 0, 1).reshape(P, H * DK0)

    def tiles(w):
        return w.reshape(-1, P, w.shape[1]).transpose(1, 0, 2).reshape(P, -1)

    def everywhere(v):
        return np.broadcast_to(v.reshape(1, -1), (P, v.size))

    cols = dict(
        ctxT=a["ctx_1024"].transpose(2, 0, 1), ctx=a["ctx_1024"].transpose(1, 0, 2), x=a["x"].transpose(1, 0, 2),
        wkT_1=a["L1_xattn_w_k"].T, wkT_3=a["L3_xattn_w_k"].T,
        wvT_13=np.concatenate([a["L1_xattn_w_v"].T, a["L3_xattn_w_v"].T], axis=1),
        ident=np.eye(P, dtype=f), ones=np.ones((P, P), f),
        hmask=(part[:, None] // DK == np.arange(H)[None]).astype(f),
        bk_3=a["L3_xattn_b_k"], bq_3=a["L3_xattn_b_q"],
        gates=everywhere(np.concatenate([a["g_xattn"], a["g_ffn"]])),
        wkT_0=heads_T(a["L0_xattn_Wk"]), wqT_0=heads_T(a["L0_xattn_Wq"]), wvT_0=heads_T(a["L0_xattn_Wv"]),
        woT_0=tiles(a["L0_xattn_Wo"].T),
        causal=np.where(part[None] > part[:, None], f(NEG), f(0)), kiota=everywhere(part.astype(f)),
        utri=(part[:, None] < part[None]).astype(f), eiota=everywhere(np.arange(NE, dtype=f)), piota=part.astype(f),
        act_sb=everywhere(np.concatenate([a["L3_ffn_act_scale"], a["L3_ffn_act_bias"]])),
        lnw_2=a["L2_ffn_ln_w"].reshape(FT, P).T, lnb_2=a["L2_ffn_ln_b"].reshape(FT, P).T, wg=a["L1_ffn_Wg"],
        wqT_1=a["L1_xattn_w_q"].T, woT_1=a["L1_xattn_w_o"].T, wqT_3=a["L3_xattn_w_q"].T, woT_3=a["L3_xattn_w_o"].T,
        woT_2=a["L2_xattn_W"].T,
        gateT=a["L0_ffn_w_gate"].T, upT=a["L0_ffn_w_up"].T, downT=tiles(a["L0_ffn_w_down"].T),
        fcT=a["L2_ffn_W_fc"].T, projT=tiles(a["L2_ffn_W_proj"].T), w1T=a["L3_ffn_w1"].T, w2T=tiles(a["L3_ffn_w2"].T),
        nw1=everywhere(a["L3_ffn_norm1_w"]), nw2=everywhere(a["L3_ffn_norm2_w"]),
    )
    arrays = {f"pack{n}_d": pack(cols, p) for n, p in enumerate(PACKS)}
    row = dict(bv_3=a["L3_xattn_b_v"], bo_1=a["L1_xattn_b_o"], bo_2=a["L2_xattn_b"],
               bo_3=a["L3_xattn_b_o"])
    arrays["rows_d"] = np.concatenate([row[n] for n in ROWS]).reshape(1, -1)
    arrays["mask0_d"] = np.ascontiguousarray(a["mask_BxSxS2_bf0"].transpose(1, 0, 2))
    arrays["mask1_d"] = np.ascontiguousarray(a["mask_BxSxS2_ik0"].transpose(1, 0, 2))
    arrays["lens_d"] = np.ascontiguousarray(everywhere(a["_lenS2"]))
    b2 = np.zeros((B, NE, B, P), f)
    for b in range(B):
        b2[b, :, b, :] = a["L1_ffn_b2"]
    arrays["b2blk_d"] = b2.reshape(B * NE, N)
    arrays["experts_d"] = np.ascontiguousarray(np.concatenate([
        a["L1_ffn_W1"], a["L1_ffn_b1"].reshape(NE, FT, P).transpose(0, 2, 1),
        a["L1_ffn_W2"].reshape(NE, FT, P, P).transpose(0, 2, 1, 3).reshape(NE, P, F)], axis=2))

    nc = bacc.Bacc("TRN2", target_bir_lowering=False, num_devices=1)
    args = [nc.dram_tensor(k, v.shape, mybir.dt.from_np(v.dtype), kind="ExternalInput").ap() for k, v in arrays.items()]
    out = nc.dram_tensor("out_d", (P, N), F32, kind="ExternalOutput").ap()
    n = len(PACKS)
    build(nc, args[:n], *args[n:], out)
    r = run(nc, [arrays], core_ids=[0])
    return np.ascontiguousarray(r.results[0]["out_d"].reshape(P, B, P).transpose(1, 0, 2))
```
